# Optimizing a Trainium2 kernel written in Bass

```python
import numpy as np
import jax
import jax.numpy as jnp

def _softmax(x, axis=-1):
    return jax.nn.softmax(x, axis=axis)

def _gelu(x):
    return jax.nn.gelu(x, approximate=True)

def _silu(x):
    return jax.nn.silu(x)

def _sigmoid(x):
    return jax.nn.sigmoid(x)

def _layernorm(x, axis=-1, eps=1e-05):
    m = jnp.mean(x, axis=axis, keepdims=True)
    v = jnp.var(x, axis=axis, keepdims=True)
    return (x - m) / jnp.sqrt(v + eps)

def _scatter_add(tgt, idx, src, axis=0):
    return tgt.at[idx].add(src)

def _segment_sum(src, seg, n):
    return jax.ops.segment_sum(src, seg, n)
kernel_name = 'mk_lm_tower_d2_tok_ids512_r4_eedafd'

def setup_inputs(seed: int=0):
    np.random.seed(seed)
    _w = jnp.asarray

    def _rec_inputs():
        import jax
        import jax.numpy as jnp
        _rk = jax.random.key(seed)
        x = jax.random.randint(jax.random.fold_in(_rk, 1), (64, 256), 0, 68, jnp.int32)
        return x
    x = _rec_inputs()

    def _L0_tok_setup():
        import jax, jax.numpy as jnp
        import numpy as np
        CODE_START, CODE_END, MEM = (64, 257, 258)
        ADDR_KEY, MEM_STORE = (206, 455)
        VOCAB, D_MODEL = (68, 128)
        B, S = (16, 2048)

        def _augment_mask(token_ids, mem_history_end):
            Bb, Ss = token_ids.shape
            idx = jnp.arange(Ss)
            is_start = token_ids == CODE_START
            is_end = token_ids == CODE_END
            end_idx = jnp.min(jnp.where(is_end, idx[None, :], Ss), axis=1)
            cs = jax.lax.cummax(jnp.where(is_start, idx[None, :], -1), axis=1)
            addr = idx[None, :] - cs - 1
            valid = (cs >= 0) & (idx[None, :] < end_idx[:, None]) & (token_ids < 64) & (addr >= 0)
            lo = addr & 15
            hi = addr >> 4 & 15
            top = addr >> 8 & 15
            bins = jnp.arange(16)
            lo_oh = (bins == lo[..., None]) & valid[..., None]
            hi_oh = (bins == hi[..., None]) & valid[..., None]
            top_oh = (bins == top[..., None]) & valid[..., None]
            mem_flag = (token_ids == MEM) & (idx[None, :] < mem_history_end)
            mask = jnp.zeros((Bb, Ss, D_MODEL), dtype=bool)
            mask = mask.at[:, :, ADDR_KEY:ADDR_KEY + 16].set(lo_oh)
            mask = mask.at[:, :, ADDR_KEY + 16:ADDR_KEY + 32].set(hi_oh)
            mask = mask.at[:, :, ADDR_KEY + 32:ADDR_KEY + 48].set(top_oh)
            mask = mask.at[:, :, MEM_STORE].set(mem_flag)
            return mask
        key = jax.random.key(seed)
        k1, k2 = jax.random.split(key)
        token_ids = jax.random.randint(k1, (B, S), 0, VOCAB)
        embed_weight = jax.random.normal(k2, (VOCAB, D_MODEL), dtype=jnp.float32) * 0.02
        return {'token_ids': token_ids, 'embed_weight': embed_weight, 'mem_history_end': 512}
    _L0_tok_all = _L0_tok_setup()
    _L0_tok_in = {k: v for k, v in _L0_tok_all.items() if k in ('embed_weight',)}
    del _L0_tok_all

    def _L0_attn_setup():
        import jax, jax.numpy as jnp
        import numpy as np
        B, S, D = (8, 512, 128)
        key = jax.random.key(seed)
        k1, k2 = jax.random.split(key)
        lstm_out = jax.random.normal(k1, (B, S, D), dtype=jnp.float32)
        limit = float(np.sqrt(6.0 / (D + D)))
        attention_weights = jax.random.uniform(k2, (D, D), dtype=jnp.float32, minval=-limit, maxval=limit)
        return {'lstm_out': lstm_out, 'attention_weights': attention_weights}
    _L0_attn_all = _L0_attn_setup()
    _L0_attn_in = {k: v for k, v in _L0_attn_all.items() if k in ('attention_weights',)}
    del _L0_attn_all

    def _L0_ffn_setup():
        import jax, jax.numpy as jnp
        import numpy as np
        K = 2
        EPS = 1e-06

        def _layernorm(x, gamma, beta):
            mu = jnp.mean(x, axis=-1, keepdims=True)
            var = jnp.mean(jnp.square(x - mu), axis=-1, keepdims=True)
            return (x - mu) * jax.lax.rsqrt(var + EPS) * gamma + beta
        key = jax.random.key(seed)
        ks = jax.random.split(key, 5)
        B, S, D, F, E = (8, 512, 128, 512, 8)
        x = jax.random.normal(ks[0], (B, S, D), dtype=jnp.float32)
        router_w = jax.random.normal(ks[1], (D, E), dtype=jnp.float32) * 0.02
        w1 = jax.random.normal(ks[2], (E, D, F), dtype=jnp.float32) * 0.02
        b1 = jnp.zeros((E, F), dtype=jnp.float32)
        w2 = jax.random.normal(ks[3], (E, F, D), dtype=jnp.float32) * 0.02
        b2 = jnp.zeros((E, D), dtype=jnp.float32)
        gamma = jnp.ones((E, D), dtype=jnp.float32)
        beta = jnp.zeros((E, D), dtype=jnp.float32)
        return {'x': x, 'router_w': router_w, 'w1': w1, 'b1': b1, 'w2': w2, 'b2': b2, 'gamma': gamma, 'beta': beta}
    _L0_ffn_all = _L0_ffn_setup()
    _L0_ffn_in = {k: v for k, v in _L0_ffn_all.items() if k in ('router_w', 'w1', 'b1', 'w2', 'b2', 'gamma', 'beta')}
    del _L0_ffn_all

    def _L1_attn_setup():
        import jax, jax.numpy as jnp
        import numpy as np
        D_MODEL = 128
        EXPAND = 2
        D_INNER = EXPAND * D_MODEL
        D_STATE = 64
        NGROUPS = 1
        HEADDIM = 64
        NHEADS = D_INNER // HEADDIM
        CHUNK = 64
        D_CONV = 4
        D_IN_PROJ = 2 * D_INNER + 2 * NGROUPS * D_STATE + NHEADS
        CONV_DIM = D_INNER + 2 * NGROUPS * D_STATE
        BATCH, SEQLEN = (4, 2048)
        EPS = 1e-05

        def _segsum(x):
            T = x.shape[-1]
            xe = jnp.broadcast_to(x[..., None], (*x.shape, T))
            m_strict = jnp.tril(jnp.ones((T, T), bool), -1)
            xe = jnp.where(m_strict, xe, 0.0)
            s = jnp.cumsum(xe, axis=-2)
            m_incl = jnp.tril(jnp.ones((T, T), bool), 0)
            return jnp.where(m_incl, s, -jnp.inf)

        def _causal_dwconv(x, w, b):
            k = w.shape[-1]
            y = jax.lax.conv_general_dilated(x, w, window_strides=(1,), padding=[(k - 1, 0)], dimension_numbers=('NCH', 'OIH', 'NCH'), feature_group_count=x.shape[1])
            return y + b[None, :, None]

        def _ssd_scan(X, A, Bm, Cm, chunk):
            b, L, h, p = X.shape
            g, n = (Bm.shape[2], Bm.shape[3])
            c = L // chunk
            X = X.reshape(b, c, chunk, h, p)
            A = A.reshape(b, c, chunk, h).transpose(0, 3, 1, 2)
            Bm = Bm.reshape(b, c, chunk, g, n)
            Cm = Cm.reshape(b, c, chunk, g, n)
            A_cumsum = jnp.cumsum(A, axis=-1)
            Lmat = jnp.exp(_segsum(A))
            hpg = h // g
            B_exp = jnp.repeat(Bm, hpg, axis=3) if hpg > 1 else Bm
            C_exp = jnp.repeat(Cm, hpg, axis=3) if hpg > 1 else Cm
            Y_diag = jnp.einsum('bclhn,bcshn,bhcls,bcshp->bclhp', C_exp, B_exp, Lmat, X)
            decay_states = jnp.exp(A_cumsum[:, :, :, -1:] - A_cumsum)
            states = jnp.einsum('bclhn,bhcl,bclhp->bchpn', B_exp, decay_states, X)
            init = jnp.zeros_like(states[:, :1])
            states = jnp.concatenate([init, states], axis=1)
            decay_chunk = jnp.exp(_segsum(jnp.pad(A_cumsum[:, :, :, -1], ((0, 0), (0, 0), (1, 0)))))
            new_states = jnp.einsum('bhzc,bchpn->bzhpn', decay_chunk, states)
            states, final_state = (new_states[:, :-1], new_states[:, -1])
            state_decay_out = jnp.exp(A_cumsum)
            Y_off = jnp.einsum('bclhn,bchpn,bhcl->bclhp', C_exp, states, state_decay_out)
            Y = (Y_diag + Y_off).reshape(b, L, h, p)
            return (Y, final_state)
        key = jax.random.key(seed)
        ks = jax.random.split(key, 8)
        z_seq = jax.random.normal(ks[0], (BATCH, SEQLEN, D_MODEL), jnp.float32)
        W_in = jax.random.normal(ks[1], (D_IN_PROJ, D_MODEL), jnp.float32) * 0.02
        conv_w = jax.random.normal(ks[2], (CONV_DIM, 1, D_CONV), jnp.float32) * 0.2
        conv_b = jnp.zeros((CONV_DIM,), jnp.float32)
        A_log = jax.random.uniform(ks[3], (NHEADS,), jnp.float32, 0.0, float(np.log(16.0)))
        dt_bias = jax.random.uniform(ks[4], (NHEADS,), jnp.float32, -6.0, -2.0)
        D = jnp.ones((NHEADS,), jnp.float32)
        norm_w = jnp.ones((D_INNER,), jnp.float32)
        W_out = jax.random.normal(ks[5], (D_MODEL, D_INNER), jnp.float32) * 0.03
        return {'z_seq': z_seq, 'W_in': W_in, 'conv_w': conv_w, 'conv_b': conv_b, 'A_log': A_log, 'dt_bias': dt_bias, 'D': D, 'norm_w': norm_w, 'W_out': W_out}
    _L1_attn_all = _L1_attn_setup()
    _L1_attn_in = {k: v for k, v in _L1_attn_all.items() if k in ('W_in', 'conv_w', 'conv_b', 'A_log', 'dt_bias', 'D', 'norm_w', 'W_out')}
    del _L1_attn_all

    def _L1_ffn_setup():
        import jax, jax.numpy as jnp
        import numpy as np
        T = 128
        B = 64
        C = 256

        def _triu_apply(x, W, b):
            Wm = jnp.tril(W)
            return jnp.einsum('bct,st->bcs', x, Wm) + b
        key = jax.random.key(seed)
        ks = jax.random.split(key, 5)
        x = jax.random.normal(ks[0], (B, C, T), dtype=jnp.float32)
        scale = 1.0 / jnp.sqrt(jnp.arange(1, T + 1, dtype=jnp.float32))[:, None]
        W1 = jax.random.uniform(ks[1], (T, T), jnp.float32, -1.0, 1.0) * scale
        b1 = jax.random.uniform(ks[2], (T,), jnp.float32, -1.0, 1.0) * scale[:, 0]
        W2 = jax.random.uniform(ks[3], (T, T), jnp.float32, -1.0, 1.0) * scale
        b2 = jax.random.uniform(ks[4], (T,), jnp.float32, -1.0, 1.0) * scale[:, 0]
        return {'x': x, 'W1': W1, 'b1': b1, 'W2': W2, 'b2': b2}
    _L1_ffn_all = _L1_ffn_setup()
    _L1_ffn_in = {k: v for k, v in _L1_ffn_all.items() if k in ('W1', 'b1', 'W2', 'b2')}
    del _L1_ffn_all
    return {'x': x, 'L0_tok_embed_weight': _L0_tok_in['embed_weight'], 'L0_attn_attention_weights': _L0_attn_in['attention_weights'], 'L0_ffn_router_w': _L0_ffn_in['router_w'], 'L0_ffn_w1': _L0_ffn_in['w1'], 'L0_ffn_b1': _L0_ffn_in['b1'], 'L0_ffn_w2': _L0_ffn_in['w2'], 'L0_ffn_b2': _L0_ffn_in['b2'], 'L0_ffn_gamma': _L0_ffn_in['gamma'], 'L0_ffn_beta': _L0_ffn_in['beta'], 'L1_attn_W_in': _L1_attn_in['W_in'], 'L1_attn_conv_w': _L1_attn_in['conv_w'], 'L1_attn_conv_b': _L1_attn_in['conv_b'], 'L1_attn_A_log': _L1_attn_in['A_log'], 'L1_attn_dt_bias': _L1_attn_in['dt_bias'], 'L1_attn_D': _L1_attn_in['D'], 'L1_attn_norm_w': _L1_attn_in['norm_w'], 'L1_attn_W_out': _L1_attn_in['W_out'], 'L1_ffn_W1': _L1_ffn_in['W1'], 'L1_ffn_b1': _L1_ffn_in['b1'], 'L1_ffn_W2': _L1_ffn_in['W2'], 'L1_ffn_b2': _L1_ffn_in['b2']}

def reference(x, L0_tok_embed_weight, L0_attn_attention_weights, L0_ffn_router_w, L0_ffn_w1, L0_ffn_b1, L0_ffn_w2, L0_ffn_b2, L0_ffn_gamma, L0_ffn_beta, L1_attn_W_in, L1_attn_conv_w, L1_attn_conv_b, L1_attn_A_log, L1_attn_dt_bias, L1_attn_D, L1_attn_norm_w, L1_attn_W_out, L1_ffn_W1, L1_ffn_b1, L1_ffn_W2, L1_ffn_b2):
    import jax
    import jax.numpy as jnp

    def _L0_tok_ref(token_ids, embed_weight, mem_history_end):
        import jax, jax.numpy as jnp
        import numpy as np
        CODE_START, CODE_END, MEM = (64, 257, 258)
        ADDR_KEY, MEM_STORE = (206, 455)
        VOCAB, D_MODEL = (68, 128)
        B, S = (16, 2048)

        def _augment_mask(token_ids, mem_history_end):
            Bb, Ss = token_ids.shape
            idx = jnp.arange(Ss)
            is_start = token_ids == CODE_START
            is_end = token_ids == CODE_END
            end_idx = jnp.min(jnp.where(is_end, idx[None, :], Ss), axis=1)
            cs = jax.lax.cummax(jnp.where(is_start, idx[None, :], -1), axis=1)
            addr = idx[None, :] - cs - 1
            valid = (cs >= 0) & (idx[None, :] < end_idx[:, None]) & (token_ids < 64) & (addr >= 0)
            lo = addr & 15
            hi = addr >> 4 & 15
            top = addr >> 8 & 15
            bins = jnp.arange(16)
            lo_oh = (bins == lo[..., None]) & valid[..., None]
            hi_oh = (bins == hi[..., None]) & valid[..., None]
            top_oh = (bins == top[..., None]) & valid[..., None]
            mem_flag = (token_ids == MEM) & (idx[None, :] < mem_history_end)
            mask = jnp.zeros((Bb, Ss, D_MODEL), dtype=bool)
            mask = mask.at[:, :, ADDR_KEY:ADDR_KEY + 16].set(lo_oh)
            mask = mask.at[:, :, ADDR_KEY + 16:ADDR_KEY + 32].set(hi_oh)
            mask = mask.at[:, :, ADDR_KEY + 32:ADDR_KEY + 48].set(top_oh)
            mask = mask.at[:, :, MEM_STORE].set(mem_flag)
            return mask
        x = embed_weight[token_ids]
        mask = _augment_mask(token_ids, mem_history_end)
        return jnp.where(mask, jnp.asarray(1.0, x.dtype), x)

    def _L0_attn_ref(lstm_out, attention_weights):
        import jax, jax.numpy as jnp
        import numpy as np
        B, S, D = (8, 512, 128)
        proj = jnp.einsum('bsd,de->bse', lstm_out, attention_weights)
        scores = jnp.tanh(jnp.einsum('bsd,btd->bst', proj, lstm_out))
        attn = jax.nn.softmax(scores, axis=-1)
        return jnp.einsum('bst,btd->bsd', attn, lstm_out)

    def _L0_ffn_ref(x, router_w, w1, b1, w2, b2, gamma, beta):
        import jax, jax.numpy as jnp
        import numpy as np
        K = 2
        EPS = 1e-06

        def _layernorm(x, gamma, beta):
            mu = jnp.mean(x, axis=-1, keepdims=True)
            var = jnp.mean(jnp.square(x - mu), axis=-1, keepdims=True)
            return (x - mu) * jax.lax.rsqrt(var + EPS) * gamma + beta
        B, S, D = x.shape
        E = w1.shape[0]
        xf = x.reshape(-1, D)
        logits = xf @ router_w
        gate_vals, idx = jax.lax.top_k(logits, K)
        gates = jax.nn.softmax(gate_vals, axis=-1)
        out = jnp.zeros_like(xf)
        for e in range(E):
            h = jax.nn.relu(xf @ w1[e] + b1[e]) @ w2[e] + b2[e]
            y = _layernorm(xf + h, gamma[e], beta[e])
            w = jnp.sum(jnp.where(idx == e, gates, 0.0), axis=-1)
            out = out + w[:, None] * y
        return out.reshape(B, S, D)

    def _L1_attn_ref(z_seq, W_in, conv_w, conv_b, A_log, dt_bias, D, norm_w, W_out):
        import jax, jax.numpy as jnp
        import numpy as np
        D_MODEL = 128
        EXPAND = 2
        D_INNER = EXPAND * D_MODEL
        D_STATE = 64
        NGROUPS = 1
        HEADDIM = 64
        NHEADS = D_INNER // HEADDIM
        CHUNK = 64
        D_CONV = 4
        D_IN_PROJ = 2 * D_INNER + 2 * NGROUPS * D_STATE + NHEADS
        CONV_DIM = D_INNER + 2 * NGROUPS * D_STATE
        BATCH, SEQLEN = (4, 2048)
        EPS = 1e-05

        def _segsum(x):
            T = x.shape[-1]
            xe = jnp.broadcast_to(x[..., None], (*x.shape, T))
            m_strict = jnp.tril(jnp.ones((T, T), bool), -1)
            xe = jnp.where(m_strict, xe, 0.0)
            s = jnp.cumsum(xe, axis=-2)
            m_incl = jnp.tril(jnp.ones((T, T), bool), 0)
            return jnp.where(m_incl, s, -jnp.inf)

        def _causal_dwconv(x, w, b):
            k = w.shape[-1]
            y = jax.lax.conv_general_dilated(x, w, window_strides=(1,), padding=[(k - 1, 0)], dimension_numbers=('NCH', 'OIH', 'NCH'), feature_group_count=x.shape[1])
            return y + b[None, :, None]

        def _ssd_scan(X, A, Bm, Cm, chunk):
            b, L, h, p = X.shape
            g, n = (Bm.shape[2], Bm.shape[3])
            c = L // chunk
            X = X.reshape(b, c, chunk, h, p)
            A = A.reshape(b, c, chunk, h).transpose(0, 3, 1, 2)
            Bm = Bm.reshape(b, c, chunk, g, n)
            Cm = Cm.reshape(b, c, chunk, g, n)
            A_cumsum = jnp.cumsum(A, axis=-1)
            Lmat = jnp.exp(_segsum(A))
            hpg = h // g
            B_exp = jnp.repeat(Bm, hpg, axis=3) if hpg > 1 else Bm
            C_exp = jnp.repeat(Cm, hpg, axis=3) if hpg > 1 else Cm
            Y_diag = jnp.einsum('bclhn,bcshn,bhcls,bcshp->bclhp', C_exp, B_exp, Lmat, X)
            decay_states = jnp.exp(A_cumsum[:, :, :, -1:] - A_cumsum)
            states = jnp.einsum('bclhn,bhcl,bclhp->bchpn', B_exp, decay_states, X)
            init = jnp.zeros_like(states[:, :1])
            states = jnp.concatenate([init, states], axis=1)
            decay_chunk = jnp.exp(_segsum(jnp.pad(A_cumsum[:, :, :, -1], ((0, 0), (0, 0), (1, 0)))))
            new_states = jnp.einsum('bhzc,bchpn->bzhpn', decay_chunk, states)
            states, final_state = (new_states[:, :-1], new_states[:, -1])
            state_decay_out = jnp.exp(A_cumsum)
            Y_off = jnp.einsum('bclhn,bchpn,bhcl->bclhp', C_exp, states, state_decay_out)
            Y = (Y_diag + Y_off).reshape(b, L, h, p)
            return (Y, final_state)
        b, T, _ = z_seq.shape
        zxbcdt = z_seq @ W_in.T
        z = zxbcdt[..., :D_INNER]
        xBC = zxbcdt[..., D_INNER:D_INNER + D_INNER + 2 * NGROUPS * D_STATE]
        dt_raw = zxbcdt[..., -NHEADS:]
        dt = jax.nn.softplus(dt_raw + dt_bias)
        xBC = _causal_dwconv(xBC.transpose(0, 2, 1), conv_w, conv_b).transpose(0, 2, 1)
        xBC = jax.nn.silu(xBC)
        x = xBC[..., :D_INNER]
        Bm = xBC[..., D_INNER:D_INNER + NGROUPS * D_STATE]
        Cm = xBC[..., D_INNER + NGROUPS * D_STATE:]
        A = -jnp.exp(A_log)
        x = x.reshape(b, T, NHEADS, HEADDIM)
        Bm = Bm.reshape(b, T, NGROUPS, D_STATE)
        Cm = Cm.reshape(b, T, NGROUPS, D_STATE)
        X = x * dt[..., None]
        A_disc = A[None, None, :] * dt
        y, _final = _ssd_scan(X, A_disc, Bm, Cm, CHUNK)
        y = y + x * D[None, None, :, None]
        y = y.reshape(b, T, D_INNER)
        rms = jnp.linalg.norm(y, axis=-1, keepdims=True) * D_INNER ** (-0.5)
        y = norm_w * (y / (rms + EPS))
        y = y * jax.nn.silu(z)
        return y @ W_out.T

    def _L1_ffn_ref(x, W1, b1, W2, b2):
        import jax, jax.numpy as jnp
        import numpy as np
        T = 128
        B = 64
        C = 256

        def _triu_apply(x, W, b):
            Wm = jnp.tril(W)
            return jnp.einsum('bct,st->bcs', x, Wm) + b
        h = _triu_apply(x, W1, b1)
        h = jax.nn.gelu(h, approximate=False)
        return _triu_apply(h, W2, b2)
    h = _L0_tok_ref(x, L0_tok_embed_weight, 512)
    h = h + _L0_attn_ref(_layernorm(h, axis=-1), L0_attn_attention_weights)
    h = h + _L0_ffn_ref(_layernorm(h, axis=-1), L0_ffn_router_w, L0_ffn_w1, L0_ffn_b1, L0_ffn_w2, L0_ffn_b2, L0_ffn_gamma, L0_ffn_beta)
    h = h + _L1_attn_ref(_layernorm(h, axis=-1), L1_attn_W_in, L1_attn_conv_w, L1_attn_conv_b, L1_attn_A_log, L1_attn_dt_bias, L1_attn_D, L1_attn_norm_w, L1_attn_W_out)
    h = h + _L1_ffn_ref(_layernorm(h, axis=-1), L1_ffn_W1, L1_ffn_b1, L1_ffn_W2, L1_ffn_b2)
    return h

_drawn_inputs = setup_inputs


def setup_inputs(seed=0):
    import zlib

    import numpy as np

    out = dict(_drawn_inputs(seed))
    spreads = {'L0_ffn_b1': (0.0, 0.456),
     'L0_ffn_b2': (0.0, 0.1),
     'L0_ffn_gamma': (1.0, 0.2),
     'L0_ffn_beta': (0.0, 0.1),
     'L1_attn_conv_b': (0.0, 0.1),
     'L1_attn_D': (1.0, 0.6),
     'L1_attn_norm_w': (1.0, 0.6)}
    factors = {'L1_attn_A_log': 8.0, 'L1_attn_dt_bias': 64.0}
    for name, (base, spread) in spreads.items():
        noise = np.random.default_rng([zlib.crc32(name.encode()), seed]).standard_normal(out[name].shape)
        drawn = base * np.exp(spread * noise) if base else spread * noise
        out[name] = jnp.asarray(drawn.astype(out[name].dtype))
    for name, factor in factors.items():
        out[name] = (out[name] * factor).astype(out[name].dtype)
    return out
```

```python
from contextlib import ExitStack

import concourse.bass as bass
from concourse import mybir

F32 = mybir.dt.float32
U8 = mybir.dt.uint8
I32 = mybir.dt.int32
U32 = mybir.dt.uint32
ALU = mybir.AluOpType
ACT = mybir.ActivationFunctionType
AX = mybir.AxisListType

P = 128
BANK = 512
EPS_LN = 1e-5
EPS_FFN = 1e-6
EPS_RMS = 1e-5


def lm_tower(nc, x, emb, attn_w, router_w, w1, b1, w2, b2, gamma, beta,
             W_in, conv_w, conv_b, A_log, dt_bias, Dskip, norm_w, W_out,
             tri_w1, tri_b1, tri_w2, tri_b2, out):
    B, T = x.shape
    V, D = emb.shape
    E, _, F = w1.shape
    FT = F // P
    CONV, _, TAPS = conv_w.shape
    H = A_log.shape[0]
    DI = norm_w.shape[0]
    HD = DI // H
    NS = (CONV - DI) // 2
    PAD = TAPS - 1
    RR = B * V
    N2 = 2 * P
    NI = RR // N2
    NTILE = RR // P
    CH = T // P
    NCH = B * CH
    assert D == P and CH == 2 and RR % N2 == 0 and V < P and F % P == 0

    ctx = ExitStack()
    with ctx:
        def sb(name, shape, dt=F32):
            return ctx.enter_context(nc.sbuf_tensor(name, shape, dt))

        def sem(name):
            return ctx.enter_context(nc.semaphore(name))

        bank = [ctx.enter_context(nc.psum_tensor(f"bank{i}", [P, BANK], F32)) for i in range(8)]

        shared = sb("shared", [P, 16384])
        place = [0]

        def phase():
            place[0] = 0

        def take(shape, dt=F32):
            size = 1
            for s in shape[1:]:
                size *= s
            view = shared[0:shape[0], place[0]:place[0] + size]
            place[0] += size
            assert place[0] <= shared.shape[1], place[0]
            if dt != F32:
                view = view.bitcast(dt)
            if len(shape) > 2:
                axes = "abc"[:len(shape) - 1]
                view = view.rearrange(f"p ({' '.join(axes)}) -> p {' '.join(axes)}",
                                      **dict(zip(axes[1:], shape[2:])))
            return view

        ident = sb("ident", [P, P])
        upper = sb("upper", [P, P])
        later = sb("later", [P, P])
        mean_w = sb("mean_w", [P, P])
        vocab = sb("vocab", [V, 1])
        experts8 = sb("experts8", [P, E])
        half_pow = sb("half_pow", [P, 1])
        eps_ln = sb("eps_ln", [P, 1])
        eps_ffn = sb("eps_ffn", [P, 1])

        onehot = sb("onehot", [V, B, PAD + T], U8)
        hT = sb("hT", [P, RR])
        xT = sb("xT", [P, RR])
        arena = sb("arena", [P, NCH * P])
        w1_sb = arena[:, 0:E * F].rearrange("p (e f) -> p e f", e=E)
        w2_sb = arena[:, E * F:2 * E * F].rearrange("p (e c d) -> p e c d", e=E, c=FT)
        xrows = arena[:, 2 * E * F:2 * E * F + RR]
        TOKB = 8
        TOKN = 4
        tok = arena[0:V, 2 * E * F:2 * E * F + TOKN * TOKB * T].bitcast(I32).rearrange(
            "p (n b t) -> p n b t", n=TOKN, b=TOKB)
        h3 = arena[:, :]

        phase()
        gamma_bc = take([P, E * D])
        b2_bc = take([P, E * D])
        cen2, sqr2 = (take([P, 2, N2]) for _ in range(2))
        cen, sqr = cen2[:, 0, :], sqr2[:, 0, :]
        dev, rstd = (take([P, N2]) for _ in range(2))
        kept = place[0]
        emb_sb = sb("emb_sb", [V, D])
        attn_sb = sb("attn_sb", [D, D])
        router_sb = sb("router_sb", [D, E])
        b1_rows = take([E * FT, P])
        b1_col = sb("b1_col", [P, E * FT])
        beta_sb = sb("beta_sb", [E, D])
        NZX = 2 * DI + 2 * NS
        win_rows = take([P, NZX // P, D])
        windt_rows = take([H, D])
        win_T = sb("win_T", [D, NZX])
        windt_T = sb("windt_T", [D, H])
        convw_raw = arena[0:V, 2 * E * F:2 * E * F + CONV * TAPS]
        tapw = sb("tapw", [V, TAPS, CONV])
        convb_row = sb("convb_row", [1, CONV])
        convb_half = sb("convb_half", [1, CONV])
        a_neg = sb("a_neg", [P, H])
        alog_bc = sb("alog_bc", [P, H])
        dtb_bc = sb("dtb_bc", [V, H])
        d_bc = sb("d_bc", [P, H])
        normw_col = sb("normw_col", [P, DI // P])
        normw_rows = take([DI // P, P])
        wout_rows = take([D, DI])
        wout_T = sb("wout_T", [P, DI // P, D])
        tri1_rows = take([P, P])
        tri2_rows = take([P, P])
        tri1_T = sb("tri1_T", [P, P])
        tri2_T = sb("tri2_T", [P, P])
        trib1_col = sb("trib1_col", [P, 1])
        trib2_bc = sb("trib2_bc", [P, P])

        counts = sb("counts", [V, B])
        rden = sb("rden", [V, B])
        lne = take([V, D])
        lneT = take([D, V])
        projT = take([D, V])
        tanh_s = take([V, V])
        expT = take([V, V])
        stat = sb("stat", [P, 16])
        GA = 4
        weighted = take([V, 2, GA, D])
        h1rows = take([V, 2, GA, D])

        xT_now = take([P, 2, N2])
        logit = take([P, 2, E])
        top_v = take([P, 2, 8])
        top_i = take([P, 2, 8], U32)
        vals = take([P, NTILE, 2])
        idxs = take([P, NTILE, 2])
        gdiff = take([P, NTILE])
        gexp = take([P, NTILE])
        gates = take([P, NTILE, 2])
        pick = take([P, NTILE, E])
        wgate = sb("wgate", [P, NTILE, E])

        place[0] = kept
        hid = take([P, 2, FT, N2])
        xb2 = take([P, 2, E * D])
        pre = take([P, 2, E * D])
        bns = take([P, 2 * E, 6])
        sm = take([P, 8, 2 * E])
        summed = take([P, 2, D])
        w_now = take([P, 2, E])
        wT_now = take([E, N2])

        phase()
        hot = take([V + 1, 4, PAD + T])
        taps = take([V + 1, 2, TAPS, CONV])
        tables_end = place[0]
        GD = 8
        dt_in = take([D, 2, GD * V])
        dt_t = take([V, 5, B * H])
        place[0] = tables_end
        xT_seq = take([D, 2, V])
        hT_seq = take([D, 2, V])
        dt_tab = sb("dt_tab", [V, B, 2, H])
        tanh_z = take([V, DI])
        ztab = take([V, 4, DI])
        xtab = take([V, CONV])
        htab = take([V, 4, D])
        tanh_x = take([P, CONV])
        xbc = take([P, 2, CONV])
        dts = take([P, 2, 2, 2 * H])
        amask = take([P, 2, H, P])
        xdt = take([P, 2, DI])
        xskip = take([P, 2, DI])
        xtail = take([P, DI])
        bcT = take([NS, 2, 2 * P])
        cbm = take([P, 2, P])
        edge = take([P, 2, H])
        decay = take([P, 2, H, P])
        mix = take([P, 2, H, P])
        state = take([NS, DI])
        yoff = take([P, DI])
        y = take([P, 2, DI])
        ysq = take([P, DI])
        ssum = take([P, 1])
        ms = take([P, 1])
        rms = take([P, 3])
        gated = take([P, DI])
        gT = take([P, DI])

        h3_bns = sb("h3_bns", [P, NCH, 6])
        h3_s = sb("h3_s", [P, 5, NCH])
        TD = 4
        phase()
        NT = NCH // TD
        xn = take([P, 2, TD, D])
        xnT = take([P, 2, TD * P])
        gel = take([P, 2, TD * P])
        res = take([P, 4, TD, D])
        fin = take([P, 4, TD, D])

        names = """ld_att ld_ffn ld_ssm ld_mlp ld_rout const_ok zero_ok tok_ld0 tok_ld1 tok_ld2 tok_ld3
            tok_used dchain achain pchain e_var e_sd e_ln e_lnT e_lnT_c e_pT e_pT_c e_sc e_tanh e_exp e_cnt
            e_den e_rden w_tr w_trc
            at_w0 at_w1 at_num0 at_num1 at_h0 at_h1 at_t0 at_t1 at_s0 at_s1
            r_mean r_c r_sq r_var r_sd r_x r_cp r_tr r_rt r_xf r_lg r_gd r_ge r_gates
            b_up b_relu b_dn b_y b_xb2 b_pre00 b_pre01 b_pre10 b_pre11 b_var b_sd b_u b_ug b_o b_z b_h2 b_mean b_c b_sq b_v2 b_sd2
            b_x b_wn b_wt b_wtc rchain bchain
            s_in s_in1 s_raw s_v s_e s_l s_dt s_aneg
            c_seq c_tab c_tx c_tz c_zt c_ht c_taps c_cv c_tanh c_x c_dt c_dtc c_adt
            c_mask c_xdt c_xsk c_xtl c_bc c_bcc c_cb c_cbm c_seg c_dec c_edg c_edc c_mix
            c_yd c_st c_stc c_yo c_y c_sq c_rms c_zg c_g c_gt c_gtc c_out c_h3 c_bn cchain gchain
            f_st f_sd f_rs m_xn m_xt m_xtc m_1 m_gel m_2 m_res m_fin m_st0 m_st1 m_st2 m_st3 mchain zpad taps0 w_nw r_top r_ti b_bn""".split()
        S = {n: sem(n) for n in names}

        class Chain:

            def __init__(self, eng, name):
                self.eng, self.sem, self.base, self.n = eng, S[name], 0, 0

            def start(self, base):
                self.base, self.n = base, 0

            def link(self, ins):
                self.n += 1
                ins.then_inc(self.sem, 1)
                self.eng.wait_ge(self.sem, self.base + self.n)

        def bc_rows(ap, n):
            return ap.unsqueeze(0).to_broadcast([n] + list(ap.shape))

        def flat(ap):
            return ap.rearrange("e d -> (e d)")

        R_LINKS, B_LINKS = 2, 5
        C_LINKS_D, C_LINKS_P = 3, 1
        POST = [TAPS]

        STEPS = 8

        def rolling(eng, step, count, body, depth):
            first = -(-depth // body)
            full = count // body
            for k in range(first * body):
                step(k // body, k % body, lambda lag: k >= lag)
            with eng.Fori(first, full) as m:
                for r in range(body):
                    step(m, r, lambda lag: True)
            for k in range(full * body, count + depth):
                step(k // body, k % body, lambda lag: k - lag < count)

        def pipeline(eng, step):
            rolling(eng, step, NCH, STEPS, 4)

        def wait_past(eng, name, value):
            if not (isinstance(value, int) and value <= 0):
                eng.wait_ge(S[name], value)

        def spot(r, lag):
            s = (r - lag) % STEPS
            return s % 2, s // 2

        def half(n, c):
            return (n - c) // 2

        block = ctx.enter_context(nc.Block())

        @block.sync
        def _(sp):
            att = [(emb_sb[:, :], emb), (attn_sb[:, :], attn_w)]
            for dst, src in att:
                sp.dma_start(dst, src).then_inc(S["ld_att"], 16)
            for n in range(TOKN):
                sp.dma_start(tok[:, n], bc_rows(x[n * TOKB:(n + 1) * TOKB, :], V)).then_inc(S[f"tok_ld{n}"], 16)
            rout = [(router_sb[:, :], router_w), (b1_rows[:, :], b1.rearrange("e (c p) -> (e c) p", p=P)),
                    (win_rows[:, :, :], W_in[0:NZX, :].rearrange("(c p) d -> p c d", p=P)),
                    (windt_rows[:, :], W_in[NZX:NZX + H, :]),
                    (wout_rows[:, :], W_out), (tri1_rows[:, :], tri_w1), (tri2_rows[:, :], tri_w2),
                    (normw_rows, norm_w.rearrange("(c p) -> c p", p=P))]
            for dst, src in rout:
                sp.dma_start(dst, src).then_inc(S["ld_rout"], 16)
            for n in range(TOKN, B // TOKB):
                sp.wait_ge(S["tok_used"], n - TOKN + 1)
                sp.dma_start(tok[:, n % TOKN], bc_rows(x[n * TOKB:(n + 1) * TOKB, :], V)).then_inc(
                    S[f"tok_ld{n % TOKN}"], 16)
            ffn = [(w1_sb, w1.rearrange("e d f -> d e f")),
                   (b2_bc[:, :], bc_rows(flat(b2), P)), (gamma_bc[:, :], bc_rows(flat(gamma), P)),
                   (beta_sb[:, :], beta)]
            for dst, src in ffn:
                sp.dma_start(dst, src).then_inc(S["ld_ffn"], 16)
            for e in range(E):
                sp.dma_start(w2_sb[:, e], w2[e].rearrange("(c p) d -> p c d", p=P)).then_inc(S["ld_ffn"], 16)
            ssm = [(convw_raw, bc_rows(conv_w.rearrange("c o k -> (c o k)"), V)),
                   (convb_row[:, :], bc_rows(conv_b, 1)), (alog_bc[:, :], bc_rows(A_log, P)),
                   (dtb_bc[:, :], bc_rows(dt_bias, V)), (d_bc[:, :], bc_rows(Dskip, P))]
            sp.wait_ge(S["b_x"], NI)
            for dst, src in ssm:
                sp.dma_start(dst, src).then_inc(S["ld_ssm"], 16)
            mlp = [(trib1_col[:, :], tri_b1.unsqueeze(1)), (trib2_bc[:, :], bc_rows(tri_b2, P))]
            for dst, src in mlp:
                sp.dma_start(dst, src).then_inc(S["ld_mlp"], 16)
            sp.wait_ge(S["s_aneg"], 1)
            sp.wait_ge(S["taps0"], 1)
            for q in range(2):
                sp.dma_start(taps[V:V + 1, q, TAPS - 1, :], convb_half[:, :]).then_inc(S["zpad"], 16)
            rows = out.rearrange("b (c p) d -> p (b c) d", p=P)
            with sp.Fori(1, NT // 4 + 1) as m:
                for q in range(4):
                    sp.wait_ge(S["m_fin"], 4 * m - 3 + q)
                    sp.dma_start(rows[:, bass.ds(4 * TD * m - (4 - q) * TD, TD), :], fin[:, q]).then_inc(S[f"m_st{q}"], 16)
            for q in range(4):
                sp.wait_ge(S[f"m_st{q}"], 16 * (NT // 4))

        N_ATT, N_ROUT, N_FFN, N_SSM, N_MLP = 2, 8, 4 + E, 5, 2

        @block.gpsimd
        def _(pool):
            g = nc.gpsimd
            g.memset(ident[:, :], 0.0).then_inc(S["zero_ok"], 1)
            g.memset(upper[:, :], 1.0).then_inc(S["zero_ok"], 1)
            g.memset(later[:, :], 1.0).then_inc(S["zero_ok"], 1)
            pool.wait_ge(S["zero_ok"], 3)
            g.affine_select(out=ident[:, :], in_=ident[:, :], compare_op=ALU.not_equal, fill=1.0, base=0,
                            pattern=[[-1, P]], channel_multiplier=1).then_inc(S["const_ok"], 1)
            g.affine_select(out=upper[:, :], in_=upper[:, :], compare_op=ALU.is_ge, fill=0.0, base=0,
                            pattern=[[1, P]], channel_multiplier=-1).then_inc(S["const_ok"], 1)
            g.affine_select(out=later[:, :], in_=later[:, :], compare_op=ALU.is_gt, fill=0.0, base=0,
                            pattern=[[-1, P]], channel_multiplier=1).then_inc(S["const_ok"], 1)
            g.iota(vocab[:, :], pattern=[[0, 1]], base=0, channel_multiplier=1,
                   allow_small_or_imprecise_dtypes=True).then_inc(S["const_ok"], 1)
            g.iota(experts8[:, :], pattern=[[1, E]], base=0, channel_multiplier=0,
                   allow_small_or_imprecise_dtypes=True).then_inc(S["const_ok"], 1)
            g.memset(mean_w[:, :], 1.0 / D).then_inc(S["const_ok"], 1)
            g.memset(half_pow[:, :], 0.5).then_inc(S["const_ok"], 1)
            g.memset(eps_ln[:, :], EPS_LN).then_inc(S["const_ok"], 1)
            g.memset(eps_ffn[:, :], EPS_FFN).then_inc(S["const_ok"], 1)
            g.memset(onehot[:, :, 0:PAD], 0.0).then_inc(S["const_ok"], 1)

            def routing_pool(m, r, valid):
                k = 2 * m + r
                if valid(0):
                    pool.wait_ge(S["r_c"], k + 1)
                    wait_past(pool, "r_var", k - 1)
                    g.tensor_tensor(sqr2[:, r], cen2[:, r], cen2[:, r], ALU.mult).then_inc(S["r_sq"], 1)
                if valid(2):
                    pool.wait_ge(S["r_x"], k - 1)
                    g.tensor_copy(xT[:, bass.ds((k - 2) * N2, N2)], xT_now[:, r]).then_inc(S["r_cp"], 1)

            rolling(pool, routing_pool, NI, 2, 2)

            def add_b2(i, gg, first):
                for j in range(2):
                    pool.wait_ge(S["r_xf"], NI)
                    if not first:
                        pool.wait_ge(S[f"b_pre{gg}{j}"], i - 1)
                    g.tensor_tensor(xb2[:, j, gg * BANK:(gg + 1) * BANK].rearrange("p (e d) -> p e d", d=D),
                                    b2_bc[:, gg * BANK:(gg + 1) * BANK].rearrange("p (e d) -> p e d", d=D),
                                    xrows[:, bass.ds((i - 1) * N2 + j * P, P)].unsqueeze(1).to_broadcast([P, 4, D]),
                                    ALU.add).then_inc(S["b_xb2"], 1)

            def expert_pool(i, first, cur, back):
                if cur:
                    if not first:
                        pool.wait_ge(S["b_wt"], i - 1)
                    g.tensor_copy(w_now[:, :, :], wgate[:, bass.ds(2 * (i - 1), 2), :]).then_inc(S["b_wn"], 1)
                    add_b2(i, 0, first)
                if back:
                    for j in range(2):
                        pool.wait_ge(S["b_u"], 2 * i - 3 + j)
                        g.tensor_tensor(pre[:, j, :], pre[:, j, :], gamma_bc[:, :], ALU.mult).then_inc(S["b_ug"], 1)
                if cur:
                    add_b2(i, 1, first)
                if back:
                    pool.wait_ge(S["b_c"], i - 1)
                    g.tensor_tensor(sqr, cen, cen, ALU.mult).then_inc(S["b_sq"], 1)

            pool.wait_ge(S["r_gates"], 1)
            pool.wait_ge(S["r_xf"], NI)
            pool.wait_ge(S["r_cp"], NI)
            pool.wait_ge(S["ld_ffn"], 16 * N_FFN)
            expert_pool(1, True, True, False)
            with pool.Fori(2, NI + 1) as i:
                expert_pool(i, False, True, True)
            expert_pool(NI + 1, False, False, True)

            pool.wait_ge(S["b_x"], NI)
            chain = Chain(pool, "gchain")

            def tables(b, q, first):
                if not first:
                    pool.wait_ge(S["c_tab"], b - 1)
                if not (isinstance(b, int) and b < 4):
                    pool.wait_ge(S["c_out"], 2 * b - 6)
                g.tensor_copy(xT_seq[:, q % 2], xT[:, bass.ds(b * V, V)])
                g.tensor_copy(hT_seq[:, q % 2], hT[:, bass.ds(b * V, V)])
                g.tensor_copy(hot[0:V, q, :], onehot[:, bass.ds(b, 1), :].rearrange("p a t -> p (a t)")).then_inc(
                    S["c_seq"], 1)

            def tap_tables(b, q):
                pool.wait_ge(S["c_tx"], b + 1)
                if not (isinstance(b, int) and b < 2):
                    pool.wait_ge(S["c_cv"], 2 * b - 2)
                g.tensor_tensor(taps[0:V, q], xtab[:, :].unsqueeze(1).to_broadcast([V, TAPS, CONV]),
                                tapw[:, :, :], ALU.mult).then_inc(S["c_taps"], 1)

            def by_head(ap):
                return ap.rearrange("p (h d) -> p h d", h=H)

            def steps_of(q, c, part):
                return dts[:, q % 2, c, part * H:(part + 1) * H]

            def mask_pool(n, q, c):
                pool.wait_ge(S["c_ht"], half(n, c) + 1)
                if not (isinstance(n, int) and n < 1):
                    pool.wait_ge(S["c_seg"], n - 1)
                g.tensor_tensor(amask[:, c], upper[:, :].unsqueeze(1).to_broadcast([P, H, P]),
                                steps_of(q, c, 1).unsqueeze(2).to_broadcast([P, H, P]), ALU.mult).then_inc(S["c_mask"], 1)

            def inputs_pool(n, q, c):
                pool.wait_ge(S["c_x"], n + 1)
                if not (isinstance(n, int) and n < 1):
                    pool.wait_ge(S["c_y"], n - 1)
                chain.start(n)
                chain.link(g.tensor_tensor(by_head(xdt[:, c]), by_head(xbc[:, c, 0:DI]),
                                           steps_of(q, c, 0).unsqueeze(2).to_broadcast([P, H, HD]), ALU.mult))
                g.tensor_tensor(by_head(xskip[:, c]), by_head(xbc[:, c, 0:DI]),
                                d_bc[:, :].unsqueeze(2).to_broadcast([P, H, HD]), ALU.mult).then_inc(S["c_xsk"], 1)

            def tail_pool(n, c):
                pool.wait_ge(S["c_edc"], n + 1)
                g.tensor_tensor(by_head(xtail[:, :]), by_head(xdt[:, c]),
                                edge[:, c].unsqueeze(2).to_broadcast([P, H, HD]), ALU.mult).then_inc(S["c_xtl"], 1)

            def rms_pool(n):
                pool.wait_ge(S["c_sq"], n + 1)
                g.tensor_tensor(rms[:, 0:1], ms[:, :], half_pow[:, :], ALU.pow).then_inc(S["c_rms"], 1)

            def step(m, r, valid):
                k = STEPS * m + r
                c2, q2 = spot(r, 2)
                c3, q3 = spot(r, 3)
                if valid(3):
                    inputs_pool(k - 3, q3, c3)
                if valid(4):
                    rms_pool(k - 4)
                if r % 2 == 0 and valid(0):
                    tables(4 * m + r // 2, r // 2, isinstance(m, int) and m == 0)
                if c3 == 0 and valid(3):
                    tail_pool(k - 3, c3)
                if r % 2 == 1 and valid(1):
                    tap_tables(4 * m + r // 2, r // 2 % 2)
                if valid(2):
                    mask_pool(k - 2, q2, c2)

            g.memset(hot[:, :, :], 1.0)
            g.memset(taps[:, :, :, :], 0.0).then_inc(S["taps0"], 1)
            pool.wait_ge(S["s_dt"], 1)
            pipeline(pool, step)

            pool.wait_ge(S["c_h3"], NCH)
            pool.wait_ge(S["ld_mlp"], 16 * N_MLP)
            def mlp_pool(m, r, valid):
                k = 4 * m + r
                if valid(0):
                    now = pool.snap(k - 3) if not isinstance(k, int) else k - 3
                    pool.wait_ge(S["c_h3"], NCH)
                    wait_past(pool, "m_fin", now)
                    g.tensor_tensor(res[:, r], h3[:, bass.ds(k * TD * P, TD * P)].rearrange("p (c d) -> p c d", d=D),
                                    trib2_bc[:, :].unsqueeze(1).to_broadcast([P, TD, D]), ALU.add).then_inc(S["m_res"], 1)

            rolling(pool, mlp_pool, NT, 4, 3)

        @block.tensor
        def _(pe):
            t = nc.tensor
            mm = t.matmul

            pe.wait_ge(S["const_ok"], 10)
            pe.wait_ge(S["e_ln"], 1)
            t.transpose(bank[3][:, 0:V], lne[:, :], ident[0:V, 0:V]).then_inc(S["e_lnT"], 1)
            pe.wait_ge(S["e_lnT_c"], 1)
            pe.wait_ge(S["ld_att"], 16 * N_ATT)
            mm(bank[3][:, 128:128 + V], attn_sb[:, :], lneT[:, :], start=True, stop=True).then_inc(S["e_pT"], 1)
            pe.wait_ge(S["e_pT_c"], 1)
            mm(bank[3][0:V, 256:256 + V], lneT[:, :], projT[:, :], start=True, stop=True).then_inc(S["e_sc"], 1)

            pe.wait_ge(S["ld_rout"], 16 * N_ROUT)
            for c in range(4):
                last = t.transpose(bank[0][:, c * P:(c + 1) * P], win_rows[:, c, :], ident[:, :])
            last.then_inc(S["w_tr"], 1)
            t.transpose(bank[1][:, 0:P], win_rows[:, 4, :], ident[:, :])
            t.transpose(bank[1][:, P:P + H], windt_rows[:, :], ident[0:H, 0:H])
            t.transpose(bank[1][:, P + H:P + H + DI // P], normw_rows, ident[0:DI // P, 0:DI // P])
            for c in range(DI // P):
                last = t.transpose(bank[1][:, (2 + c) * P - 64:(3 + c) * P - 64], wout_rows[:, c * P:(c + 1) * P], ident[:, :])
            last.then_inc(S["w_tr"], 1)
            t.transpose(bank[2][:, 0:P], tri1_rows[:, :], ident[:, :])
            t.transpose(bank[2][:, P:2 * P], tri2_rows[:, :], ident[:, :])
            t.transpose(bank[2][:, 2 * P:2 * P + E * FT], b1_rows[:, :], ident[0:E * FT, 0:E * FT]).then_inc(S["w_tr"], 1)

            pe.wait_ge(S["e_exp"], 1)
            pe.wait_ge(S["e_cnt"], 1)
            mm(bank[4][0:V, 0:B], expT[:, :], counts[:, :], start=True, stop=True).then_inc(S["e_den"], 1)
            pe.wait_ge(S["w_trc"], 3)
            with pe.Fori(1, B // GA // 2 + 1) as m:
                for q in range(2):
                    pe.wait_ge(S[f"at_w{q}"], m)
                    pe.wait_ge(S[f"at_h{q}"], m - 1)
                    mm(bank[q][0:V, :], expT[:, :], weighted[:, q].rearrange("p j d -> p (j d)"),
                       start=True, stop=True).then_inc(S[f"at_num{q}"], 1)
                for q in range(2):
                    pe.wait_ge(S[f"at_h{q}"], m)
                    pe.wait_ge(S[f"at_s{q}"], m - 1)
                    for j in range(GA):
                        last = t.transpose(bank[2 + q][:, j * V:(j + 1) * V], h1rows[:, q, j, :], ident[0:V, 0:V])
                    last.then_inc(S[f"at_t{q}"], 1)

            for q in range(2):
                pe.wait_ge(S[f"at_s{q}"], B // GA // 2)
            def routing_pe(m, r, valid):
                k = 2 * m + r
                if valid(0):
                    wait_past(pe, "r_c", k)
                    mm(bank[0][:, 0:N2], mean_w[:, :], hT[:, bass.ds(k * N2, N2)], start=True, stop=True).then_inc(S["r_mean"], 1)
                if valid(1):
                    pe.wait_ge(S["r_sq"], k)
                    wait_past(pe, "r_sd", k - 1)
                    mm(bank[1][:, 0:N2], mean_w[:, :], sqr2[:, 1 - r], start=True, stop=True).then_inc(S["r_var"], 1)
                if valid(2):
                    pe.wait_ge(S["r_x"], k - 1)
                    wait_past(pe, "r_lg", k - 2)
                    for j in range(2):
                        last = mm(bank[3][:, j * E:(j + 1) * E], xT_now[:, r, j * P:(j + 1) * P], router_sb[:, :], start=True, stop=True)
                    last.then_inc(S["r_rt"], 1)
                    wait_past(pe, "r_xf", k - 2)
                    for j in range(2):
                        last = t.transpose(bank[2][:, j * P:(j + 1) * P], xT_now[:, r, j * P:(j + 1) * P], ident[:, :])
                    last.then_inc(S["r_tr"], 1)

            rolling(pe, routing_pe, NI, 2, 2)

            def up(i, e, first):
                for hb in range(FT // 2):
                    k = 16 * (i - 1) + 2 * e + hb
                    if not (first and e < 1):
                        pe.wait_ge(S["b_relu"], k - 1)
                    u = bank[hb]
                    for f in range(2):
                        ft = 2 * hb + f
                        last = mm(u[:, f * N2:(f + 1) * N2], w1_sb[:, e, ft * P:(ft + 1) * P],
                                  xT[:, bass.ds((i - 1) * N2, N2)], start=True, stop=True)
                    last.then_inc(S["b_up"], 1)

            def down(i, e, first):
                pe.wait_ge(S["b_relu"], 16 * (i - 1) + 2 * e + 2)
                gg, k4 = divmod(e, 4)
                for j in range(2):
                    if k4 == 0 and not first:
                        pe.wait_ge(S[f"b_pre{gg}{j}"], i - 1)
                    for ft in range(FT):
                        last = mm(bank[2 + 2 * gg + j][:, k4 * P:(k4 + 1) * P], hid[:, e % 2, ft, j * P:(j + 1) * P],
                                  w2_sb[:, e, ft, :], start=(ft == 0), stop=(ft == FT - 1))
                    if k4 == 3 and j == 0:
                        last.then_inc(S["b_y"], 1)
                last.then_inc(S["b_dn"], 1)

            def sum_rows(i):
                pe.wait_ge(S["b_wtc"], i)
                pe.wait_ge(S["b_o"], i)
                mm(bank[6][:, 0:N2], beta_sb[:, :], wT_now[:, :], start=True, stop=False, skip_group_check=True)
                for j in range(2):
                    last = mm(bank[6][:, j * P:(j + 1) * P], summed[:, j, :], ident[:, :], start=False, stop=True, skip_group_check=True)
                last.then_inc(S["b_z"], 1)

            def expert_pe(i, first, cur, back):
                for e in range(E + 1):
                    if cur and e < E:
                        up(i, e, first)
                    if cur and e > 0:
                        down(i, e - 1, first)
                    if back and e == 4:
                        sum_rows(i - 1)
                    if back and e == 5:
                        pe.wait_ge(S["b_h2"], i - 1)
                        mm(bank[6][:, N2:2 * N2], mean_w[:, :], hT[:, bass.ds((i - 2) * N2, N2)], start=True, stop=True).then_inc(S["b_mean"], 1)
                    if back and e == 6:
                        pe.wait_ge(S["b_sq"], i - 1)
                        mm(bank[7][:, 0:N2], mean_w[:, :], sqr, start=True, stop=True).then_inc(S["b_v2"], 1)
                    if cur and e == 7:
                        pe.wait_ge(S["b_wn"], i)
                        if back:
                            pe.wait_ge(S["b_sd2"], i - 1)
                        for j in range(2):
                            last = t.transpose(bank[7][0:E, N2 + j * P:N2 + (j + 1) * P], w_now[:, j, :], ident[:, :])
                        last.then_inc(S["b_wt"], 1)

            pe.wait_ge(S["r_xf"], NI)
            pe.wait_ge(S["r_lg"], NI)
            pe.wait_ge(S["r_cp"], NI)
            pe.wait_ge(S["ld_ffn"], 16 * N_FFN)
            expert_pe(1, True, True, False)
            with pe.Fori(2, NI + 1) as i:
                expert_pe(i, False, True, True)
            expert_pe(NI + 1, False, False, True)

            with pe.Fori(1, B // GD // 2 + 1) as m:
                for q in range(2):
                    pe.wait_ge(S["s_in1" if q else "s_in"], m)
                    for j in range(GD):
                        last = mm(bank[0][0:V, bass.ds((2 * m - 2 + q) * GD * H + j * H, H)], dt_in[:, q, j * V:(j + 1) * V], windt_T[:, :],
                                  start=True, stop=True)
                    last.then_inc(S["s_raw"], 1)

            def tables(b, q, first):
                pe.wait_ge(S["c_seq"], b + 1)
                pe.wait_ge(S["c_zt"], b)
                pe.wait_ge(S["c_ht"], b)
                mm(bank[0][0:V, 0:BANK], xT_seq[:, q % 2], win_T[:, 0:BANK], start=True, stop=True)
                mm(bank[1][0:V, 0:P], xT_seq[:, q % 2], win_T[:, BANK:NZX], start=True, stop=True)
                t.transpose(bank[1][0:V, P:2 * P], hT_seq[:, q % 2], ident[:, :])
                for c in range(2):
                    last = mm(bank[1][:, 2 * P + 2 * H * c:2 * P + 2 * H * (c + 1)], hot[0:V, q, PAD + c * P:PAD + (c + 1) * P],
                              dt_tab[:, bass.ds(b, 1), :, :].rearrange("v a k h -> v (a k h)"), start=True, stop=True)
                last.then_inc(S["c_tab"], 1)

            def convolve(n, q, c, ks):
                if ks[0] == 0:
                    pe.wait_ge(S["c_taps"], half(n, c) + 1)
                    pe.wait_ge(S["c_x"], n)
                for k in ks:
                    last = mm(bank[2][:, 0:CONV], hot[:, q, c * P + k:c * P + k + P], taps[:, q % 2, k, :],
                              start=(k == 0), stop=(k == TAPS - 1), skip_group_check=True)
                if k == TAPS - 1:
                    last.then_inc(S["c_cv"], 1)

            def decay_sums(n, c):
                pe.wait_ge(S["c_mask"], n + 1)
                pe.wait_ge(S["c_dec"], n)
                mm(bank[3][:, :], later[:, :], amask[:, c].rearrange("p h l -> p (h l)"), start=True, stop=True).then_inc(S["c_seg"], 1)

            def turn_bc(n, q, c):
                pe.wait_ge(S["c_x"], n + 1)
                pe.wait_ge(S["c_cbm"], n)
                mm(bank[4][:, 2 * P:2 * P + H], (upper if c else later)[:, :], dts[:, q % 2, c, H:2 * H], start=True, stop=True)
                t.transpose(bank[4][0:NS, 0:P], xbc[:, c, DI:DI + NS], ident[:, :])
                t.transpose(bank[4][0:NS, P:2 * P], xbc[:, c, DI + NS:CONV], ident[:, :]).then_inc(S["c_bc"], 1)

            def scores(n, c):
                pe.wait_ge(S["c_edc"], n + 1)
                mm(bank[4][:, 3 * P:4 * P], bcT[:, c, 0:P], bcT[:, c, P:2 * P], start=True, stop=True).then_inc(S["c_cb"], 1)

            def mixed(n, c):
                pe.wait_ge(S["c_mix"], n + 1)
                pe.wait_ge(S["c_xsk"], n + 1)
                pe.wait_ge(S["c_y"], n)
                if c == 0:
                    pe.wait_ge(S["c_xtl"], half(n, 0) + 1)
                    mm(bank[6][0:NS, DI:2 * DI], xbc[:, c, DI:DI + NS], xtail[:, :], start=True, stop=True).then_inc(S["c_st"], 1)
                else:
                    pe.wait_ge(S["c_stc"], half(n, 1) + 1)
                    mm(bank[5][:, DI:2 * DI], bcT[:, c, P:2 * P], state[:, :], start=True, stop=True)
                for h in range(H):
                    last = mm(bank[5][:, h * HD:(h + 1) * HD], mix[:, c, h, :], xdt[:, c, h * HD:(h + 1) * HD], start=True, stop=True)
                last.then_inc(S["c_yd"], 1)

            def gate_rows(n, q, c):
                pe.wait_ge(S["c_g"], n)
                mm(bank[6][:, 0:DI], hot[0:V, q, PAD + c * P:PAD + (c + 1) * P], ztab[:, q, :], start=True, stop=True).then_inc(S["c_zg"], 1)

            def turn_gated(n):
                pe.wait_ge(S["c_h3"], n)
                pe.wait_ge(S["c_g"], n + 1)
                for c in range(DI // P):
                    last = t.transpose(bank[7][:, c * P:(c + 1) * P], gated[:, c * P:(c + 1) * P], ident[:, :])
                last.then_inc(S["c_gt"], 1)

            def project(n, q, c):
                pe.wait_ge(S["c_gtc"], n + 1)
                o = bank[7][:, DI:DI + P]
                mm(o, hot[0:V, q, PAD + c * P:PAD + (c + 1) * P], htab[:, q, :], start=True, stop=False)
                mm(o, gT[:, 0:P], wout_T[:, 0, :], start=False, stop=False)
                mm(o, gT[:, P:2 * P], wout_T[:, 1, :], start=False, stop=True).then_inc(S["c_out"], 1)

            def step(m, r, valid):
                k = STEPS * m + r
                c2, q2 = spot(r, 2)
                c3, q3 = spot(r, 3)
                c4, q4 = spot(r, 4)
                if valid(3):
                    decay_sums(k - 3, c3)
                    turn_bc(k - 3, q3, c3)
                if valid(2):
                    convolve(k - 2, q2, c2, (0, 1))
                if valid(3):
                    scores(k - 3, c3)
                if valid(2):
                    convolve(k - 2, q2, c2, (2, 3))
                if valid(4):
                    turn_gated(k - 4)
                if valid(3):
                    gate_rows(k - 3, q3, c3)
                    mixed(k - 3, c3)
                if valid(4):
                    project(k - 4, q4, c4)
                if r % 2 == 0 and valid(0):
                    tables(4 * m + r // 2, r // 2, isinstance(m, int) and m == 0)

            pe.wait_ge(S["s_dt"], 1)
            pipeline(pe, step)

            pe.wait_ge(S["c_h3"], NCH)
            def mlp_pe(m, r, valid):
                k = 4 * m + r
                if valid(1):
                    q = (r - 1) % 2
                    pe.wait_ge(S["m_xn"], k)
                    wait_past(pe, "m_xtc", k - 2)
                    for c in range(TD):
                        last = t.transpose(bank[q][:, c * P:(c + 1) * P], xn[:, q, c, :], ident[:, :])
                    last.then_inc(S["m_xt"], 1)
                if valid(2):
                    q = r % 2
                    pe.wait_ge(S["m_xtc"], k - 1)
                    wait_past(pe, "m_gel", k - 3)
                    mm(bank[2 + q][:, :], tri1_T[:, :], xnT[:, q, :], start=True, stop=True).then_inc(S["m_1"], 1)
                if valid(3):
                    q = (r - 1) % 2
                    pe.wait_ge(S["m_gel"], k - 2)
                    wait_past(pe, "m_fin", k - 4)
                    for c in range(TD):
                        last = mm(bank[4 + q][:, c * P:(c + 1) * P], gel[:, q, c * P:(c + 1) * P], tri2_T[:, :], start=True, stop=True)
                    last.then_inc(S["m_2"], 1)

            rolling(pe, mlp_pe, NT, 4, 3)

        @block.scalar
        def _(act):
            a = nc.scalar
            act.wait_ge(S["e_var"], 1)
            a.activation(stat[0:V, 9:10], stat[0:V, 8:9], ACT.Sqrt).then_inc(S["e_sd"], 1)
            act.wait_ge(S["e_sc"], 1)
            a.activation(tanh_s[:, :], bank[3][0:V, 256:256 + V], ACT.Tanh).then_inc(S["e_tanh"], 1)
            act.wait_ge(S["e_tanh"], 1)
            a.activation(expT[:, :], tanh_s[:, :], ACT.Exp).then_inc(S["e_exp"], 1)

            act.wait_ge(S["e_cnt"], 1)
            act.wait_ge(S["e_rden"], 1)
            with act.Fori(1, B // GA // 2 + 1) as m:
                for q in range(2):
                    act.wait_ge(S[f"at_num{q}"], m - 1)
                    for j in range(GA):
                        last = a.activation(weighted[:, q, j, :], lne[:, :], ACT.Copy,
                                            scale=counts[:, bass.ds((2 * (m - 1) + q) * GA + j, 1)])
                    last.then_inc(S[f"at_w{q}"], 1)
                for q in range(2):
                    act.wait_ge(S[f"at_t{q}"], m)
                    a.copy(hT[:, bass.ds((2 * (m - 1) + q) * GA * V, GA * V)], bank[2 + q][:, 0:GA * V]).then_inc(S[f"at_s{q}"], 1)

            def routing_act(m, r, valid):
                k = 2 * m + r
                if valid(2):
                    act.wait_ge(S["r_tr"], k - 1)
                    a.copy(xrows[:, bass.ds((k - 2) * N2, N2)], bank[2][:, 0:N2]).then_inc(S["r_xf"], 1)
                if valid(1):
                    act.wait_ge(S["r_var"], k)
                    wait_past(act, "r_x", k - 1)
                    a.activation(dev[:, :], bank[1][:, 0:N2], ACT.Sqrt, bias=eps_ln[:, :]).then_inc(S["r_sd"], 1)

            rolling(act, routing_act, NI, 2, 2)
            act.wait_ge(S["r_gd"], 1)
            a.activation(gexp[:, :], gdiff[:, :], ACT.Exp).then_inc(S["r_ge"], 1)

            def relu(i, e, first):
                for hb in range(FT // 2):
                    k = 16 * (i - 1) + 2 * e + hb
                    act.wait_ge(S["b_up"], k + 1)
                    if hb == 0 and not (first and e < 2):
                        act.wait_ge(S["b_dn"], 8 * (i - 1) + e - 1)
                    for f in range(2):
                        ft = 2 * hb + f
                        last = a.activation(hid[:, e % 2, ft, :], bank[hb][:, f * N2:(f + 1) * N2], ACT.Relu,
                                            bias=b1_col[:, e * FT + ft:e * FT + ft + 1])
                    last.then_inc(S["b_relu"], 1)

            def expert_act(i, first, cur, back):
                for e in range(E):
                    if cur:
                        relu(i, e, first)
                    if back and e == 0:
                        act.wait_ge(S["b_var"], i - 1)
                        a.activation(sm[:, 5, :], sm[:, 4, :], ACT.Sqrt, bias=eps_ffn[:, :], scale=1.0 / D).then_inc(S["b_sd"], 1)
                    if back and e == 6:
                        act.wait_ge(S["b_v2"], i - 1)
                        a.activation(dev[:, :], bank[7][:, 0:N2], ACT.Sqrt, bias=eps_ln[:, :]).then_inc(S["b_sd2"], 1)
                    if cur and e == 7:
                        act.wait_ge(S["b_wt"], i)
                        if back:
                            act.wait_ge(S["b_z"], i - 1)
                        a.copy(wT_now[:, :], bank[7][0:E, N2:2 * N2]).then_inc(S["b_wtc"], 1)

            act.wait_ge(S["w_trc"], 3)
            expert_act(1, True, True, False)
            with act.Fori(2, NI + 1) as i:
                expert_act(i, False, True, True)
            expert_act(NI + 1, False, False, True)

            act.wait_ge(S["b_x"], NI)
            with act.Fori(1, B // GD // 2 + 1) as m:
                act.wait_ge(S["s_raw"], 2 * m - 2)
                a.copy(dt_in[:, 1], xT[:, bass.ds((2 * m - 1) * GD * V, GD * V)]).then_inc(S["s_in1"], 1)

            act.wait_ge(S["s_v"], 1)
            a.activation(dt_t[:, 1, :], dt_t[:, 1, :], ACT.Exp, scale=-1.0).then_inc(S["s_e"], 1)
            act.wait_ge(S["s_v"], 2)
            a.activation(dt_t[:, 4, :], dt_t[:, 2, :], ACT.Ln).then_inc(S["s_l"], 1)
            act.wait_ge(S["ld_ssm"], 16 * N_SSM)
            a.activation(a_neg[:, :], alog_bc[:, :], ACT.Exp).then_inc(S["s_l"], 1)

            def tables(b, q):
                act.wait_ge(S["c_tab"], b + 1)
                act.wait_ge(S["c_taps"], b)
                a.copy(xtab[:, 0:DI], bank[0][0:V, DI:2 * DI])
                a.copy(xtab[:, DI:CONV], bank[1][0:V, 0:P]).then_inc(S["c_tx"], 1)
                a.copy(htab[:, q, :], bank[1][0:V, P:2 * P])
                if not (isinstance(b, int) and b < 1):
                    act.wait_ge(S["c_xsk"], 2 * b - 2)
                    act.wait_ge(S["c_bc"], 2 * b - 2)
                a.copy(dts[:, q % 2].rearrange("p c h -> p (c h)"), bank[1][:, 2 * P:2 * P + 4 * H]).then_inc(S["c_ht"], 1)
                a.activation(tanh_z[:, :], bank[0][0:V, 0:DI], ACT.Tanh).then_inc(S["c_tz"], 1)

            def conv_tanh(n):
                act.wait_ge(S["c_cv"], n + 1)
                a.activation(tanh_x[:, :], bank[2][:, 0:CONV], ACT.Tanh).then_inc(S["c_tanh"], 1)

            def decays(n, r):
                if not (isinstance(n, int) and n < 1):
                    act.wait_ge(S["c_mix"], n - 1)
                act.wait_ge(S["c_seg"], n + 1)
                a.activation(decay[:, r].rearrange("p h l -> p (h l)"), bank[3][:, :], ACT.Exp).then_inc(S["c_dec"], 1)

            def edges(n, r):
                if not (isinstance(n, int) and n < 1):
                    act.wait_ge(S["c_y"], n - 1)
                act.wait_ge(S["c_bc"], n + 1)
                a.copy(bcT[:, r, :], bank[4][0:NS, 0:2 * P])
                a.activation(edge[:, r, :], bank[4][:, 2 * P:2 * P + H], ACT.Exp).then_inc(S["c_edc"], 1)

            def square_sum(n, r):
                act.wait_ge(S["c_y"], n + 1)
                a.activation(ysq[:, :], y[:, r, :], ACT.Square, accum_out=ssum[:, :]).then_inc(S["c_bn"], 1)
                act.wait_ge(S["c_bn"], n + 1)
                act.wait_ge(S["c_rms"], n)
                a.mul(ms[:, :], ssum[:, :], 1.0 / DI).then_inc(S["c_sq"], 1)

            def step(m, r, valid):
                k = STEPS * m + r
                c3, c4 = (spot(r, lag)[0] for lag in (3, 4))
                if valid(4):
                    square_sum(k - 4, c4)
                if valid(3):
                    decays(k - 3, c3)
                    edges(k - 3, c3)
                if valid(2):
                    conv_tanh(k - 2)
                if valid(4):
                    act.wait_ge(S["c_gt"], k - 3)
                    a.copy(gT[:, :], bank[7][:, 0:DI]).then_inc(S["c_gtc"], 1)
                if valid(4):
                    act.wait_ge(S["c_out"], k - 3)
                    a.copy(h3[:, bass.ds((k - 4) * P, P)], bank[7][:, DI:DI + P]).then_inc(S["c_h3"], 1)
                if r % 2 == 0 and valid(0):
                    tables(4 * m + r // 2, r // 2)

            act.wait_ge(S["s_dt"], 1)
            pipeline(act, step)

            act.wait_ge(S["f_st"], 1)
            a.activation(h3_s[:, 3, :], h3_s[:, 2, :], ACT.Sqrt, bias=eps_ln[:, :], scale=1.0 / D).then_inc(S["f_sd"], 1)
            act.wait_ge(S["ld_mlp"], 16 * N_MLP)
            def mlp_act(m, r, valid):
                k = 4 * m + r
                if valid(2):
                    act.wait_ge(S["m_1"], k - 1)
                    wait_past(act, "m_2", k - 3)
                    a.activation(gel[:, r % 2, :], bank[2 + r % 2][:, :], ACT.Gelu, bias=trib1_col[:, :]).then_inc(S["m_gel"], 1)

            rolling(act, mlp_act, NT, 4, 3)

        @block.vector
        def _(dve):
            v = nc.vector
            chain = Chain(dve, "dchain")
            link = chain.link

            dve.wait_ge(S["ld_att"], 16 * N_ATT)
            link(v.bn_stats(stat[0:V, 0:6], emb_sb[:, :]))
            link(v.bn_aggr(stat[0:V, 6:8], stat[0:V, 0:6]))
            v.tensor_scalar(stat[0:V, 8:9], stat[0:V, 7:8], EPS_LN, None, ALU.add).then_inc(S["e_var"], 1)
            dve.wait_ge(S["e_sd"], 1)
            link(v.reciprocal(stat[0:V, 10:11], stat[0:V, 9:10]))
            v.tensor_scalar(lne[:, :], emb_sb[:, :], stat[0:V, 6:7], stat[0:V, 10:11], ALU.subtract, ALU.mult).then_inc(S["e_ln"], 1)
            dve.wait_ge(S["e_lnT"], 1)
            v.tensor_copy(lneT[:, :], bank[3][:, 0:V]).then_inc(S["e_lnT_c"], 1)
            dve.wait_ge(S["e_pT"], 1)
            v.tensor_copy(projT[:, :], bank[3][:, 128:128 + V]).then_inc(S["e_pT_c"], 1)

            dve.wait_ge(S["const_ok"], 10)
            for n in range(B // TOKB):
                dve.wait_ge(S[f"tok_ld{n % TOKN}"], 16 * (n // TOKN + 1))
                hots = onehot[:, n * TOKB:(n + 1) * TOKB, PAD:PAD + T]
                ins = v.tensor_scalar(hots, tok[:, n % TOKN], vocab[:, :], None, ALU.is_equal)
                ins.then_inc(S["tok_used"], 1)
                dve.wait_ge(S["tok_used"], n + 1)
                last = v.tensor_reduce(counts[:, n * TOKB:(n + 1) * TOKB], hots, AX.X, ALU.add)
            last.then_inc(S["e_cnt"], 1)

            dve.wait_ge(S["w_tr"], 1)
            v.tensor_scalar(win_T[:, 0:DI], bank[0][:, 0:DI], 0.5, None, ALU.mult)
            v.tensor_copy(win_T[:, DI:BANK], bank[0][:, DI:BANK]).then_inc(S["w_trc"], 1)
            dve.wait_ge(S["w_tr"], 2)
            v.tensor_copy(win_T[:, BANK:NZX], bank[1][:, 0:P])
            v.tensor_copy(windt_T[:, :], bank[1][:, P:P + H])
            v.tensor_copy(normw_col[:, :], bank[1][:, P + H:P + H + DI // P]).then_inc(S["w_nw"], 1)
            dve.wait_ge(S["w_nw"], 1)
            for c in range(DI // P):
                last = v.tensor_scalar(wout_T[:, c, :], bank[1][:, (2 + c) * P - 64:(3 + c) * P - 64], normw_col[:, c:c + 1], None, ALU.mult)
            last.then_inc(S["w_trc"], 1)
            dve.wait_ge(S["w_tr"], 3)
            v.tensor_tensor(tri1_T[:, :], bank[2][:, 0:P], upper[:, :], ALU.mult)
            v.tensor_tensor(tri2_T[:, :], bank[2][:, P:2 * P], upper[:, :], ALU.mult)
            v.tensor_copy(b1_col[:, :], bank[2][:, 2 * P:2 * P + E * FT]).then_inc(S["w_trc"], 1)

            dve.wait_ge(S["e_den"], 1)
            v.reciprocal(rden[:, :], bank[4][0:V, 0:B]).then_inc(S["e_rden"], 1)
            dve.wait_ge(S["e_rden"], 1)
            with dve.Fori(1, B // GA // 2 + 1) as m:
                for q in range(2):
                    dve.wait_ge(S[f"at_num{q}"], m)
                    dve.wait_ge(S[f"at_t{q}"], m - 1)
                    for j in range(GA):
                        last = v.scalar_tensor_tensor(out=h1rows[:, q, j, :], in0=bank[q][0:V, j * D:(j + 1) * D],
                                                      scalar=rden[:, bass.ds((2 * (m - 1) + q) * GA + j, 1)],
                                                      in1=emb_sb[:, :], op0=ALU.mult, op1=ALU.add)
                    last.then_inc(S[f"at_h{q}"], 1)

            for q in range(2):
                dve.wait_ge(S[f"at_s{q}"], B // GA // 2)

            def apart():
                dve.wait_ge(S["ld_att"], 16 * N_ATT)

            def routing_dve(m, r, valid):
                k = 2 * m + r
                if valid(0):
                    wait_past(dve, "r_x", k - 1)
                    dve.wait_ge(S["r_mean"], k + 1)
                    v.tensor_tensor(cen2[:, r], hT[:, bass.ds(k * N2, N2)], bank[0][:, 0:N2], ALU.subtract).then_inc(S["r_c"], 1)
                if valid(2):
                    now = dve.snap(k - 1) if not isinstance(k, int) else k - 1
                    dve.wait_ge(S["r_rt"], now)
                    v.tensor_copy(logit[:, :, :].rearrange("p j e -> p (j e)"), bank[3][:, 0:2 * E]).then_inc(S["r_lg"], 1)
                    apart()
                    dve.wait_ge(S["r_lg"], now)
                    v.max(top_v[:, 0, :], logit[:, 0, :])
                    v.max(top_v[:, 1, :], logit[:, 1, :]).then_inc(S["r_top"], 1)
                    apart()
                    dve.wait_ge(S["r_top"], now)
                    v.max_index(top_i[:, 0, :], top_v[:, 0, :], logit[:, 0, :])
                    v.max_index(top_i[:, 1, :], top_v[:, 1, :], logit[:, 1, :]).then_inc(S["r_ti"], 1)
                    dve.wait_ge(S["r_ti"], now)
                    v.tensor_copy(idxs[:, bass.ds(2 * (k - 2), 2), :], top_i[:, :, 0:2])
                    v.tensor_copy(vals[:, bass.ds(2 * (k - 2), 2), :], top_v[:, :, 0:2])
                if valid(1):
                    dve.wait_ge(S["r_sd"], k)
                    v.reciprocal(rstd[:, :], dev[:, :]).then_inc(S["rchain"], 1)
                    wait_past(dve, "r_cp", k - 2)
                    wait_past(dve, "r_tr", k - 2)
                    dve.wait_ge(S["rchain"], k)
                    v.tensor_tensor(xT_now[:, 1 - r], cen2[:, 1 - r], rstd[:, :], ALU.mult).then_inc(S["r_x"], 1)

            rolling(dve, routing_dve, NI, 2, 2)

            link(v.memset(stat[:, 15:16], 0.0))
            v.tensor_tensor(gdiff[:, :], vals[:, :, 1], vals[:, :, 0], ALU.subtract).then_inc(S["r_gd"], 1)
            dve.wait_ge(S["r_ge"], 1)
            link(v.tensor_scalar(gates[:, :, 1], gexp[:, :], 1.0, None, ALU.add))
            link(v.reciprocal(gates[:, :, 0], gates[:, :, 1]))
            link(v.tensor_tensor(gates[:, :, 1], gexp[:, :], gates[:, :, 0], ALU.mult))
            every = experts8[:, :].unsqueeze(1).to_broadcast([P, NTILE, E])
            for s in range(2):
                link(v.tensor_tensor(pick[:, :, :], every, idxs[:, :, s].unsqueeze(2).to_broadcast([P, NTILE, E]), ALU.is_equal))
                dst = pick if s else wgate
                link(v.tensor_tensor(dst[:, :, :], pick[:, :, :], gates[:, :, s].unsqueeze(2).to_broadcast([P, NTILE, E]), ALU.mult))
            v.tensor_tensor(wgate[:, :, :], wgate[:, :, :], pick[:, :, :], ALU.add).then_inc(S["r_gates"], 1)
            dve.wait_ge(S["r_gates"], 1)

            bch = Chain(dve, "bchain")

            def expert_sums(i, gg):
                for j in range(2):
                    k = 4 * (i - 1) + 2 * gg + j
                    if gg == 0:
                        wait_past(dve, "b_o", i - 1)
                    if j == 0:
                        dve.wait_ge(S["b_y"], 2 * (i - 1) + gg + 1)
                    else:
                        dve.wait_ge(S["b_dn"], 8 * (i - 1) + 4 * gg + 4)
                    dve.wait_ge(S["b_xb2"], k + 1)
                    v.tensor_tensor(pre[:, j, gg * BANK:(gg + 1) * BANK], bank[2 + 2 * gg + j][:, :], xb2[:, j, gg * BANK:(gg + 1) * BANK],
                                    ALU.add).then_inc(S[f"b_pre{gg}{j}"], 1)
                    dve.wait_ge(S[f"b_pre{gg}{j}"], i)
                    for e in range(4 * gg, 4 * gg + 4):
                        last = v.bn_stats(bns[:, j * E + e, :], pre[:, j, e * D:(e + 1) * D])
                if gg == 1:
                    last.then_inc(S["b_bn"], 1)

            def expert_norms(i, sums):
                bch.start((i - 1) * B_LINKS)
                col = [bns[:, :, c] for c in range(6)]
                dve.wait_ge(S["b_bn"], i)
                v.tensor_tensor(sm[:, 0, :], col[1], col[4], ALU.add)
                v.tensor_tensor(sm[:, 1, :], col[1], col[4], ALU.subtract)
                bch.link(v.tensor_tensor(sm[:, 2, :], col[2], col[5], ALU.add))
                v.tensor_scalar(sm[:, 0, :], sm[:, 0, :], 0.5, None, ALU.mult)
                bch.link(v.tensor_tensor(sm[:, 3, :], sm[:, 1, :], sm[:, 1, :], ALU.mult))
                v.scalar_tensor_tensor(out=sm[:, 4, :], in0=sm[:, 3, :], scalar=D / 4.0, in1=sm[:, 2, :],
                                       op0=ALU.mult, op1=ALU.add).then_inc(S["b_var"], 1)
                dve.wait_ge(S["b_sd"], i)
                bch.link(v.reciprocal(sm[:, 6, :], sm[:, 5, :]))
                bch.link(v.tensor_tensor(sm[:, 7, :].rearrange("p (j e) -> p j e", e=E), sm[:, 6, :].rearrange("p (j e) -> p j e", e=E),
                                         wgate[:, bass.ds(2 * (i - 1), 2), :], ALU.mult))
                for j in range(2):
                    for k in range(j * E, (j + 1) * E):
                        part = pre[:, k // E, (k % E) * D:(k % E + 1) * D]
                        last = v.tensor_scalar(part, part, sm[:, 0, k:k + 1], sm[:, 7, k:k + 1], ALU.subtract, ALU.mult)
                    last.then_inc(S["b_u"], 1)
                for j in range(2):
                    dve.wait_ge(S["b_ug"], 2 * i - 1 + j)
                    last = v.tensor_reduce(summed[:, j, :], pre[:, j, :].rearrange("p (e d) -> p d e", d=D), AX.X, ALU.add)
                last.then_inc(S["b_o"], 1)
                if sums:
                    expert_sums(i + 1, 0)
                now = bass.ds((i - 1) * N2, N2)
                dve.wait_ge(S["b_z"], i)
                v.tensor_tensor(hT[:, now], bank[6][:, 0:N2], hT[:, now], ALU.add).then_inc(S["b_h2"], 1)
                dve.wait_ge(S["b_mean"], i)
                v.tensor_tensor(cen, hT[:, now], bank[6][:, N2:2 * N2], ALU.subtract).then_inc(S["b_c"], 1)
                dve.wait_ge(S["b_sd2"], i)
                bch.link(v.reciprocal(rstd[:, :], dev[:, :]))
                v.tensor_tensor(xT[:, now], cen, rstd[:, :], ALU.mult).then_inc(S["b_x"], 1)

            expert_sums(1, 0)
            expert_sums(1, 1)
            with dve.Fori(2, NI + 1) as i:
                expert_norms(i - 1, True)
                assert bch.n == B_LINKS
                expert_sums(i, 1)
            expert_norms(NI, False)

            dve.wait_ge(S["b_x"], NI)
            with dve.Fori(1, B // GD // 2 + 1) as m:
                dve.wait_ge(S["s_raw"], 2 * m - 2)
                v.tensor_copy(dt_in[:, 0], xT[:, bass.ds((2 * m - 2) * GD * V, GD * V)]).then_inc(S["s_in"], 1)

            dve.wait_ge(S["s_raw"], B // GD)
            dve.wait_ge(S["ld_ssm"], 16 * N_SSM)
            link(v.tensor_tensor(dt_t[:, 0, :].rearrange("p (b h) -> p b h", h=H), bank[0][0:V, 0:B * H].rearrange("p (b h) -> p b h", h=H),
                                 dtb_bc[:, :].unsqueeze(1).to_broadcast([V, B, H]), ALU.add))
            link(v.tensor_scalar(dt_t[:, 2, :], dt_t[:, 0, :], -1.0, None, ALU.mult))
            v.tensor_tensor(dt_t[:, 1, :], dt_t[:, 0, :], dt_t[:, 2, :], ALU.max).then_inc(S["s_v"], 1)
            dve.wait_ge(S["s_e"], 1)
            v.tensor_scalar(dt_t[:, 2, :], dt_t[:, 1, :], 1.0, None, ALU.add).then_inc(S["s_v"], 1)
            dve.wait_ge(S["s_v"], 2)
            link(v.tensor_scalar(dt_t[:, 3, :], dt_t[:, 2, :], 1.0, None, ALU.subtract))
            dve.wait_ge(S["s_l"], 1)
            link(v.tensor_scalar(dt_t[:, 2, :], dt_t[:, 3, :], 0.0, None, ALU.is_equal))
            v.tensor_tensor(dt_t[:, 3, :], dt_t[:, 3, :], dt_t[:, 2, :], ALU.add)
            link(v.tensor_tensor(dt_t[:, 4, :], dt_t[:, 4, :], dt_t[:, 2, :], ALU.add))
            link(v.reciprocal(dt_t[:, 2, :], dt_t[:, 3, :]))
            link(v.tensor_tensor(dt_t[:, 4, :], dt_t[:, 4, :], dt_t[:, 2, :], ALU.mult))
            link(v.tensor_tensor(dt_t[:, 4, :], dt_t[:, 4, :], dt_t[:, 1, :], ALU.mult))
            by_seq = dt_t[:, :, :].rearrange("v k (b h) -> v k b h", h=H)
            v.scalar_tensor_tensor(out=dt_tab[:, :, 0, :], in0=by_seq[:, 0], scalar=0.0, in1=by_seq[:, 4], op0=ALU.max, op1=ALU.add)
            v.tensor_scalar(tapw[:, :, :], convw_raw.rearrange("p (c k) -> p k c", k=TAPS), 0.5, None, ALU.mult)
            v.tensor_scalar(convb_half[:, :], convb_row[:, :], 0.5, None, ALU.mult).then_inc(S["s_aneg"], 1)
            dve.wait_ge(S["s_l"], 2)
            link(v.tensor_scalar(a_neg[:, :], a_neg[:, :], -1.0, None, ALU.mult))
            link(v.tensor_tensor(dt_tab[:, :, 1, :], dt_tab[:, :, 0, :], a_neg[0:V, :].unsqueeze(1).to_broadcast([V, B, H]), ALU.mult))
            dve.wait_ge(S["zpad"], 32)
            v.memset(stat[:, 14:15], 0.0).then_inc(S["s_dt"], 1)

            cch = Chain(dve, "cchain")

            def z_table(b, q):
                dve.wait_ge(S["c_tz"], b + 1)
                dve.wait_ge(S["c_ht"], b + 1)
                v.scalar_tensor_tensor(out=ztab[:, q, :], in0=tanh_z[:, :], scalar=1.0, in1=bank[0][0:V, 0:DI],
                                       op0=ALU.add, op1=ALU.mult).then_inc(S["c_zt"], 1)

            def silu(n, r, c):
                if c == 0:
                    dve.wait_ge(S["c_st"], half(n, 0))
                dve.wait_ge(S["c_tanh"], n + 1)
                v.scalar_tensor_tensor(out=xbc[:, r, :], in0=tanh_x[:, :], scalar=1.0, in1=bank[2][:, 0:CONV],
                                       op0=ALU.add, op1=ALU.mult).then_inc(S["c_x"], 1)

            def causal_scores(n, r):
                dve.wait_ge(S["c_cb"], n + 1)
                v.tensor_tensor(cbm[:, r, :], bank[4][:, 3 * P:4 * P], upper[:, :], ALU.mult).then_inc(S["c_cbm"], 1)
                dve.wait_ge(S["c_cbm"], n + 1)
                dve.wait_ge(S["c_dec"], n + 1)
                v.tensor_tensor(mix[:, r], decay[:, r], cbm[:, r].unsqueeze(1).to_broadcast([P, H, P]), ALU.mult).then_inc(S["c_mix"], 1)

            def combine(n, r, c):
                dve.wait_ge(S["c_yd"], n + 1)
                dve.wait_ge(S["c_xsk"], n + 1)
                if c == 0:
                    v.tensor_copy(state[:, :], bank[6][0:NS, DI:2 * DI]).then_inc(S["c_stc"], 1)
                    v.tensor_tensor(y[:, r, :], bank[5][:, 0:DI], xskip[:, r, :], ALU.add).then_inc(S["c_y"], 1)
                else:
                    cch.start(2 * half(n, 1))
                    v.tensor_tensor(yoff[:, :].rearrange("p (h d) -> p h d", h=H), bank[5][:, DI:2 * DI].rearrange("p (h d) -> p h d", h=H),
                                    edge[:, r, :].unsqueeze(2).to_broadcast([P, H, HD]), ALU.mult)
                    cch.link(v.tensor_tensor(y[:, r, :], bank[5][:, 0:DI], xskip[:, r, :], ALU.add))
                    cch.link(v.memset(stat[:, 13:14], 0.0))
                    v.tensor_tensor(y[:, r, :], y[:, r, :], yoff[:, :], ALU.add).then_inc(S["c_y"], 1)

            def gate(n, r):
                dve.wait_ge(S["c_rms"], n + 1)
                v.tensor_scalar(rms[:, 1:2], rms[:, 0:1], EPS_RMS, None, ALU.add).then_inc(S["c_yo"], 1)
                dve.wait_ge(S["c_yo"], 2 * n + 1)
                v.reciprocal(rms[:, 2:3], rms[:, 1:2]).then_inc(S["c_yo"], 1)
                dve.wait_ge(S["c_yo"], 2 * n + 2)
                dve.wait_ge(S["c_zg"], n + 1)
                v.scalar_tensor_tensor(out=gated[:, :], in0=y[:, r, :], scalar=rms[:, 2:3], in1=bank[6][:, 0:DI],
                                       op0=ALU.mult, op1=ALU.mult).then_inc(S["c_g"], 1)

            def step(m, r, valid):
                k = STEPS * m + r
                c2, c3, c4 = (spot(r, lag)[0] for lag in (2, 3, 4))
                if valid(4):
                    gate(k - 4, c4)
                if valid(3):
                    causal_scores(k - 3, c3)
                if valid(2):
                    silu(k - 2, c2, c2)
                if valid(3):
                    combine(k - 3, c3, c3)
                if r % 2 == 0 and valid(0):
                    z_table(4 * m + r // 2, r // 2)
                if valid(4):
                    n = k - 4
                    dve.wait_ge(S["c_h3"], n + 1)
                    v.bn_stats(h3_bns[:, bass.ds(n, 1), :].rearrange("p a s -> p (a s)"), h3[:, bass.ds(n * P, P)]).then_inc(S["c_dt"], 1)

            dve.wait_ge(S["s_dt"], 1)
            pipeline(dve, step)

            dve.wait_ge(S["c_dt"], NCH)
            col = [h3_bns[:, :, c] for c in range(6)]
            v.tensor_tensor(h3_s[:, 0, :], col[1], col[4], ALU.add)
            v.tensor_tensor(h3_s[:, 1, :], col[1], col[4], ALU.subtract)
            link(v.tensor_tensor(h3_s[:, 2, :], col[2], col[5], ALU.add))
            v.tensor_scalar(h3_s[:, 0, :], h3_s[:, 0, :], 0.5, None, ALU.mult)
            link(v.tensor_tensor(h3_s[:, 3, :], h3_s[:, 1, :], h3_s[:, 1, :], ALU.mult))
            v.scalar_tensor_tensor(out=h3_s[:, 2, :], in0=h3_s[:, 3, :], scalar=D / 4.0, in1=h3_s[:, 2, :],
                                   op0=ALU.mult, op1=ALU.add).then_inc(S["f_st"], 1)
            dve.wait_ge(S["f_sd"], 1)
            link(v.reciprocal(h3_s[:, 4, :], h3_s[:, 3, :]))

            def mlp_dve(m, r, valid):
                k = 4 * m + r
                if valid(0):
                    wait_past(dve, "m_xt", k - 1)
                    for c in range(TD):
                        n = TD * k + c
                        last = v.tensor_scalar(xn[:, r % 2, c, :], h3[:, bass.ds(n * P, P)], h3_s[:, 0, bass.ds(n, 1)], h3_s[:, 4, bass.ds(n, 1)],
                                               ALU.subtract, ALU.mult)
                    last.then_inc(S["m_xn"], 1)
                if valid(1):
                    q = (r - 1) % 2
                    dve.wait_ge(S["m_xt"], k)
                    wait_past(dve, "m_1", k - 2)
                    v.tensor_copy(xnT[:, q, :], bank[q][:, :]).then_inc(S["m_xtc"], 1)
                if valid(3):
                    q = (r - 3) % 4
                    dve.wait_ge(S["m_2"], k - 2)
                    dve.wait_ge(S["m_res"], k - 2)
                    wait_past(dve, f"m_st{q}", 16 * (m + (r - 3 - q) // 4))
                    v.tensor_tensor(fin[:, q], bank[4 + q % 2][:, :].rearrange("p (c d) -> p c d", d=D), res[:, q], ALU.add).then_inc(S["m_fin"], 1)

            rolling(dve, mlp_dve, NT, 4, 3)


_INS = ['x', 'L0_tok_embed_weight', 'L0_attn_attention_weights', 'L0_ffn_router_w', 'L0_ffn_w1', 'L0_ffn_b1',
        'L0_ffn_w2', 'L0_ffn_b2', 'L0_ffn_gamma', 'L0_ffn_beta', 'L1_attn_W_in', 'L1_attn_conv_w',
        'L1_attn_conv_b', 'L1_attn_A_log', 'L1_attn_dt_bias', 'L1_attn_D', 'L1_attn_norm_w', 'L1_attn_W_out',
        'L1_ffn_W1', 'L1_ffn_b1', 'L1_ffn_W2', 'L1_ffn_b2']


def kernel(**inputs):
    import numpy as _np
    import concourse.bacc as _bacc
    from concourse import mybir as _mybir
    from concourse.bass_utils import run_bass_kernel_spmd as _run

    nc = _bacc.Bacc("TRN2", target_bir_lowering=False, num_devices=1)
    arrays, args = {}, []
    for name in _INS:
        a = _np.ascontiguousarray(inputs[name])
        arrays[f"in_{name}"] = a
        args.append(nc.dram_tensor(f"in_{name}", a.shape, _mybir.dt.from_np(a.dtype), kind="ExternalInput").ap())
    b, t = inputs['x'].shape
    d = inputs['L0_tok_embed_weight'].shape[1]
    out = nc.dram_tensor("out", (b, t, d), _mybir.dt.float32, kind="ExternalOutput").ap()
    lm_tower(nc, *args, out)
    r = _run(nc, [arrays], core_ids=[0])
    return r.results[0]["out"]
```

```python
from contextlib import ExitStack

import concourse.bass as bass
from concourse import mybir

F32 = mybir.dt.float32
F32R = mybir.dt.float32r
U8 = mybir.dt.uint8
I32 = mybir.dt.int32
U32 = mybir.dt.uint32
ALU = mybir.AluOpType
ACT = mybir.ActivationFunctionType
AX = mybir.AxisListType

P = 128
BANK = 512
EPS_LN = 1e-5
EPS_FFN = 1e-6
EPS_RMS = 1e-5


def lm_tower(nc, x, emb, attn_w, router_w, w1, b1, w2, b2, gamma, beta,
             W_in, conv_w, conv_b, A_log, dt_bias, Dskip, norm_w, W_out,
             tri_w1, tri_b1, tri_w2, tri_b2, out):
    B, T = x.shape
    V, D = emb.shape
    E, _, F = w1.shape
    FT = F // P
    CONV, _, TAPS = conv_w.shape
    H = A_log.shape[0]
    DI = norm_w.shape[0]
    HD = DI // H
    NS = (CONV - DI) // 2
    PAD = TAPS - 1
    RR = B * V
    N2 = 2 * P
    NI = RR // N2
    NTILE = RR // P
    CH = T // P
    NCH = B * CH
    assert D == P and CH == 2 and RR % N2 == 0 and V < P and F % P == 0

    ctx = ExitStack()
    with ctx:
        def sb(name, shape, dt=F32):
            return ctx.enter_context(nc.sbuf_tensor(name, shape, dt))

        def sem(name):
            return ctx.enter_context(nc.semaphore(name))

        bank = [ctx.enter_context(nc.psum_tensor(f"bank{i}", [P, BANK], F32)) for i in range(8)]

        REGION = 16384
        early = ExitStack()
        region = [early.enter_context(nc.sbuf_tensor("early", [P, REGION], F32, side="right"))]
        place = [0]

        def phase():
            place[0] = 0

        def take(shape, dt=F32):
            size = 1
            for s in shape[1:]:
                size *= s
            view = region[0][0:shape[0], place[0]:place[0] + size]
            place[0] += size
            assert place[0] <= region[0].shape[1], place[0]
            if dt != F32:
                view = view.bitcast(dt)
            if len(shape) > 2:
                axes = "abc"[:len(shape) - 1]
                view = view.rearrange(f"p ({' '.join(axes)}) -> p {' '.join(axes)}",
                                      **dict(zip(axes[1:], shape[2:])))
            return view

        ident = sb("ident", [P, P])
        upper = sb("upper", [P, P])
        later = sb("later", [P, P])
        mean_w = sb("mean_w", [P, P])
        vocab = sb("vocab", [V, 1])
        experts8 = sb("experts8", [P, E])
        half_pow = sb("half_pow", [P, 1])
        eps_ln = sb("eps_ln", [P, 1])
        eps_ffn = sb("eps_ffn", [P, 1])

        onehot = sb("onehot", [V, B, PAD + T], U8)
        hT = sb("hT", [P, RR])
        xT = sb("xT", [P, RR])
        arena = sb("arena", [P, NCH * P])
        w1_sb = arena[:, 0:E * F].rearrange("p (e f) -> p e f", e=E)
        w2_sb = arena[:, E * F:2 * E * F].rearrange("p (e c d) -> p e c d", e=E, c=FT)
        xrows = arena[:, 2 * E * F:2 * E * F + RR]
        TOKB = 8
        TOKN = 4
        tok = arena[0:V, 2 * E * F:2 * E * F + TOKN * TOKB * T].bitcast(I32).rearrange(
            "p (n b t) -> p n b t", n=TOKN, b=TOKB)
        h3 = arena[:, :]

        phase()
        gamma_bc = take([P, E * D])
        b2_bc = take([P, E * D])
        cen2, sqr2 = (take([P, 2, N2]) for _ in range(2))
        cen, sqr = cen2[:, 0, :], sqr2[:, 0, :]
        dev, rstd = (take([P, N2]) for _ in range(2))
        kept = place[0]
        emb_sb = sb("emb_sb", [V, D])
        attn_sb = sb("attn_sb", [D, D])
        router_sb = sb("router_sb", [D, E])
        b1_rows = take([E * FT, P])
        b1_col = sb("b1_col", [P, E * FT])
        beta_sb = sb("beta_sb", [E, D])
        NZX = 2 * DI + 2 * NS
        win_rows = take([P, NZX // P, D])
        windt_rows = take([H, D])
        win_T = sb("win_T", [D, NZX])
        windt_T = sb("windt_T", [D, H])
        convw_raw = arena[0:V, 2 * E * F:2 * E * F + CONV * TAPS]
        tapw = sb("tapw", [V + 1, TAPS, CONV])
        ones = sb("ones", [P, 1])
        convb_row = sb("convb_row", [1, CONV])
        convb_half = sb("convb_half", [1, CONV])
        a_neg = sb("a_neg", [P, H])
        alog_bc = sb("alog_bc", [P, H])
        dtb_bc = sb("dtb_bc", [V, H])
        d_bc = sb("d_bc", [P, H])
        normw_col = sb("normw_col", [P, DI // P])
        normw_rows = take([DI // P, P])
        wout_rows = take([D, DI])
        wout_T = sb("wout_T", [P, DI // P, D])
        tri1_rows = take([P, P])
        tri2_rows = take([P, P])
        tri1_T = sb("tri1_T", [P, P])
        tri2_T = sb("tri2_T", [P, P])
        trib1_col = sb("trib1_col", [P, 1])
        trib2_bc = sb("trib2_bc", [P, P])

        counts = sb("counts", [V, B])
        rden = sb("rden", [V, B])
        lne = take([V, D])
        lneT = take([D, V])
        projT = take([D, V])
        tanh_s = take([V, V])
        expT = take([V, V])
        stat = sb("stat", [P, 16])
        GA = 4
        weighted = take([V, 2, GA, D])
        h1rows = take([V, 2, GA, D])

        xT_now = take([P, 2, N2])
        logit = take([P, 2, E])
        top_v = take([P, 2, 8])
        top_i = take([P, 2, 8], U32)
        vals = take([P, NTILE, 2])
        idxs = take([P, NTILE, 2])
        gdiff = take([P, NTILE])
        gexp = take([P, NTILE])
        gates = take([P, NTILE, 2])
        pick = take([P, NTILE, E])
        wgate = sb("wgate", [P, NTILE, E])

        place[0] = kept
        hid = take([P, 2, FT, N2])
        xb2 = take([P, 2, E * D])
        pre = take([P, 2, E * D])
        bns = take([P, 2 * E, 6])
        sm = take([P, 8, 2 * E])
        summed = take([P, 2, D])
        w_now = take([P, 2, E])
        wT_now = take([E, N2])

        GD = 8
        early.close()

        def rounded(name, shape):
            return ctx.enter_context(nc.sbuf_tensor(name, shape, F32R, side="right"))

        hot_r = rounded("hot_r", [V + 1, 4, PAD + T])
        hot = hot_r[:, :, :].bitcast(F32)
        taps_hi = rounded("taps_hi", [V + 1, 2, TAPS, CONV])
        taps_lo = rounded("taps_lo", [V + 1, 2, TAPS, CONV])
        region[0] = ctx.enter_context(nc.sbuf_tensor("late", [P, REGION - 4 * (PAD + T) - 4 * TAPS * CONV - 4], F32, side="right"))
        phase()
        dt_in = take([D, 2, GD * V])
        dt_t = take([V, 5, B * H])
        phase()
        xT_seq = take([D, 2, V])
        hT_seq = take([D, 2, V])
        dt_tab = sb("dt_tab", [V, B, 2, H])
        ztab = take([V, 4, DI])
        xtab = take([V + 1, CONV])
        products = take([V + 1, 2, CONV])
        htab = take([V, 4, D])
        tanh_x = take([P, CONV])
        xbc = take([P, 2, CONV])
        dts = take([P, 4, 2, 2 * H])
        amask = take([P, H, P])
        xdt = take([P, 2, DI])
        xskip = take([P, 2, DI])
        xtail = take([P, DI])
        yoff = xtail
        bcT = take([NS, 2, 2 * P])
        cbm = take([P, 2, P])
        edge = take([P, 2, H])
        decay = take([P, 2, H, P])
        state = take([NS, DI])
        y = take([P, 2, DI])
        ssum = take([P, 1])
        ms = take([P, 1])
        rms = take([P, 3])
        gated = take([P, DI])
        gT = take([P, DI])

        h3_bns = sb("h3_bns", [P, NCH, 6])
        h3_s = sb("h3_s", [P, 5, NCH])
        TD = 4
        phase()
        NT = NCH // TD
        xn = take([P, 2, TD, D])
        xnT = take([P, 2, TD * P])
        gel = take([P, 2, TD * P])
        res = take([P, 4, TD, D])
        fin = take([P, 4, TD, D])

        names = """ld_att ld_ffn ld_ssm ld_mlp ld_rout const_ok zero_ok tok_ld0 tok_ld1 tok_ld2 tok_ld3
            tok_used dchain e_var e_sd e_ln e_lnT e_lnT_c e_pT e_pT_c e_sc e_tanh e_exp e_cnt
            e_den e_rden w_tr w_trc at_w0 at_w1 at_num0 at_num1 at_h0 at_h1 at_t0 at_t1 at_s0
            at_s1 r_mean r_c r_sq r_var r_sd r_x r_cp r_tr r_rt r_xf r_lg r_gd r_ge r_gates b_up
            b_relu b_dn b_y b_xb2 b_pre00 b_pre01 b_pre10 b_pre11 b_var b_sd b_u b_ug b_o b_z
            b_h2 b_mean b_c b_sq b_v2 b_sd2 b_x b_wn b_wt b_wtc rchain bchain s_in s_in1 s_raw
            s_v s_e s_l s_dt s_aneg c_seq c_tab c_tx c_tz c_zt c_ht c_taps c_cv c_tanh c_x c_dt
            c_mask c_xsk c_xtl c_bc c_cb c_cbm c_seg c_dec c_edc c_mix c_yd c_st c_stc c_yo c_y
            c_sq c_rms c_zg c_g c_gt c_gtc c_out c_h3 c_bn gchain f_st f_sd m_xn m_xt m_xtc m_1
            m_gel m_2 m_res m_fin m_st0 m_st1 m_st2 m_st3 zpad taps0 w_nw r_top r_ti b_bn c_prod
            c_hi c_ones c_yin c_dts""".split()
        S = {n: sem(n) for n in names}

        class Chain:

            def __init__(self, eng, name):
                self.eng, self.sem, self.base, self.n = eng, S[name], 0, 0

            def start(self, base):
                self.base, self.n = base, 0

            def link(self, ins):
                self.n += 1
                ins.then_inc(self.sem, 1)
                self.eng.wait_ge(self.sem, self.base + self.n)

        def bc_rows(ap, n):
            return ap.unsqueeze(0).to_broadcast([n] + list(ap.shape))

        def flat(ap):
            return ap.rearrange("e d -> (e d)")

        R_LINKS, B_LINKS = 2, 5
        C_LINKS_D, C_LINKS_P = 3, 1
        POST = [TAPS]

        STEPS = 8

        def rolling(eng, step, count, body, depth):
            first = -(-depth // body)
            full = count // body
            for k in range(first * body):
                step(k // body, k % body, lambda lag: k >= lag)
            with eng.Fori(first, full) as m:
                for r in range(body):
                    step(m, r, lambda lag: True)
            for k in range(full * body, count + depth):
                step(k // body, k % body, lambda lag: k - lag < count)

        def pipeline(eng, step):
            rolling(eng, step, NCH, STEPS, 6)

        def wait_past(eng, name, value):
            if not (isinstance(value, int) and value <= 0):
                eng.wait_ge(S[name], value)

        def spot(r, lag):
            s = (r - lag) % STEPS
            return s % 2, s // 2

        def half(n, c):
            return (n - c) // 2

        block = ctx.enter_context(nc.Block())

        @block.sync
        def _(sp):
            att = [(emb_sb[:, :], emb), (attn_sb[:, :], attn_w)]
            for dst, src in att:
                sp.dma_start(dst, src).then_inc(S["ld_att"], 16)
            for n in range(TOKN):
                sp.dma_start(tok[:, n], bc_rows(x[n * TOKB:(n + 1) * TOKB, :], V)).then_inc(S[f"tok_ld{n}"], 16)
            rout = [(router_sb[:, :], router_w), (b1_rows[:, :], b1.rearrange("e (c p) -> (e c) p", p=P)),
                    (win_rows[:, :, :], W_in[0:NZX, :].rearrange("(c p) d -> p c d", p=P)),
                    (windt_rows[:, :], W_in[NZX:NZX + H, :]),
                    (wout_rows[:, :], W_out), (tri1_rows[:, :], tri_w1), (tri2_rows[:, :], tri_w2),
                    (normw_rows, norm_w.rearrange("(c p) -> c p", p=P))]
            for dst, src in rout:
                sp.dma_start(dst, src).then_inc(S["ld_rout"], 16)
            for n in range(TOKN, B // TOKB):
                sp.wait_ge(S["tok_used"], n - TOKN + 1)
                sp.dma_start(tok[:, n % TOKN], bc_rows(x[n * TOKB:(n + 1) * TOKB, :], V)).then_inc(
                    S[f"tok_ld{n % TOKN}"], 16)
            ffn = [(w1_sb, w1.rearrange("e d f -> d e f")),
                   (b2_bc[:, :], bc_rows(flat(b2), P)), (gamma_bc[:, :], bc_rows(flat(gamma), P)),
                   (beta_sb[:, :], beta)]
            for dst, src in ffn:
                sp.dma_start(dst, src).then_inc(S["ld_ffn"], 16)
            for e in range(E):
                sp.dma_start(w2_sb[:, e], w2[e].rearrange("(c p) d -> p c d", p=P)).then_inc(S["ld_ffn"], 16)
            ssm = [(convw_raw, bc_rows(conv_w.rearrange("c o k -> (c o k)"), V)),
                   (convb_row[:, :], bc_rows(conv_b, 1)), (alog_bc[:, :], bc_rows(A_log, P)),
                   (dtb_bc[:, :], bc_rows(dt_bias, V)), (d_bc[:, :], bc_rows(Dskip, P))]
            sp.wait_ge(S["b_x"], NI)
            for dst, src in ssm:
                sp.dma_start(dst, src).then_inc(S["ld_ssm"], 16)
            mlp = [(trib1_col[:, :], tri_b1.unsqueeze(1)), (trib2_bc[:, :], bc_rows(tri_b2, P))]
            for dst, src in mlp:
                sp.dma_start(dst, src).then_inc(S["ld_mlp"], 16)
            sp.wait_ge(S["s_aneg"], 1)
            sp.dma_start(tapw[V:V + 1, TAPS - 1, :], convb_half[:, :]).then_inc(S["zpad"], 16)
            rows = out.rearrange("b (c p) d -> p (b c) d", p=P)
            with sp.Fori(1, NT // 4 + 1) as m:
                for q in range(4):
                    sp.wait_ge(S["m_fin"], 4 * m - 3 + q)
                    sp.dma_start(rows[:, bass.ds(4 * TD * m - (4 - q) * TD, TD), :], fin[:, q]).then_inc(S[f"m_st{q}"], 16)
            for q in range(4):
                sp.wait_ge(S[f"m_st{q}"], 16 * (NT // 4))

        N_ATT, N_ROUT, N_FFN, N_SSM, N_MLP = 2, 8, 4 + E, 5, 2

        @block.gpsimd
        def _(pool):
            g = nc.gpsimd
            g.memset(ident[:, :], 0.0).then_inc(S["zero_ok"], 1)
            g.memset(upper[:, :], 1.0).then_inc(S["zero_ok"], 1)
            g.memset(later[:, :], 1.0).then_inc(S["zero_ok"], 1)
            pool.wait_ge(S["zero_ok"], 3)
            g.affine_select(out=ident[:, :], in_=ident[:, :], compare_op=ALU.not_equal, fill=1.0, base=0,
                            pattern=[[-1, P]], channel_multiplier=1).then_inc(S["const_ok"], 1)
            g.affine_select(out=upper[:, :], in_=upper[:, :], compare_op=ALU.is_ge, fill=0.0, base=0,
                            pattern=[[1, P]], channel_multiplier=-1).then_inc(S["const_ok"], 1)
            g.affine_select(out=later[:, :], in_=later[:, :], compare_op=ALU.is_gt, fill=0.0, base=0,
                            pattern=[[-1, P]], channel_multiplier=1).then_inc(S["const_ok"], 1)
            g.iota(vocab[:, :], pattern=[[0, 1]], base=0, channel_multiplier=1,
                   allow_small_or_imprecise_dtypes=True).then_inc(S["const_ok"], 1)
            g.iota(experts8[:, :], pattern=[[1, E]], base=0, channel_multiplier=0,
                   allow_small_or_imprecise_dtypes=True).then_inc(S["const_ok"], 1)
            g.memset(mean_w[:, :], 1.0 / D).then_inc(S["const_ok"], 1)
            g.memset(half_pow[:, :], 0.5).then_inc(S["const_ok"], 1)
            g.memset(eps_ln[:, :], EPS_LN).then_inc(S["const_ok"], 1)
            g.memset(eps_ffn[:, :], EPS_FFN).then_inc(S["const_ok"], 1)
            g.memset(onehot[:, :, 0:PAD], 0.0).then_inc(S["const_ok"], 1)
            g.memset(ones[:, :], 1.0).then_inc(S["taps0"], 1)
            g.memset(tapw[:, :, :], 0.0).then_inc(S["taps0"], 1)

            def routing_pool(m, r, valid):
                k = 2 * m + r
                if valid(0):
                    pool.wait_ge(S["r_c"], k + 1)
                    wait_past(pool, "r_var", k - 1)
                    g.tensor_tensor(sqr2[:, r], cen2[:, r], cen2[:, r], ALU.mult).then_inc(S["r_sq"], 1)
                if valid(2):
                    pool.wait_ge(S["r_x"], k - 1)
                    g.tensor_copy(xT[:, bass.ds((k - 2) * N2, N2)], xT_now[:, r]).then_inc(S["r_cp"], 1)

            rolling(pool, routing_pool, NI, 2, 2)

            def add_b2(i, gg, first):
                for j in range(2):
                    pool.wait_ge(S["r_xf"], NI)
                    if not first:
                        pool.wait_ge(S[f"b_pre{gg}{j}"], i - 1)
                    g.tensor_tensor(xb2[:, j, gg * BANK:(gg + 1) * BANK].rearrange("p (e d) -> p e d", d=D),
                                    b2_bc[:, gg * BANK:(gg + 1) * BANK].rearrange("p (e d) -> p e d", d=D),
                                    xrows[:, bass.ds((i - 1) * N2 + j * P, P)].unsqueeze(1).to_broadcast([P, 4, D]),
                                    ALU.add).then_inc(S["b_xb2"], 1)

            def expert_pool(i, first, cur, back):
                if cur:
                    if not first:
                        pool.wait_ge(S["b_wt"], i - 1)
                    g.tensor_copy(w_now[:, :, :], wgate[:, bass.ds(2 * (i - 1), 2), :]).then_inc(S["b_wn"], 1)
                    add_b2(i, 0, first)
                if back:
                    for j in range(2):
                        pool.wait_ge(S["b_u"], 2 * i - 3 + j)
                        g.tensor_tensor(pre[:, j, :], pre[:, j, :], gamma_bc[:, :], ALU.mult).then_inc(S["b_ug"], 1)
                if cur:
                    add_b2(i, 1, first)
                if back:
                    pool.wait_ge(S["b_c"], i - 1)
                    g.tensor_tensor(sqr, cen, cen, ALU.mult).then_inc(S["b_sq"], 1)

            pool.wait_ge(S["r_gates"], 1)
            pool.wait_ge(S["r_xf"], NI)
            pool.wait_ge(S["r_cp"], NI)
            pool.wait_ge(S["ld_ffn"], 16 * N_FFN)
            expert_pool(1, True, True, False)
            with pool.Fori(2, NI + 1) as i:
                expert_pool(i, False, True, True)
            expert_pool(NI + 1, False, False, True)

            pool.wait_ge(S["b_x"], NI)
            chain = Chain(pool, "gchain")

            def tap_products(b, pair):
                if pair == 0:
                    pool.wait_ge(S["c_tx"], b + 1)
                wait_past(pool, "c_taps", 2 * b + pair)
                g.tensor_tensor(products[:, :, :], xtab[:, :].unsqueeze(1).to_broadcast([V + 1, 2, CONV]),
                                tapw[:, 2 * pair:2 * pair + 2, :], ALU.mult).then_inc(S["c_prod"], 1)

            def by_head(ap):
                return ap.rearrange("p (h d) -> p h d", h=H)

            def steps_of(q, c, part):
                return dts[:, q, c, part * H:(part + 1) * H]

            def mask_pool(n, q, c):
                pool.wait_ge(S["c_dts"], half(n, c) + 1)
                wait_past(pool, "c_seg", n)
                g.tensor_tensor(amask[:, :, :], upper[:, :].unsqueeze(1).to_broadcast([P, H, P]),
                                steps_of(q, c, 1).unsqueeze(2).to_broadcast([P, H, P]), ALU.mult).then_inc(S["c_mask"], 1)

            def inputs_pool(n, q, c):
                pool.wait_ge(S["c_x"], n + 1)
                if not (isinstance(n, int) and n < 1):
                    pool.wait_ge(S["c_y"], n - 1)
                chain.start(n)
                chain.link(g.tensor_tensor(by_head(xdt[:, c]), by_head(xbc[:, c, 0:DI]),
                                           steps_of(q, c, 0).unsqueeze(2).to_broadcast([P, H, HD]), ALU.mult))
                g.tensor_tensor(by_head(xskip[:, c]), by_head(xbc[:, c, 0:DI]),
                                d_bc[:, :].unsqueeze(2).to_broadcast([P, H, HD]), ALU.mult).then_inc(S["c_xsk"], 1)

            def tail_pool(n, c):
                pool.wait_ge(S["c_edc"], n + 1)
                wait_past(pool, "c_y", n)
                g.tensor_tensor(by_head(xtail[:, :]), by_head(xdt[:, c]),
                                edge[:, c].unsqueeze(2).to_broadcast([P, H, HD]), ALU.mult).then_inc(S["c_xtl"], 1)

            def rms_pool(n):
                pool.wait_ge(S["c_sq"], n + 1)
                g.tensor_tensor(rms[:, 0:1], ms[:, :], half_pow[:, :], ALU.pow).then_inc(S["c_rms"], 1)

            def step(m, r, valid):
                k = STEPS * m + r
                c3, q3 = spot(r, 3)
                c4, q4 = spot(r, 4)
                if valid(5) and c4 == 1:
                    rms_pool(k - 5)
                if valid(3):
                    mask_pool(k - 3, q3, c3)
                if c4 == 0 and valid(4):
                    tail_pool(k - 4, c4)
                if valid(5) and c4 == 0:
                    rms_pool(k - 5)
                if r % 2 == 1 and valid(1):
                    tap_products(4 * m + r // 2, 0)
                if r % 2 == 0 and valid(2):
                    tap_products(4 * m + r // 2 - 1, 1)
                if valid(3):
                    inputs_pool(k - 3, q3, c3)

            pool.wait_ge(S["taps0"], 2)
            g.tensor_copy(hot_r[:, :, :].rearrange("v q t -> v (q t)"), ones[0:V + 1, :].to_broadcast([V + 1, 4 * (PAD + T)]))
            pool.wait_ge(S["s_dt"], 1)
            g.memset(xtab[:, :], 1.0).then_inc(S["c_ones"], 1)
            pool.wait_ge(S["c_ones"], 1)
            pipeline(pool, step)

            pool.wait_ge(S["c_h3"], NCH)
            pool.wait_ge(S["ld_mlp"], 16 * N_MLP)
            def mlp_pool(m, r, valid):
                k = 4 * m + r
                if valid(0):
                    now = pool.snap(k - 3) if not isinstance(k, int) else k - 3
                    pool.wait_ge(S["c_h3"], NCH)
                    wait_past(pool, "m_fin", now)
                    g.tensor_tensor(res[:, r], h3[:, bass.ds(k * TD * P, TD * P)].rearrange("p (c d) -> p c d", d=D),
                                    trib2_bc[:, :].unsqueeze(1).to_broadcast([P, TD, D]), ALU.add).then_inc(S["m_res"], 1)

            rolling(pool, mlp_pool, NT, 4, 3)

        @block.tensor
        def _(pe):
            t = nc.tensor
            mm = t.matmul

            pe.wait_ge(S["const_ok"], 10)
            pe.wait_ge(S["e_ln"], 1)
            t.transpose(bank[3][:, 0:V], lne[:, :], ident[0:V, 0:V]).then_inc(S["e_lnT"], 1)
            pe.wait_ge(S["e_lnT_c"], 1)
            pe.wait_ge(S["ld_att"], 16 * N_ATT)
            mm(bank[3][:, 128:128 + V], attn_sb[:, :], lneT[:, :], start=True, stop=True).then_inc(S["e_pT"], 1)
            pe.wait_ge(S["e_pT_c"], 1)
            mm(bank[3][0:V, 256:256 + V], lneT[:, :], projT[:, :], start=True, stop=True).then_inc(S["e_sc"], 1)

            pe.wait_ge(S["ld_rout"], 16 * N_ROUT)
            for c in range(4):
                last = t.transpose(bank[0][:, c * P:(c + 1) * P], win_rows[:, c, :], ident[:, :])
            last.then_inc(S["w_tr"], 1)
            t.transpose(bank[1][:, 0:P], win_rows[:, 4, :], ident[:, :])
            t.transpose(bank[1][:, P:P + H], windt_rows[:, :], ident[0:H, 0:H])
            t.transpose(bank[1][:, P + H:P + H + DI // P], normw_rows, ident[0:DI // P, 0:DI // P])
            for c in range(DI // P):
                last = t.transpose(bank[1][:, (2 + c) * P - 64:(3 + c) * P - 64], wout_rows[:, c * P:(c + 1) * P], ident[:, :])
            last.then_inc(S["w_tr"], 1)
            t.transpose(bank[2][:, 0:P], tri1_rows[:, :], ident[:, :])
            t.transpose(bank[2][:, P:2 * P], tri2_rows[:, :], ident[:, :])
            t.transpose(bank[2][:, 2 * P:2 * P + E * FT], b1_rows[:, :], ident[0:E * FT, 0:E * FT]).then_inc(S["w_tr"], 1)

            pe.wait_ge(S["e_exp"], 1)
            pe.wait_ge(S["e_cnt"], 1)
            mm(bank[4][0:V, 0:B], expT[:, :], counts[:, :], start=True, stop=True).then_inc(S["e_den"], 1)
            pe.wait_ge(S["w_trc"], 3)
            with pe.Fori(1, B // GA // 2 + 1) as m:
                for q in range(2):
                    pe.wait_ge(S[f"at_w{q}"], m)
                    pe.wait_ge(S[f"at_h{q}"], m - 1)
                    mm(bank[q][0:V, :], expT[:, :], weighted[:, q].rearrange("p j d -> p (j d)"),
                       start=True, stop=True).then_inc(S[f"at_num{q}"], 1)
                for q in range(2):
                    pe.wait_ge(S[f"at_h{q}"], m)
                    pe.wait_ge(S[f"at_s{q}"], m - 1)
                    for j in range(GA):
                        last = t.transpose(bank[2 + q][:, j * V:(j + 1) * V], h1rows[:, q, j, :], ident[0:V, 0:V])
                    last.then_inc(S[f"at_t{q}"], 1)

            for q in range(2):
                pe.wait_ge(S[f"at_s{q}"], B // GA // 2)
            def routing_pe(m, r, valid):
                k = 2 * m + r
                if valid(0):
                    wait_past(pe, "r_c", k)
                    mm(bank[0][:, 0:N2], mean_w[:, :], hT[:, bass.ds(k * N2, N2)], start=True, stop=True).then_inc(S["r_mean"], 1)
                if valid(1):
                    pe.wait_ge(S["r_sq"], k)
                    wait_past(pe, "r_sd", k - 1)
                    mm(bank[1][:, 0:N2], mean_w[:, :], sqr2[:, 1 - r], start=True, stop=True).then_inc(S["r_var"], 1)
                if valid(2):
                    pe.wait_ge(S["r_x"], k - 1)
                    wait_past(pe, "r_lg", k - 2)
                    for j in range(2):
                        last = mm(bank[3][:, j * E:(j + 1) * E], xT_now[:, r, j * P:(j + 1) * P], router_sb[:, :], start=True, stop=True)
                    last.then_inc(S["r_rt"], 1)
                    wait_past(pe, "r_xf", k - 2)
                    for j in range(2):
                        last = t.transpose(bank[2][:, j * P:(j + 1) * P], xT_now[:, r, j * P:(j + 1) * P], ident[:, :])
                    last.then_inc(S["r_tr"], 1)

            rolling(pe, routing_pe, NI, 2, 2)

            def up(i, e, first):
                for hb in range(FT // 2):
                    k = 16 * (i - 1) + 2 * e + hb
                    if not (first and e < 1):
                        pe.wait_ge(S["b_relu"], k - 1)
                    u = bank[hb]
                    for f in range(2):
                        ft = 2 * hb + f
                        last = mm(u[:, f * N2:(f + 1) * N2], w1_sb[:, e, ft * P:(ft + 1) * P],
                                  xT[:, bass.ds((i - 1) * N2, N2)], start=True, stop=True)
                    last.then_inc(S["b_up"], 1)

            def down(i, e, first):
                pe.wait_ge(S["b_relu"], 16 * (i - 1) + 2 * e + 2)
                gg, k4 = divmod(e, 4)
                for j in range(2):
                    if k4 == 0 and not first:
                        pe.wait_ge(S[f"b_pre{gg}{j}"], i - 1)
                    for ft in range(FT):
                        last = mm(bank[2 + 2 * gg + j][:, k4 * P:(k4 + 1) * P], hid[:, e % 2, ft, j * P:(j + 1) * P],
                                  w2_sb[:, e, ft, :], start=(ft == 0), stop=(ft == FT - 1))
                    if k4 == 3 and j == 0:
                        last.then_inc(S["b_y"], 1)
                last.then_inc(S["b_dn"], 1)

            def sum_rows(i):
                pe.wait_ge(S["b_wtc"], i)
                pe.wait_ge(S["b_o"], i)
                mm(bank[6][:, 0:N2], beta_sb[:, :], wT_now[:, :], start=True, stop=False, skip_group_check=True)
                for j in range(2):
                    last = mm(bank[6][:, j * P:(j + 1) * P], summed[:, j, :], ident[:, :], start=False, stop=True, skip_group_check=True)
                last.then_inc(S["b_z"], 1)

            def expert_pe(i, first, cur, back):
                for e in range(E + 1):
                    if cur and e < E:
                        up(i, e, first)
                    if cur and e > 0:
                        down(i, e - 1, first)
                    if back and e == 4:
                        sum_rows(i - 1)
                    if back and e == 5:
                        pe.wait_ge(S["b_h2"], i - 1)
                        mm(bank[6][:, N2:2 * N2], mean_w[:, :], hT[:, bass.ds((i - 2) * N2, N2)], start=True, stop=True).then_inc(S["b_mean"], 1)
                    if back and e == 6:
                        pe.wait_ge(S["b_sq"], i - 1)
                        mm(bank[7][:, 0:N2], mean_w[:, :], sqr, start=True, stop=True).then_inc(S["b_v2"], 1)
                    if cur and e == 7:
                        pe.wait_ge(S["b_wn"], i)
                        if back:
                            pe.wait_ge(S["b_sd2"], i - 1)
                        for j in range(2):
                            last = t.transpose(bank[7][0:E, N2 + j * P:N2 + (j + 1) * P], w_now[:, j, :], ident[:, :])
                        last.then_inc(S["b_wt"], 1)

            pe.wait_ge(S["r_xf"], NI)
            pe.wait_ge(S["r_lg"], NI)
            pe.wait_ge(S["r_cp"], NI)
            pe.wait_ge(S["ld_ffn"], 16 * N_FFN)
            expert_pe(1, True, True, False)
            with pe.Fori(2, NI + 1) as i:
                expert_pe(i, False, True, True)
            expert_pe(NI + 1, False, False, True)

            with pe.Fori(1, B // GD // 2 + 1) as m:
                for q in range(2):
                    pe.wait_ge(S["s_in1" if q else "s_in"], m)
                    for j in range(GD):
                        last = mm(bank[0][0:V, bass.ds((2 * m - 2 + q) * GD * H + j * H, H)], dt_in[:, q, j * V:(j + 1) * V], windt_T[:, :],
                                  start=True, stop=True)
                    last.then_inc(S["s_raw"], 1)

            def tables(b, q):
                pe.wait_ge(S["c_seq"], b + 1)
                wait_past(pe, "c_zt", b)
                wait_past(pe, "c_ht", b)
                wait_past(pe, "c_dts", b)
                mm(bank[0][0:V, 0:BANK], xT_seq[:, q % 2], win_T[:, 0:BANK], start=True, stop=True)
                mm(bank[1][0:V, 0:P], xT_seq[:, q % 2], win_T[:, BANK:NZX], start=True, stop=True)
                t.transpose(bank[1][0:V, P:2 * P], hT_seq[:, q % 2], ident[:, :])
                for c in range(2):
                    last = mm(bank[1][:, 2 * P + 2 * H * c:2 * P + 2 * H * (c + 1)], hot[0:V, q, PAD + c * P:PAD + (c + 1) * P],
                              dt_tab[:, bass.ds(b, 1), :, :].rearrange("v a k h -> v (a k h)"), start=True, stop=True)
                last.then_inc(S["c_tab"], 1)

            def convolve(n, q, c, pair):
                pe.wait_ge(S["c_taps"], 2 * half(n, c) + pair + 1)
                if pair == 0:
                    wait_past(pe, "c_x", n)
                for k in (2 * pair, 2 * pair + 1):
                    for part in (taps_hi, taps_lo):
                        last = mm(bank[2][:, 0:CONV], hot_r[:, q, c * P + k:c * P + k + P], part[:, q % 2, k, :],
                                  start=(k == 0 and part is taps_hi), stop=(k == TAPS - 1 and part is taps_lo), skip_group_check=True)
                if pair == 1:
                    last.then_inc(S["c_cv"], 1)

            def decay_sums(n, c):
                pe.wait_ge(S["c_mask"], n + 1)
                pe.wait_ge(S["c_dec"], n)
                mm(bank[3][:, :], later[:, :], amask[:, :, :].rearrange("p h l -> p (h l)"), start=True, stop=True).then_inc(S["c_seg"], 1)

            def turn_bc(n, q, c):
                pe.wait_ge(S["c_x"], n + 1)
                pe.wait_ge(S["c_cbm"], n)
                mm(bank[4][:, 2 * P:2 * P + H], (upper if c else later)[:, :], dts[:, q, c, H:2 * H], start=True, stop=True)
                t.transpose(bank[4][0:NS, 0:P], xbc[:, c, DI:DI + NS], ident[:, :])
                t.transpose(bank[4][0:NS, P:2 * P], xbc[:, c, DI + NS:CONV], ident[:, :]).then_inc(S["c_bc"], 1)

            def scores(n, c):
                pe.wait_ge(S["c_edc"], n + 1)
                mm(bank[4][:, 3 * P:4 * P], bcT[:, c, 0:P], bcT[:, c, P:2 * P], start=True, stop=True).then_inc(S["c_cb"], 1)

            def mixed(n, c):
                pe.wait_ge(S["c_mix"], n + 1)
                pe.wait_ge(S["c_xsk"], n + 1)
                wait_past(pe, "c_y", n)
                if c == 1:
                    pe.wait_ge(S["c_stc"], half(n, 1) + 1)
                    mm(bank[5][:, DI:2 * DI], bcT[:, c, P:2 * P], state[:, :], start=True, stop=True)
                for h in range(H):
                    last = mm(bank[5][:, h * HD:(h + 1) * HD], decay[:, c, h, :], xdt[:, c, h * HD:(h + 1) * HD], start=True, stop=True)
                last.then_inc(S["c_yd"], 1)

            def chunk_state(n, c):
                pe.wait_ge(S["c_xtl"], half(n, 0) + 1)
                wait_past(pe, "c_g", n)
                mm(bank[6][0:NS, DI:2 * DI], xbc[:, c, DI:DI + NS], xtail[:, :], start=True, stop=True).then_inc(S["c_st"], 1)

            def gate_rows(n, q, c):
                wait_past(pe, "c_g", n)
                wait_past(pe, "c_stc", half(n, c) + 1)
                mm(bank[6][:, 0:DI], hot[0:V, q, PAD + c * P:PAD + (c + 1) * P], ztab[:, q, :], start=True, stop=True).then_inc(S["c_zg"], 1)

            def turn_gated(n):
                pe.wait_ge(S["c_h3"], n)
                pe.wait_ge(S["c_g"], n + 1)
                for c in range(DI // P):
                    last = t.transpose(bank[7][:, c * P:(c + 1) * P], gated[:, c * P:(c + 1) * P], ident[:, :])
                last.then_inc(S["c_gt"], 1)

            def project(n, q, c):
                pe.wait_ge(S["c_gtc"], n + 1)
                o = bank[7][:, DI:DI + P]
                mm(o, hot[0:V, q, PAD + c * P:PAD + (c + 1) * P], htab[:, q, :], start=True, stop=False)
                mm(o, gT[:, 0:P], wout_T[:, 0, :], start=False, stop=False)
                mm(o, gT[:, P:2 * P], wout_T[:, 1, :], start=False, stop=True).then_inc(S["c_out"], 1)

            def step(m, r, valid):
                k = STEPS * m + r
                c3, q3 = spot(r, 3)
                c4, q4 = spot(r, 4)
                c5, q5 = spot(r, 5)
                c6, q6 = spot(r, 6)
                if valid(6):
                    turn_gated(k - 6)
                if valid(4):
                    decay_sums(k - 4, c4)
                    turn_bc(k - 4, q4, c4)
                if valid(3):
                    convolve(k - 3, q3, c3, 0)
                if valid(5):
                    gate_rows(k - 5, q5, c5)
                if valid(4):
                    scores(k - 4, c4)
                if valid(3):
                    convolve(k - 3, q3, c3, 1)
                if valid(6):
                    project(k - 6, q6, c6)
                if valid(4):
                    mixed(k - 4, c4)
                if r % 2 == 0 and valid(0):
                    tables(4 * m + r // 2, r // 2)
                if valid(4) and c4 == 0:
                    chunk_state(k - 4, c4)

            pe.wait_ge(S["s_dt"], 1)
            pipeline(pe, step)

            pe.wait_ge(S["c_h3"], NCH)
            def mlp_pe(m, r, valid):
                k = 4 * m + r
                if valid(1):
                    q = (r - 1) % 2
                    pe.wait_ge(S["m_xn"], k)
                    wait_past(pe, "m_xtc", k - 2)
                    for c in range(TD):
                        last = t.transpose(bank[q][:, c * P:(c + 1) * P], xn[:, q, c, :], ident[:, :])
                    last.then_inc(S["m_xt"], 1)
                if valid(2):
                    q = r % 2
                    pe.wait_ge(S["m_xtc"], k - 1)
                    wait_past(pe, "m_gel", k - 3)
                    mm(bank[2 + q][:, :], tri1_T[:, :], xnT[:, q, :], start=True, stop=True).then_inc(S["m_1"], 1)
                if valid(3):
                    q = (r - 1) % 2
                    pe.wait_ge(S["m_gel"], k - 2)
                    wait_past(pe, "m_fin", k - 4)
                    for c in range(TD):
                        last = mm(bank[4 + q][:, c * P:(c + 1) * P], gel[:, q, c * P:(c + 1) * P], tri2_T[:, :], start=True, stop=True)
                    last.then_inc(S["m_2"], 1)

            rolling(pe, mlp_pe, NT, 4, 3)

        @block.scalar
        def _(act):
            a = nc.scalar
            act.wait_ge(S["e_var"], 1)
            a.activation(stat[0:V, 9:10], stat[0:V, 8:9], ACT.Sqrt).then_inc(S["e_sd"], 1)
            act.wait_ge(S["e_sc"], 1)
            a.activation(tanh_s[:, :], bank[3][0:V, 256:256 + V], ACT.Tanh).then_inc(S["e_tanh"], 1)
            act.wait_ge(S["e_tanh"], 1)
            a.activation(expT[:, :], tanh_s[:, :], ACT.Exp).then_inc(S["e_exp"], 1)

            act.wait_ge(S["e_cnt"], 1)
            act.wait_ge(S["e_rden"], 1)
            with act.Fori(1, B // GA // 2 + 1) as m:
                for q in range(2):
                    act.wait_ge(S[f"at_num{q}"], m - 1)
                    for j in range(GA):
                        last = a.activation(weighted[:, q, j, :], lne[:, :], ACT.Copy,
                                            scale=counts[:, bass.ds((2 * (m - 1) + q) * GA + j, 1)])
                    last.then_inc(S[f"at_w{q}"], 1)
                for q in range(2):
                    act.wait_ge(S[f"at_t{q}"], m)
                    a.copy(hT[:, bass.ds((2 * (m - 1) + q) * GA * V, GA * V)], bank[2 + q][:, 0:GA * V]).then_inc(S[f"at_s{q}"], 1)

            def routing_act(m, r, valid):
                k = 2 * m + r
                if valid(2):
                    act.wait_ge(S["r_tr"], k - 1)
                    a.copy(xrows[:, bass.ds((k - 2) * N2, N2)], bank[2][:, 0:N2]).then_inc(S["r_xf"], 1)
                if valid(1):
                    act.wait_ge(S["r_var"], k)
                    wait_past(act, "r_x", k - 1)
                    a.activation(dev[:, :], bank[1][:, 0:N2], ACT.Sqrt, bias=eps_ln[:, :]).then_inc(S["r_sd"], 1)

            rolling(act, routing_act, NI, 2, 2)
            act.wait_ge(S["r_gd"], 1)
            a.activation(gexp[:, :], gdiff[:, :], ACT.Exp).then_inc(S["r_ge"], 1)

            def relu(i, e, first):
                for hb in range(FT // 2):
                    k = 16 * (i - 1) + 2 * e + hb
                    act.wait_ge(S["b_up"], k + 1)
                    if hb == 0 and not (first and e < 2):
                        act.wait_ge(S["b_dn"], 8 * (i - 1) + e - 1)
                    for f in range(2):
                        ft = 2 * hb + f
                        last = a.activation(hid[:, e % 2, ft, :], bank[hb][:, f * N2:(f + 1) * N2], ACT.Relu,
                                            bias=b1_col[:, e * FT + ft:e * FT + ft + 1])
                    last.then_inc(S["b_relu"], 1)

            def expert_act(i, first, cur, back):
                for e in range(E):
                    if cur:
                        relu(i, e, first)
                    if back and e == 0:
                        act.wait_ge(S["b_var"], i - 1)
                        a.activation(sm[:, 5, :], sm[:, 4, :], ACT.Sqrt, bias=eps_ffn[:, :], scale=1.0 / D).then_inc(S["b_sd"], 1)
                    if back and e == 6:
                        act.wait_ge(S["b_v2"], i - 1)
                        a.activation(dev[:, :], bank[7][:, 0:N2], ACT.Sqrt, bias=eps_ln[:, :]).then_inc(S["b_sd2"], 1)
                    if cur and e == 7:
                        act.wait_ge(S["b_wt"], i)
                        if back:
                            act.wait_ge(S["b_z"], i - 1)
                        a.copy(wT_now[:, :], bank[7][0:E, N2:2 * N2]).then_inc(S["b_wtc"], 1)

            act.wait_ge(S["w_trc"], 3)
            expert_act(1, True, True, False)
            with act.Fori(2, NI + 1) as i:
                expert_act(i, False, True, True)
            expert_act(NI + 1, False, False, True)

            act.wait_ge(S["b_x"], NI)
            with act.Fori(1, B // GD // 2 + 1) as m:
                act.wait_ge(S["s_raw"], 2 * m - 2)
                a.copy(dt_in[:, 1], xT[:, bass.ds((2 * m - 1) * GD * V, GD * V)]).then_inc(S["s_in1"], 1)

            act.wait_ge(S["s_v"], 1)
            a.activation(dt_t[:, 1, :], dt_t[:, 1, :], ACT.Exp, scale=-1.0).then_inc(S["s_e"], 1)
            act.wait_ge(S["s_v"], 2)
            a.activation(dt_t[:, 4, :], dt_t[:, 2, :], ACT.Ln).then_inc(S["s_l"], 1)
            act.wait_ge(S["ld_ssm"], 16 * N_SSM)
            a.activation(a_neg[:, :], alog_bc[:, :], ACT.Exp).then_inc(S["s_l"], 1)

            def tables(b, q):
                act.wait_ge(S["c_tab"], b + 1)
                wait_past(act, "c_prod", 2 * b)
                a.copy(xtab[0:V, 0:DI], bank[0][0:V, DI:2 * DI])
                a.copy(xtab[0:V, DI:CONV], bank[1][0:V, 0:P]).then_inc(S["c_tx"], 1)
                a.copy(dts[:, q].rearrange("p c h -> p (c h)"), bank[1][:, 2 * P:2 * P + 4 * H]).then_inc(S["c_dts"], 1)

            def more_tables(b, q):
                act.wait_ge(S["c_tab"], b + 1)
                wait_past(act, "c_out", 2 * b - 6)
                a.copy(htab[:, q, :], bank[1][0:V, P:2 * P]).then_inc(S["c_ht"], 1)
                a.activation(ztab[:, q, :], bank[0][0:V, 0:DI], ACT.Tanh).then_inc(S["c_tz"], 1)

            def round_taps(b, q, pair):
                act.wait_ge(S["c_prod"], 2 * b + pair + 1)
                wait_past(act, "c_cv", 2 * b - 2)
                a.copy(taps_hi[:, q, 2 * pair:2 * pair + 2, :], products[:, :, :]).then_inc(S["c_hi"], 1)

            def conv_tanh(n):
                act.wait_ge(S["c_cv"], n + 1)
                a.activation(tanh_x[:, :], bank[2][:, 0:CONV], ACT.Tanh).then_inc(S["c_tanh"], 1)

            def decays(n, r):
                wait_past(act, "c_y", n - 1)
                act.wait_ge(S["c_seg"], n + 1)
                a.activation(decay[:, r].rearrange("p h l -> p (h l)"), bank[3][:, :], ACT.Exp).then_inc(S["c_dec"], 1)

            def edges(n, r):
                if not (isinstance(n, int) and n < 1):
                    act.wait_ge(S["c_y"], n - 1)
                act.wait_ge(S["c_bc"], n + 1)
                a.copy(bcT[:, r, :], bank[4][0:NS, 0:2 * P])
                a.activation(edge[:, r, :], bank[4][:, 2 * P:2 * P + H], ACT.Exp).then_inc(S["c_edc"], 1)

            def square_sum(n, r):
                act.wait_ge(S["c_y"], n + 1)
                wait_past(act, "c_gt", n)
                a.activation(gated[:, :], y[:, r, :], ACT.Square, accum_out=ssum[:, :]).then_inc(S["c_bn"], 1)
                act.wait_ge(S["c_bn"], n + 1)
                act.wait_ge(S["c_rms"], n)
                a.mul(ms[:, :], ssum[:, :], 1.0 / DI).then_inc(S["c_sq"], 1)

            def step(m, r, valid):
                k = STEPS * m + r
                c4, c5 = (spot(r, lag)[0] for lag in (4, 5))
                if valid(6):
                    act.wait_ge(S["c_gt"], k - 5)
                    a.copy(gT[:, :], bank[7][:, 0:DI]).then_inc(S["c_gtc"], 1)
                if valid(5) and c5 == 0:
                    square_sum(k - 5, c5)
                if valid(4):
                    edges(k - 4, c4)
                    decays(k - 4, c4)
                if valid(5) and c5 == 1:
                    square_sum(k - 5, c5)
                if r % 2 == 1 and valid(1):
                    more_tables(4 * m + r // 2, r // 2)
                if valid(3):
                    conv_tanh(k - 3)
                if valid(6):
                    act.wait_ge(S["c_out"], k - 5)
                    a.copy(h3[:, bass.ds((k - 6) * P, P)], bank[7][:, DI:DI + P]).then_inc(S["c_h3"], 1)
                if r % 2 == 1 and valid(1):
                    round_taps(4 * m + r // 2, r // 2 % 2, 0)
                if r % 2 == 0 and valid(2):
                    round_taps(4 * m + r // 2 - 1, (r // 2 - 1) % 2, 1)
                if r % 2 == 0 and valid(0):
                    tables(4 * m + r // 2, r // 2)

            act.wait_ge(S["c_ones"], 1)
            pipeline(act, step)

            act.wait_ge(S["f_st"], 1)
            a.activation(h3_s[:, 3, :], h3_s[:, 2, :], ACT.Sqrt, bias=eps_ln[:, :], scale=1.0 / D).then_inc(S["f_sd"], 1)
            act.wait_ge(S["ld_mlp"], 16 * N_MLP)
            def mlp_act(m, r, valid):
                k = 4 * m + r
                if valid(2):
                    act.wait_ge(S["m_1"], k - 1)
                    wait_past(act, "m_2", k - 3)
                    a.activation(gel[:, r % 2, :], bank[2 + r % 2][:, :], ACT.Gelu, bias=trib1_col[:, :]).then_inc(S["m_gel"], 1)

            rolling(act, mlp_act, NT, 4, 3)

        @block.vector
        def _(dve):
            v = nc.vector
            chain = Chain(dve, "dchain")
            link = chain.link

            dve.wait_ge(S["ld_att"], 16 * N_ATT)
            link(v.bn_stats(stat[0:V, 0:6], emb_sb[:, :]))
            link(v.bn_aggr(stat[0:V, 6:8], stat[0:V, 0:6]))
            v.tensor_scalar(stat[0:V, 8:9], stat[0:V, 7:8], EPS_LN, None, ALU.add).then_inc(S["e_var"], 1)
            dve.wait_ge(S["e_sd"], 1)
            link(v.reciprocal(stat[0:V, 10:11], stat[0:V, 9:10]))
            v.tensor_scalar(lne[:, :], emb_sb[:, :], stat[0:V, 6:7], stat[0:V, 10:11], ALU.subtract, ALU.mult).then_inc(S["e_ln"], 1)
            dve.wait_ge(S["e_lnT"], 1)
            v.tensor_copy(lneT[:, :], bank[3][:, 0:V]).then_inc(S["e_lnT_c"], 1)
            dve.wait_ge(S["e_pT"], 1)
            v.tensor_copy(projT[:, :], bank[3][:, 128:128 + V]).then_inc(S["e_pT_c"], 1)

            dve.wait_ge(S["const_ok"], 10)
            for n in range(B // TOKB):
                dve.wait_ge(S[f"tok_ld{n % TOKN}"], 16 * (n // TOKN + 1))
                hots = onehot[:, n * TOKB:(n + 1) * TOKB, PAD:PAD + T]
                ins = v.tensor_scalar(hots, tok[:, n % TOKN], vocab[:, :], None, ALU.is_equal)
                ins.then_inc(S["tok_used"], 1)
                dve.wait_ge(S["tok_used"], n + 1)
                last = v.tensor_reduce(counts[:, n * TOKB:(n + 1) * TOKB], hots, AX.X, ALU.add)
            last.then_inc(S["e_cnt"], 1)

            dve.wait_ge(S["w_tr"], 1)
            v.tensor_scalar(win_T[:, 0:DI], bank[0][:, 0:DI], 0.5, None, ALU.mult)
            v.tensor_copy(win_T[:, DI:BANK], bank[0][:, DI:BANK]).then_inc(S["w_trc"], 1)
            dve.wait_ge(S["w_tr"], 2)
            v.tensor_copy(win_T[:, BANK:NZX], bank[1][:, 0:P])
            v.tensor_copy(windt_T[:, :], bank[1][:, P:P + H])
            v.tensor_copy(normw_col[:, :], bank[1][:, P + H:P + H + DI // P]).then_inc(S["w_nw"], 1)
            dve.wait_ge(S["w_nw"], 1)
            for c in range(DI // P):
                last = v.tensor_scalar(wout_T[:, c, :], bank[1][:, (2 + c) * P - 64:(3 + c) * P - 64], normw_col[:, c:c + 1], None, ALU.mult)
            last.then_inc(S["w_trc"], 1)
            dve.wait_ge(S["w_tr"], 3)
            v.tensor_tensor(tri1_T[:, :], bank[2][:, 0:P], upper[:, :], ALU.mult)
            v.tensor_tensor(tri2_T[:, :], bank[2][:, P:2 * P], upper[:, :], ALU.mult)
            v.tensor_copy(b1_col[:, :], bank[2][:, 2 * P:2 * P + E * FT]).then_inc(S["w_trc"], 1)

            dve.wait_ge(S["e_den"], 1)
            v.reciprocal(rden[:, :], bank[4][0:V, 0:B]).then_inc(S["e_rden"], 1)
            dve.wait_ge(S["e_rden"], 1)
            with dve.Fori(1, B // GA // 2 + 1) as m:
                for q in range(2):
                    dve.wait_ge(S[f"at_num{q}"], m)
                    dve.wait_ge(S[f"at_t{q}"], m - 1)
                    for j in range(GA):
                        last = v.scalar_tensor_tensor(out=h1rows[:, q, j, :], in0=bank[q][0:V, j * D:(j + 1) * D],
                                                      scalar=rden[:, bass.ds((2 * (m - 1) + q) * GA + j, 1)],
                                                      in1=emb_sb[:, :], op0=ALU.mult, op1=ALU.add)
                    last.then_inc(S[f"at_h{q}"], 1)

            for q in range(2):
                dve.wait_ge(S[f"at_s{q}"], B // GA // 2)

            def apart():
                dve.wait_ge(S["ld_att"], 16 * N_ATT)

            def routing_dve(m, r, valid):
                k = 2 * m + r
                if valid(0):
                    wait_past(dve, "r_x", k - 1)
                    dve.wait_ge(S["r_mean"], k + 1)
                    v.tensor_tensor(cen2[:, r], hT[:, bass.ds(k * N2, N2)], bank[0][:, 0:N2], ALU.subtract).then_inc(S["r_c"], 1)
                if valid(2):
                    now = dve.snap(k - 1) if not isinstance(k, int) else k - 1
                    dve.wait_ge(S["r_rt"], now)
                    v.tensor_copy(logit[:, :, :].rearrange("p j e -> p (j e)"), bank[3][:, 0:2 * E]).then_inc(S["r_lg"], 1)
                    apart()
                    dve.wait_ge(S["r_lg"], now)
                    v.max(top_v[:, 0, :], logit[:, 0, :])
                    v.max(top_v[:, 1, :], logit[:, 1, :]).then_inc(S["r_top"], 1)
                    apart()
                    dve.wait_ge(S["r_top"], now)
                    v.max_index(top_i[:, 0, :], top_v[:, 0, :], logit[:, 0, :])
                    v.max_index(top_i[:, 1, :], top_v[:, 1, :], logit[:, 1, :]).then_inc(S["r_ti"], 1)
                    dve.wait_ge(S["r_ti"], now)
                    v.tensor_copy(idxs[:, bass.ds(2 * (k - 2), 2), :], top_i[:, :, 0:2])
                    v.tensor_copy(vals[:, bass.ds(2 * (k - 2), 2), :], top_v[:, :, 0:2])
                if valid(1):
                    dve.wait_ge(S["r_sd"], k)
                    v.reciprocal(rstd[:, :], dev[:, :]).then_inc(S["rchain"], 1)
                    wait_past(dve, "r_cp", k - 2)
                    wait_past(dve, "r_tr", k - 2)
                    dve.wait_ge(S["rchain"], k)
                    v.tensor_tensor(xT_now[:, 1 - r], cen2[:, 1 - r], rstd[:, :], ALU.mult).then_inc(S["r_x"], 1)

            rolling(dve, routing_dve, NI, 2, 2)

            link(v.memset(stat[:, 15:16], 0.0))
            v.tensor_tensor(gdiff[:, :], vals[:, :, 1], vals[:, :, 0], ALU.subtract).then_inc(S["r_gd"], 1)
            dve.wait_ge(S["r_ge"], 1)
            link(v.tensor_scalar(gates[:, :, 1], gexp[:, :], 1.0, None, ALU.add))
            link(v.reciprocal(gates[:, :, 0], gates[:, :, 1]))
            link(v.tensor_tensor(gates[:, :, 1], gexp[:, :], gates[:, :, 0], ALU.mult))
            every = experts8[:, :].unsqueeze(1).to_broadcast([P, NTILE, E])
            for s in range(2):
                link(v.tensor_tensor(pick[:, :, :], every, idxs[:, :, s].unsqueeze(2).to_broadcast([P, NTILE, E]), ALU.is_equal))
                dst = pick if s else wgate
                link(v.tensor_tensor(dst[:, :, :], pick[:, :, :], gates[:, :, s].unsqueeze(2).to_broadcast([P, NTILE, E]), ALU.mult))
            v.tensor_tensor(wgate[:, :, :], wgate[:, :, :], pick[:, :, :], ALU.add).then_inc(S["r_gates"], 1)
            dve.wait_ge(S["r_gates"], 1)

            bch = Chain(dve, "bchain")

            def expert_sums(i, gg):
                for j in range(2):
                    k = 4 * (i - 1) + 2 * gg + j
                    if gg == 0:
                        wait_past(dve, "b_o", i - 1)
                    if j == 0:
                        dve.wait_ge(S["b_y"], 2 * (i - 1) + gg + 1)
                    else:
                        dve.wait_ge(S["b_dn"], 8 * (i - 1) + 4 * gg + 4)
                    dve.wait_ge(S["b_xb2"], k + 1)
                    v.tensor_tensor(pre[:, j, gg * BANK:(gg + 1) * BANK], bank[2 + 2 * gg + j][:, :], xb2[:, j, gg * BANK:(gg + 1) * BANK],
                                    ALU.add).then_inc(S[f"b_pre{gg}{j}"], 1)
                    dve.wait_ge(S[f"b_pre{gg}{j}"], i)
                    for e in range(4 * gg, 4 * gg + 4):
                        last = v.bn_stats(bns[:, j * E + e, :], pre[:, j, e * D:(e + 1) * D])
                if gg == 1:
                    last.then_inc(S["b_bn"], 1)

            def expert_norms(i, sums):
                bch.start((i - 1) * B_LINKS)
                col = [bns[:, :, c] for c in range(6)]
                dve.wait_ge(S["b_bn"], i)
                v.tensor_tensor(sm[:, 0, :], col[1], col[4], ALU.add)
                v.tensor_tensor(sm[:, 1, :], col[1], col[4], ALU.subtract)
                bch.link(v.tensor_tensor(sm[:, 2, :], col[2], col[5], ALU.add))
                v.tensor_scalar(sm[:, 0, :], sm[:, 0, :], 0.5, None, ALU.mult)
                bch.link(v.tensor_tensor(sm[:, 3, :], sm[:, 1, :], sm[:, 1, :], ALU.mult))
                v.scalar_tensor_tensor(out=sm[:, 4, :], in0=sm[:, 3, :], scalar=D / 4.0, in1=sm[:, 2, :],
                                       op0=ALU.mult, op1=ALU.add).then_inc(S["b_var"], 1)
                dve.wait_ge(S["b_sd"], i)
                bch.link(v.reciprocal(sm[:, 6, :], sm[:, 5, :]))
                bch.link(v.tensor_tensor(sm[:, 7, :].rearrange("p (j e) -> p j e", e=E), sm[:, 6, :].rearrange("p (j e) -> p j e", e=E),
                                         wgate[:, bass.ds(2 * (i - 1), 2), :], ALU.mult))
                for j in range(2):
                    for k in range(j * E, (j + 1) * E):
                        part = pre[:, k // E, (k % E) * D:(k % E + 1) * D]
                        last = v.tensor_scalar(part, part, sm[:, 0, k:k + 1], sm[:, 7, k:k + 1], ALU.subtract, ALU.mult)
                    last.then_inc(S["b_u"], 1)
                for j in range(2):
                    dve.wait_ge(S["b_ug"], 2 * i - 1 + j)
                    last = v.tensor_reduce(summed[:, j, :], pre[:, j, :].rearrange("p (e d) -> p d e", d=D), AX.X, ALU.add)
                last.then_inc(S["b_o"], 1)
                if sums:
                    expert_sums(i + 1, 0)
                now = bass.ds((i - 1) * N2, N2)
                dve.wait_ge(S["b_z"], i)
                v.tensor_tensor(hT[:, now], bank[6][:, 0:N2], hT[:, now], ALU.add).then_inc(S["b_h2"], 1)
                dve.wait_ge(S["b_mean"], i)
                v.tensor_tensor(cen, hT[:, now], bank[6][:, N2:2 * N2], ALU.subtract).then_inc(S["b_c"], 1)
                dve.wait_ge(S["b_sd2"], i)
                bch.link(v.reciprocal(rstd[:, :], dev[:, :]))
                v.tensor_tensor(xT[:, now], cen, rstd[:, :], ALU.mult).then_inc(S["b_x"], 1)

            expert_sums(1, 0)
            expert_sums(1, 1)
            with dve.Fori(2, NI + 1) as i:
                expert_norms(i - 1, True)
                assert bch.n == B_LINKS
                expert_sums(i, 1)
            expert_norms(NI, False)

            dve.wait_ge(S["b_x"], NI)
            with dve.Fori(1, B // GD // 2 + 1) as m:
                dve.wait_ge(S["s_raw"], 2 * m - 2)
                v.tensor_copy(dt_in[:, 0], xT[:, bass.ds((2 * m - 2) * GD * V, GD * V)]).then_inc(S["s_in"], 1)

            dve.wait_ge(S["s_raw"], B // GD)
            dve.wait_ge(S["ld_ssm"], 16 * N_SSM)
            link(v.tensor_tensor(dt_t[:, 0, :].rearrange("p (b h) -> p b h", h=H), bank[0][0:V, 0:B * H].rearrange("p (b h) -> p b h", h=H),
                                 dtb_bc[:, :].unsqueeze(1).to_broadcast([V, B, H]), ALU.add))
            link(v.tensor_scalar(dt_t[:, 2, :], dt_t[:, 0, :], -1.0, None, ALU.mult))
            v.tensor_tensor(dt_t[:, 1, :], dt_t[:, 0, :], dt_t[:, 2, :], ALU.max).then_inc(S["s_v"], 1)
            dve.wait_ge(S["s_e"], 1)
            v.tensor_scalar(dt_t[:, 2, :], dt_t[:, 1, :], 1.0, None, ALU.add).then_inc(S["s_v"], 1)
            dve.wait_ge(S["s_v"], 2)
            link(v.tensor_scalar(dt_t[:, 3, :], dt_t[:, 2, :], 1.0, None, ALU.subtract))
            dve.wait_ge(S["s_l"], 1)
            link(v.tensor_scalar(dt_t[:, 2, :], dt_t[:, 3, :], 0.0, None, ALU.is_equal))
            v.tensor_tensor(dt_t[:, 3, :], dt_t[:, 3, :], dt_t[:, 2, :], ALU.add)
            link(v.tensor_tensor(dt_t[:, 4, :], dt_t[:, 4, :], dt_t[:, 2, :], ALU.add))
            link(v.reciprocal(dt_t[:, 2, :], dt_t[:, 3, :]))
            link(v.tensor_tensor(dt_t[:, 4, :], dt_t[:, 4, :], dt_t[:, 2, :], ALU.mult))
            link(v.tensor_tensor(dt_t[:, 4, :], dt_t[:, 4, :], dt_t[:, 1, :], ALU.mult))
            by_seq = dt_t[:, :, :].rearrange("v k (b h) -> v k b h", h=H)
            v.scalar_tensor_tensor(out=dt_tab[:, :, 0, :], in0=by_seq[:, 0], scalar=0.0, in1=by_seq[:, 4], op0=ALU.max, op1=ALU.add)
            dve.wait_ge(S["taps0"], 2)
            v.tensor_scalar(tapw[0:V, :, :], convw_raw.rearrange("p (c k) -> p k c", k=TAPS), 0.5, None, ALU.mult)
            v.tensor_scalar(convb_half[:, :], convb_row[:, :], 0.5, None, ALU.mult).then_inc(S["s_aneg"], 1)
            dve.wait_ge(S["s_l"], 2)
            link(v.tensor_scalar(a_neg[:, :], a_neg[:, :], -1.0, None, ALU.mult))
            link(v.tensor_tensor(dt_tab[:, :, 1, :], dt_tab[:, :, 0, :], a_neg[0:V, :].unsqueeze(1).to_broadcast([V, B, H]), ALU.mult))
            dve.wait_ge(S["zpad"], 16)
            v.memset(stat[:, 14:15], 0.0).then_inc(S["s_dt"], 1)

            def by_head(ap):
                return ap.rearrange("p (h d) -> p h d", h=H)

            def sequence(b, q):
                wait_past(dve, "c_tab", b - 1)
                wait_past(dve, "c_out", 2 * b - 6)
                v.tensor_copy(xT_seq[:, q % 2], xT[:, bass.ds(b * V, V)])
                v.tensor_copy(hT_seq[:, q % 2], hT[:, bass.ds(b * V, V)])
                v.tensor_copy(hot_r[0:V, q, :], onehot[:, bass.ds(b, 1), :].rearrange("p a t -> p (a t)")).then_inc(S["c_seq"], 1)

            def tap_rests(b, q, pair):
                dve.wait_ge(S["c_hi"], 2 * b + pair + 1)
                taps = slice(2 * pair, 2 * pair + 2)
                v.tensor_tensor(taps_lo[:, q, taps, :], products[:, :, :], taps_hi[:, q, taps, :].bitcast(F32), ALU.subtract).then_inc(
                    S["c_taps"], 1)

            def z_table(b, q):
                dve.wait_ge(S["c_tz"], b + 1)
                dve.wait_ge(S["c_ht"], b + 1)
                v.scalar_tensor_tensor(out=ztab[:, q, :], in0=ztab[:, q, :], scalar=1.0, in1=bank[0][0:V, 0:DI],
                                       op0=ALU.add, op1=ALU.mult).then_inc(S["c_zt"], 1)

            def silu(n, r, c):
                if c == 0:
                    dve.wait_ge(S["c_st"], half(n, 0))
                dve.wait_ge(S["c_tanh"], n + 1)
                v.scalar_tensor_tensor(out=xbc[:, r, :], in0=tanh_x[:, :], scalar=1.0, in1=bank[2][:, 0:CONV],
                                       op0=ALU.add, op1=ALU.mult).then_inc(S["c_x"], 1)

            def causal_scores(n, r):
                dve.wait_ge(S["c_cb"], n + 1)
                v.tensor_tensor(cbm[:, r, :], bank[4][:, 3 * P:4 * P], upper[:, :], ALU.mult).then_inc(S["c_cbm"], 1)
                dve.wait_ge(S["c_cbm"], n + 1)
                dve.wait_ge(S["c_dec"], n + 1)
                v.tensor_tensor(decay[:, r], decay[:, r], cbm[:, r].unsqueeze(1).to_broadcast([P, H, P]), ALU.mult).then_inc(S["c_mix"], 1)

            def combine(n, r, c):
                dve.wait_ge(S["c_yd"], n + 1)
                dve.wait_ge(S["c_xsk"], n + 1)
                if c == 0:
                    v.tensor_tensor(y[:, r, :], bank[5][:, 0:DI], xskip[:, r, :], ALU.add).then_inc(S["c_y"], 1)
                else:
                    v.tensor_tensor(by_head(yoff[:, :]), by_head(bank[5][:, DI:2 * DI]),
                                    edge[:, r, :].unsqueeze(2).to_broadcast([P, H, HD]), ALU.mult)
                    v.tensor_tensor(y[:, r, :], bank[5][:, 0:DI], xskip[:, r, :], ALU.add).then_inc(S["c_yin"], 1)
                    dve.wait_ge(S["c_yin"], half(n, 1) + 1)
                    v.tensor_tensor(y[:, r, :], y[:, r, :], yoff[:, :], ALU.add).then_inc(S["c_y"], 1)

            def gate(n, r):
                dve.wait_ge(S["c_rms"], n + 1)
                v.tensor_scalar(rms[:, 1:2], rms[:, 0:1], EPS_RMS, None, ALU.add).then_inc(S["c_yo"], 1)
                dve.wait_ge(S["c_yo"], 2 * n + 1)
                v.reciprocal(rms[:, 2:3], rms[:, 1:2]).then_inc(S["c_yo"], 1)
                dve.wait_ge(S["c_yo"], 2 * n + 2)
                dve.wait_ge(S["c_zg"], n + 1)
                v.scalar_tensor_tensor(out=gated[:, :], in0=y[:, r, :], scalar=rms[:, 2:3], in1=bank[6][:, 0:DI],
                                       op0=ALU.mult, op1=ALU.mult).then_inc(S["c_g"], 1)

            def step(m, r, valid):
                k = STEPS * m + r
                c3, c4, c5 = (spot(r, lag)[0] for lag in (3, 4, 5))
                if r % 2 == 0 and valid(2):
                    tap_rests(4 * m + r // 2 - 1, (r // 2 - 1) % 2, 0)
                if r % 2 == 1 and valid(3):
                    tap_rests(4 * m + r // 2 - 1, (r // 2 - 1) % 2, 1)
                if valid(5) and c5 == 0:
                    dve.wait_ge(S["c_st"], half(k - 5, 0) + 1)
                    v.tensor_copy(state[:, :], bank[6][0:NS, DI:2 * DI]).then_inc(S["c_stc"], 1)
                if valid(4):
                    causal_scores(k - 4, c4)
                if r % 2 == 0 and valid(0):
                    sequence(4 * m + r // 2, r // 2)
                if r % 2 == 1 and valid(1):
                    z_table(4 * m + r // 2, r // 2)
                if valid(5):
                    gate(k - 5, c5)
                if valid(3):
                    silu(k - 3, c3, c3)
                if valid(6):
                    n = k - 6
                    dve.wait_ge(S["c_h3"], n + 1)
                    v.bn_stats(h3_bns[:, bass.ds(n, 1), :].rearrange("p a s -> p (a s)"), h3[:, bass.ds(n * P, P)]).then_inc(S["c_dt"], 1)
                if valid(4):
                    combine(k - 4, c4, c4)
            dve.wait_ge(S["c_ones"], 1)
            pipeline(dve, step)

            dve.wait_ge(S["c_dt"], NCH)
            col = [h3_bns[:, :, c] for c in range(6)]
            v.tensor_tensor(h3_s[:, 0, :], col[1], col[4], ALU.add)
            v.tensor_tensor(h3_s[:, 1, :], col[1], col[4], ALU.subtract)
            link(v.tensor_tensor(h3_s[:, 2, :], col[2], col[5], ALU.add))
            v.tensor_scalar(h3_s[:, 0, :], h3_s[:, 0, :], 0.5, None, ALU.mult)
            link(v.tensor_tensor(h3_s[:, 3, :], h3_s[:, 1, :], h3_s[:, 1, :], ALU.mult))
            v.scalar_tensor_tensor(out=h3_s[:, 2, :], in0=h3_s[:, 3, :], scalar=D / 4.0, in1=h3_s[:, 2, :],
                                   op0=ALU.mult, op1=ALU.add).then_inc(S["f_st"], 1)
            dve.wait_ge(S["f_sd"], 1)
            link(v.reciprocal(h3_s[:, 4, :], h3_s[:, 3, :]))

            def mlp_dve(m, r, valid):
                k = 4 * m + r
                if valid(0):
                    wait_past(dve, "m_xt", k - 1)
                    for c in range(TD):
                        n = TD * k + c
                        last = v.tensor_scalar(xn[:, r % 2, c, :], h3[:, bass.ds(n * P, P)], h3_s[:, 0, bass.ds(n, 1)], h3_s[:, 4, bass.ds(n, 1)],
                                               ALU.subtract, ALU.mult)
                    last.then_inc(S["m_xn"], 1)
                if valid(1):
                    q = (r - 1) % 2
                    dve.wait_ge(S["m_xt"], k)
                    wait_past(dve, "m_1", k - 2)
                    v.tensor_copy(xnT[:, q, :], bank[q][:, :]).then_inc(S["m_xtc"], 1)
                if valid(3):
                    q = (r - 3) % 4
                    dve.wait_ge(S["m_2"], k - 2)
                    dve.wait_ge(S["m_res"], k - 2)
                    wait_past(dve, f"m_st{q}", 16 * (m + (r - 3 - q) // 4))
                    v.tensor_tensor(fin[:, q], bank[4 + q % 2][:, :].rearrange("p (c d) -> p c d", d=D), res[:, q], ALU.add).then_inc(S["m_fin"], 1)

            rolling(dve, mlp_dve, NT, 4, 3)


_INS = ['x', 'L0_tok_embed_weight', 'L0_attn_attention_weights', 'L0_ffn_router_w', 'L0_ffn_w1', 'L0_ffn_b1',
        'L0_ffn_w2', 'L0_ffn_b2', 'L0_ffn_gamma', 'L0_ffn_beta', 'L1_attn_W_in', 'L1_attn_conv_w',
        'L1_attn_conv_b', 'L1_attn_A_log', 'L1_attn_dt_bias', 'L1_attn_D', 'L1_attn_norm_w', 'L1_attn_W_out',
        'L1_ffn_W1', 'L1_ffn_b1', 'L1_ffn_W2', 'L1_ffn_b2']


def kernel(**inputs):
    import numpy as _np
    import concourse.bacc as _bacc
    from concourse import mybir as _mybir
    from concourse.bass_utils import run_bass_kernel_spmd as _run

    nc = _bacc.Bacc("TRN2", target_bir_lowering=False, num_devices=1)
    arrays, args = {}, []
    for name in _INS:
        a = _np.ascontiguousarray(inputs[name])
        arrays[f"in_{name}"] = a
        args.append(nc.dram_tensor(f"in_{name}", a.shape, _mybir.dt.from_np(a.dtype), kind="ExternalInput").ap())
    b, t = inputs['x'].shape
    d = inputs['L0_tok_embed_weight'].shape[1]
    out = nc.dram_tensor("out", (b, t, d), _mybir.dt.float32, kind="ExternalOutput").ap()
    lm_tower(nc, *args, out)
    r = _run(nc, [arrays], core_ids=[0])
    return r.results[0]["out"]
```

```python
from contextlib import ExitStack

import concourse.bass as bass
from concourse import mybir

F32 = mybir.dt.float32
F32R = mybir.dt.float32r
U8 = mybir.dt.uint8
I32 = mybir.dt.int32
U32 = mybir.dt.uint32
ALU = mybir.AluOpType
ACT = mybir.ActivationFunctionType
AX = mybir.AxisListType

P = 128
BANK = 512
EPS_LN = 1e-5
EPS_FFN = 1e-6
EPS_RMS = 1e-5


def lm_tower(nc, x, emb, attn_w, router_w, w1, b1, w2, b2, gamma, beta,
             W_in, conv_w, conv_b, A_log, dt_bias, Dskip, norm_w, W_out,
             tri_w1, tri_b1, tri_w2, tri_b2, out):
    B, T = x.shape
    V, D = emb.shape
    E, _, F = w1.shape
    FT = F // P
    CONV, _, TAPS = conv_w.shape
    H = A_log.shape[0]
    DI = norm_w.shape[0]
    HD = DI // H
    NS = (CONV - DI) // 2
    PAD = TAPS - 1
    RR = B * V
    N2 = 2 * P
    NI = RR // N2
    NTILE = RR // P
    CH = T // P
    NCH = B * CH
    assert D == P and CH == 2 and RR % N2 == 0 and V < P and F % P == 0

    ctx = ExitStack()
    with ctx:
        def sb(name, shape, dt=F32):
            return ctx.enter_context(nc.sbuf_tensor(name, shape, dt))

        def sem(name):
            return ctx.enter_context(nc.semaphore(name))

        bank = [ctx.enter_context(nc.psum_tensor(f"bank{i}", [P, BANK], F32)) for i in range(8)]

        REGION = 16384 + 1920
        early = ExitStack()
        w1_hi, w1_lo = (early.enter_context(nc.sbuf_tensor(n, [P, E, F], F32R, side="right")) for n in ("w1_hi", "w1_lo"))
        x_hi, x_lo = (early.enter_context(nc.sbuf_tensor(n, [P, 2 * P], F32R, side="right")) for n in ("x_hi", "x_lo"))
        region = [early.enter_context(nc.sbuf_tensor("early", [P, REGION - 2 * E * F - 4 * P], F32, side="right"))]
        place = [0]

        def phase():
            place[0] = 0

        def take(shape, dt=F32):
            size = 1
            for s in shape[1:]:
                size *= s
            view = region[0][0:shape[0], place[0]:place[0] + size]
            place[0] += size
            assert place[0] <= region[0].shape[1], place[0]
            if dt != F32:
                view = view.bitcast(dt)
            if len(shape) > 2:
                axes = "abc"[:len(shape) - 1]
                view = view.rearrange(f"p ({' '.join(axes)}) -> p {' '.join(axes)}",
                                      **dict(zip(axes[1:], shape[2:])))
            return view

        ident = sb("ident", [P, P])
        upper = sb("upper", [P, P])
        later = sb("later", [P, P])
        later_r = ctx.enter_context(nc.sbuf_tensor("later_r", [P, P], F32R))
        mean_w = sb("mean_w", [P, P])
        vocab = sb("vocab", [V, 1])
        experts8 = sb("experts8", [P, E])
        half_pow = sb("half_pow", [P, 1])
        eps_ln = sb("eps_ln", [P, 1])
        eps_ffn = sb("eps_ffn", [P, 1])

        onehot = sb("onehot", [V, B, PAD + T], U8)
        hT = sb("hT", [P, RR])
        xT = sb("xT", [P, RR])
        arena = sb("arena", [P, NCH * P])
        w1_sb = arena[:, 0:E * F].rearrange("p (e f) -> p e f", e=E)
        w2_sb = arena[:, E * F:2 * E * F].rearrange("p (e c d) -> p e c d", e=E, c=FT)
        xrows = arena[:, 2 * E * F:2 * E * F + RR]
        TOKB = 8
        TOKN = 4
        tok = arena[0:V, 2 * E * F:2 * E * F + TOKN * TOKB * T].bitcast(I32).rearrange(
            "p (n b t) -> p n b t", n=TOKN, b=TOKB)
        h3 = arena[:, :]

        phase()
        gamma_bc = take([P, E * D])
        b2_bc = take([P, E * D])
        cen2, sqr2 = (take([P, 2, N2]) for _ in range(2))
        cen, sqr = cen2[:, 0, :], sqr2[:, 0, :]
        dev, rstd = (take([P, N2]) for _ in range(2))
        kept = place[0]
        region_first = region[0]
        region[0] = xT
        phase()
        emb_sb = take([V, D])
        attn_sb = take([D, D])
        router_sb = sb("router_sb", [D, E])
        b1_rows = take([E * FT, P])
        b1_col = sb("b1_col", [P, E * FT])
        beta_sb = sb("beta_sb", [E, D])
        NZX = 2 * DI + 2 * NS
        win_rows = take([P, NZX // P, D])
        windt_rows = take([H, D])
        win_T = sb("win_T", [D, NZX])
        windt_T = sb("windt_T", [D, H])
        convw_raw = arena[0:V, 2 * E * F:2 * E * F + CONV * TAPS]
        tapw = sb("tapw", [V + 1, TAPS, CONV])
        ones = sb("ones", [P, 1])
        after_raw = 2 * E * F + CONV * TAPS
        convb_row = arena[0:1, after_raw:after_raw + CONV]
        convb_half = arena[0:1, after_raw + CONV:after_raw + 2 * CONV]
        a_neg = sb("a_neg", [P, H])
        alog_bc = sb("alog_bc", [P, H])
        dtb_bc = sb("dtb_bc", [V, H])
        d_bc = sb("d_bc", [P, H])
        normw_col = sb("normw_col", [P, DI // P])
        normw_rows = take([DI // P, P])
        wout_rows = take([D, DI])
        wout_T = sb("wout_T", [P, DI // P, D])
        tri1_rows = take([P, P])
        tri2_rows = take([P, P])
        tri1_T = sb("tri1_T", [P, P])
        tri2_T = sb("tri2_T", [P, P])
        trib1_col = sb("trib1_col", [P, 1])
        trib2_bc = sb("trib2_bc", [P, P])

        counts = sb("counts", [V, B])
        rden = sb("rden", [V, B])
        lne = take([V, D])
        lneT = take([D, V])
        projT = take([D, V])
        tanh_s = take([V, V])
        expT = take([V, V])
        stat = sb("stat", [P, 16])
        GA = 4
        weighted = take([V, 2, GA, D])
        h1rows = take([V, 2, GA, D])

        region[0] = region_first
        place[0] = kept
        xT_now = take([P, 2, N2])
        logits = take([P, NTILE, E])
        top_v = take([P, NTILE, 8])
        top_i = take([P, NTILE, 8], U32)
        idxs = take([P, NTILE, 2])
        gdiff = take([P, NTILE])
        gexp = take([P, NTILE])
        gates = take([P, NTILE, 2])
        pick = take([P, NTILE, E])
        wgate = sb("wgate", [P, NTILE, E])

        place[0] = kept
        hid = arena[:, 0:2 * FT * N2].rearrange("p (k f n) -> p k f n", k=2, f=FT)
        xb2 = arena[:, 2 * FT * N2:2 * FT * N2 + 2 * E * D].rearrange("p (j n) -> p j n", j=2)
        assert 2 * FT * N2 + 2 * E * D <= E * F
        pre = take([P, 2, E * D])
        bns = take([P, 2 * E, 6])
        sm = take([P, 8, 2 * E])
        summed = take([P, 2, D])
        w_now = take([P, 2, E])
        wT_now = take([E, N2])

        GD = 8
        EARLY = 6
        assert EARLY * GD * V <= (NI - 1) * N2 and EARLY + 2 == B // GD
        early.close()

        def rounded(name, shape):
            return ctx.enter_context(nc.sbuf_tensor(name, shape, F32R, side="right"))

        hot_r = rounded("hot_r", [V + 1, 4, PAD + T])
        hot = hot_r[:, :, :].bitcast(F32)
        taps_hi = rounded("taps_hi", [V + 1, 2, TAPS, CONV])
        taps_lo = rounded("taps_lo", [V + 1, 2, TAPS, CONV])
        amask_hi = rounded("amask_hi", [P, H, P])
        amask_lo = rounded("amask_lo", [P, H, P])
        z_hi = rounded("z_hi", [V, 4, DI])
        z_lo = rounded("z_lo", [V, 4, DI])
        LATE = REGION - 4 * (PAD + T) - 4 * TAPS * CONV - 2 * H * P - 8 * DI - 4
        region[0] = ctx.enter_context(nc.sbuf_tensor("late", [P, LATE], F32, side="right"))
        phase()
        dt_in = arena[:, 0:2 * GD * V].rearrange("p (q n) -> p q n", q=2)
        dt_t = take([V, 5, B * H])
        phase()
        xT_seq = take([D, 2, V])
        hT_seq = take([D, 2, V])
        dt_tab = sb("dt_tab", [V, B, 2, H])
        ztab = take([V, DI])
        xtab = take([V + 1, CONV])
        products = take([V + 1, 2, CONV])
        htab = take([V, 4, D])
        tanh_x = take([P, CONV])
        xbc = take([P, 2, CONV])
        dts = take([P, 4, 2, 2 * H])
        dts_hi = take([P, 4, 2, 2 * H])
        dts_lo = take([P, 4, 2, 2 * H])
        xdt = take([P, 2, DI])
        xskip = take([P, 2, DI])
        xtail = take([P, DI])
        yoff = xtail
        bcT = take([NS, 2, 2 * P])
        cbm = take([P, 2, P])
        edge = take([P, 2, H])
        decay = take([P, 2, H, P])
        state = take([NS, DI])
        y = take([P, 2, DI])
        ssum = take([P, 1])
        ms = take([P, 1])
        rms = take([P, 3])
        gated = take([P, DI])
        gT = take([P, DI])

        h3_bns = sb("h3_bns", [P, NCH, 6])
        TD = 4
        phase()
        NT = NCH // TD
        h3_s = take([P, 5, NCH])
        xn = take([P, 2, TD, D])
        xnT = take([P, 2, TD * P])
        gel = take([P, 2, TD * P])
        res = take([P, 4, TD, D])
        fin = take([P, 4, TD, D])

        names = """ld_att ld_w1 w1_cut b_xhi b_xlo ld_ffn ld_ssm ld_mlp ld_rout const_ok zero_ok tok_ld0 tok_ld1 tok_ld2 tok_ld3
            tok_used dchain e_var e_sd e_ln e_lnT e_lnT_c e_pT e_pT_c e_sc e_tanh e_exp e_cnt
            e_den e_rden w_tr w_trc at_w at_num at_h at_t at_s r_mean r_c r_sq r_var r_sd r_x
            r_cp r_tr r_rt r_xf r_lg r_gd r_ge r_gates b_up b_relu b_dn b_y b_xb2 b_pre00
            b_pre01 b_pre10 b_pre11 b_var b_sd b_u b_ug b_o b_z b_h2 b_mean b_c b_sq b_v2 b_sd2
            b_x b_wn b_wt b_wtc rchain bchain s_in s_raw s_v s_e s_l s_dt s_aneg c_seq c_tab
            c_tx c_tz c_zt c_ht c_taps c_cv c_tanh c_x c_dt c_mask c_xsk c_xtl c_bc c_cb c_cbm
            c_seg c_dec c_edc c_mix c_yd c_st c_stc c_yo c_y c_sq c_rms c_zg c_g c_gt c_gtc
            c_out c_h3 c_bn gchain f_st f_sd m_xn m_xt m_xtc m_1 m_gel m_2 m_res m_fin m_st0
            m_st1 m_st2 m_st3 zpad taps0 w_nw r_top r_ti b_bn c_prod c_hi c_ones c_yin c_zhi c_zlo c_dts
            c_masklo c_dtlo""".split()
        S = {n: sem(n) for n in names}

        class Chain:

            def __init__(self, eng, name):
                self.eng, self.sem, self.base, self.n = eng, S[name], 0, 0

            def start(self, base):
                self.base, self.n = base, 0

            def link(self, ins):
                self.n += 1
                ins.then_inc(self.sem, 1)
                self.eng.wait_ge(self.sem, self.base + self.n)

        def bc_rows(ap, n):
            return ap.unsqueeze(0).to_broadcast([n] + list(ap.shape))

        def flat(ap):
            return ap.rearrange("e d -> (e d)")

        B_LINKS = 5
        STEPS = 8

        def rolling(eng, step, count, body, depth):
            first = -(-depth // body)
            full = count // body
            for k in range(first * body):
                step(k // body, k % body, lambda lag: k >= lag)
            with eng.Fori(first, full) as m:
                for r in range(body):
                    step(m, r, lambda lag: True)
            for k in range(full * body, count + depth):
                step(k // body, k % body, lambda lag: k - lag < count)

        def pipeline(eng, step):
            rolling(eng, step, NCH, STEPS, 6)

        def wait_past(eng, name, value):
            if not (isinstance(value, int) and value <= 0):
                eng.wait_ge(S[name], value)

        def spot(r, lag):
            s = (r - lag) % STEPS
            return s % 2, s // 2

        def half(n, c):
            return (n - c) // 2

        block = ctx.enter_context(nc.Block())

        @block.sync
        def _(sp):
            att = [(emb_sb[:, :], emb), (attn_sb[:, :], attn_w)]
            for dst, src in att:
                sp.dma_start(dst, src).then_inc(S["ld_att"], 16)
            for n in range(TOKN):
                sp.dma_start(tok[:, n], bc_rows(x[n * TOKB:(n + 1) * TOKB, :], V)).then_inc(S[f"tok_ld{n}"], 16)
            sp.dma_start(w1_sb, w1.rearrange("e d f -> d e f")).then_inc(S["ld_w1"], 16)
            rout = [(router_sb[:, :], router_w), (b1_rows[:, :], b1.rearrange("e (c p) -> (e c) p", p=P)),
                    (win_rows[:, :, :], W_in[0:NZX, :].rearrange("(c p) d -> p c d", p=P)),
                    (windt_rows[:, :], W_in[NZX:NZX + H, :]),
                    (wout_rows[:, :], W_out), (tri1_rows[:, :], tri_w1), (tri2_rows[:, :], tri_w2),
                    (normw_rows, norm_w.rearrange("(c p) -> c p", p=P))]
            for dst, src in rout:
                sp.dma_start(dst, src).then_inc(S["ld_rout"], 16)
            for n in range(TOKN, B // TOKB):
                sp.wait_ge(S["tok_used"], n - TOKN + 1)
                sp.dma_start(tok[:, n % TOKN], bc_rows(x[n * TOKB:(n + 1) * TOKB, :], V)).then_inc(
                    S[f"tok_ld{n % TOKN}"], 16)
            ffn = [(b2_bc[:, :], bc_rows(flat(b2), P)), (gamma_bc[:, :], bc_rows(flat(gamma), P)),
                   (beta_sb[:, :], beta)]
            for dst, src in ffn:
                sp.dma_start(dst, src).then_inc(S["ld_ffn"], 16)
            for e in range(E):
                sp.dma_start(w2_sb[:, e], w2[e].rearrange("(c p) d -> p c d", p=P)).then_inc(S["ld_ffn"], 16)
            ssm = [(convw_raw, bc_rows(conv_w.rearrange("c o k -> (c o k)"), V)),
                   (convb_row[:, :], bc_rows(conv_b, 1)), (alog_bc[:, :], bc_rows(A_log, P)),
                   (dtb_bc[:, :], bc_rows(dt_bias, V)), (d_bc[:, :], bc_rows(Dskip, P))]
            sp.wait_ge(S["b_x"], NI)
            for dst, src in ssm:
                sp.dma_start(dst, src).then_inc(S["ld_ssm"], 16)
            mlp = [(trib1_col[:, :], tri_b1.unsqueeze(1)), (trib2_bc[:, :], bc_rows(tri_b2, P))]
            for dst, src in mlp:
                sp.dma_start(dst, src).then_inc(S["ld_mlp"], 16)
            sp.wait_ge(S["s_aneg"], 1)
            sp.dma_start(tapw[V:V + 1, TAPS - 1, :], convb_half[:, :]).then_inc(S["zpad"], 16)
            rows = out.rearrange("b (c p) d -> p (b c) d", p=P)
            with sp.Fori(1, NT // 4 + 1) as m:
                for q in range(4):
                    sp.wait_ge(S["m_fin"], 4 * m - 3 + q)
                    sp.dma_start(rows[:, bass.ds(4 * TD * m - (4 - q) * TD, TD), :], fin[:, q]).then_inc(S[f"m_st{q}"], 16)
            for q in range(4):
                sp.wait_ge(S[f"m_st{q}"], 16 * (NT // 4))

        N_ATT, N_ROUT, N_FFN, N_SSM, N_MLP = 2, 8, 3 + E, 5, 2

        @block.gpsimd
        def _(pool):
            g = nc.gpsimd
            g.memset(ident[:, :], 0.0).then_inc(S["zero_ok"], 1)
            g.memset(upper[:, :], 1.0).then_inc(S["zero_ok"], 1)
            g.memset(later[:, :], 1.0).then_inc(S["zero_ok"], 1)
            pool.wait_ge(S["zero_ok"], 3)
            g.affine_select(out=ident[:, :], in_=ident[:, :], compare_op=ALU.not_equal, fill=1.0, base=0,
                            pattern=[[-1, P]], channel_multiplier=1).then_inc(S["const_ok"], 1)
            g.affine_select(out=upper[:, :], in_=upper[:, :], compare_op=ALU.is_ge, fill=0.0, base=0,
                            pattern=[[1, P]], channel_multiplier=-1).then_inc(S["const_ok"], 1)
            g.affine_select(out=later[:, :], in_=later[:, :], compare_op=ALU.is_gt, fill=0.0, base=0,
                            pattern=[[-1, P]], channel_multiplier=1).then_inc(S["const_ok"], 1)
            g.iota(vocab[:, :], pattern=[[0, 1]], base=0, channel_multiplier=1,
                   allow_small_or_imprecise_dtypes=True).then_inc(S["const_ok"], 1)
            g.iota(experts8[:, :], pattern=[[1, E]], base=0, channel_multiplier=0,
                   allow_small_or_imprecise_dtypes=True).then_inc(S["const_ok"], 1)
            g.memset(mean_w[:, :], 1.0 / D).then_inc(S["const_ok"], 1)
            g.memset(half_pow[:, :], 0.5).then_inc(S["const_ok"], 1)
            g.memset(eps_ln[:, :], EPS_LN).then_inc(S["const_ok"], 1)
            g.memset(eps_ffn[:, :], EPS_FFN).then_inc(S["const_ok"], 1)
            g.memset(onehot[:, :, 0:PAD], 0.0).then_inc(S["const_ok"], 1)
            g.memset(ones[:, :], 1.0).then_inc(S["taps0"], 1)
            g.memset(tapw[:, :, :], 0.0).then_inc(S["taps0"], 1)

            pool.wait_ge(S["ld_w1"], 16)
            g.tensor_copy(w1_hi[:, :, :], w1_sb).then_inc(S["w1_cut"], 1)
            pool.wait_ge(S["w1_cut"], 1)
            g.tensor_tensor(w1_lo[:, :, :], w1_sb, w1_hi[:, :, :].bitcast(F32), ALU.subtract).then_inc(S["w1_cut"], 1)

            def routing_pool(m, r, valid):
                k = 2 * m + r
                if valid(0):
                    pool.wait_ge(S["r_c"], k + 1)
                    wait_past(pool, "r_var", k - 1)
                    g.tensor_tensor(sqr2[:, r], cen2[:, r], cen2[:, r], ALU.mult).then_inc(S["r_sq"], 1)
                if valid(2):
                    pool.wait_ge(S["r_x"], k - 1)
                    g.tensor_copy(xT[:, bass.ds((k - 2) * N2, N2)], xT_now[:, r]).then_inc(S["r_cp"], 1)

            rolling(pool, routing_pool, NI, 2, 2)

            def add_b2(i, gg, first):
                for j in range(2):
                    pool.wait_ge(S["r_xf"], NI)
                    if not first:
                        pool.wait_ge(S[f"b_pre{gg}{j}"], i - 1)
                    g.tensor_tensor(xb2[:, j, gg * BANK:(gg + 1) * BANK].rearrange("p (e d) -> p e d", d=D),
                                    b2_bc[:, gg * BANK:(gg + 1) * BANK].rearrange("p (e d) -> p e d", d=D),
                                    xrows[:, bass.ds((i - 1) * N2 + j * P, P)].unsqueeze(1).to_broadcast([P, 4, D]),
                                    ALU.add).then_inc(S["b_xb2"], 1)

            def expert_pool(i, first, cur, back):
                if cur:
                    pool.wait_ge(S["b_xhi"], i)
                    pool.wait_ge(S["b_up"], 16 * (i - 1))
                    g.tensor_tensor(x_lo[:, :], xT[:, bass.ds((i - 1) * N2, N2)], x_hi[:, :].bitcast(F32), ALU.subtract).then_inc(S["b_xlo"], 1)
                    add_b2(i, 0, first)
                if back:
                    for j in range(2):
                        pool.wait_ge(S["b_u"], 2 * i - 3 + j)
                        g.tensor_tensor(pre[:, j, :], pre[:, j, :], gamma_bc[:, :], ALU.mult).then_inc(S["b_ug"], 1)
                if cur:
                    add_b2(i, 1, first)
                    if first:
                        pool.wait_ge(S["r_gates"], 1)
                    else:
                        pool.wait_ge(S["b_wt"], i - 1)
                    g.tensor_copy(w_now[:, :, :], wgate[:, bass.ds(2 * (i - 1), 2), :]).then_inc(S["b_wn"], 1)
                if back:
                    pool.wait_ge(S["b_c"], i - 1)
                    g.tensor_tensor(sqr, cen, cen, ALU.mult).then_inc(S["b_sq"], 1)

            pool.wait_ge(S["r_xf"], NI)
            pool.wait_ge(S["r_cp"], NI)
            pool.wait_ge(S["ld_ffn"], 16 * N_FFN)
            expert_pool(1, True, True, False)
            with pool.Fori(2, NI + 1) as i:
                expert_pool(i, False, True, True)
            expert_pool(NI + 1, False, False, True)

            pool.wait_ge(S["b_x"], NI)
            chain = Chain(pool, "gchain")

            def tap_products(b, pair):
                if pair == 0:
                    pool.wait_ge(S["c_tx"], b + 1)
                wait_past(pool, "c_taps", 2 * b + pair)
                g.tensor_tensor(products[:, :, :], xtab[:, :].unsqueeze(1).to_broadcast([V + 1, 2, CONV]),
                                tapw[:, 2 * pair:2 * pair + 2, :], ALU.mult).then_inc(S["c_prod"], 1)

            def by_head(ap):
                return ap.rearrange("p (h d) -> p h d", h=H)

            def steps_of(q, c, part):
                return dts[:, q, c, part * H:(part + 1) * H]

            def mask_pool(n, q, c):
                pool.wait_ge(S["c_dts"], half(n, c) + 1)
                wait_past(pool, "c_seg", n)
                g.tensor_tensor(amask_hi[:, :, :], upper[:, :].unsqueeze(1).to_broadcast([P, H, P]),
                                steps_of(q, c, 1).unsqueeze(2).to_broadcast([P, H, P]), ALU.mult).then_inc(S["c_mask"], 1)

            def inputs_pool(n, q, c):
                pool.wait_ge(S["c_x"], n + 1)
                wait_past(pool, "c_y", n - 1)
                chain.start(n)
                chain.link(g.tensor_tensor(by_head(xdt[:, c]), by_head(xbc[:, c, 0:DI]),
                                           steps_of(q, c, 0).unsqueeze(2).to_broadcast([P, H, HD]), ALU.mult))
                g.tensor_tensor(by_head(xskip[:, c]), by_head(xbc[:, c, 0:DI]),
                                d_bc[:, :].unsqueeze(2).to_broadcast([P, H, HD]), ALU.mult).then_inc(S["c_xsk"], 1)

            def tail_pool(n, c):
                pool.wait_ge(S["c_edc"], n + 1)
                wait_past(pool, "c_y", n)
                g.tensor_tensor(by_head(xtail[:, :]), by_head(xdt[:, c]),
                                edge[:, c].unsqueeze(2).to_broadcast([P, H, HD]), ALU.mult).then_inc(S["c_xtl"], 1)

            def rms_pool(n):
                pool.wait_ge(S["c_sq"], n + 1)
                g.tensor_tensor(rms[:, 0:1], ms[:, :], half_pow[:, :], ALU.pow).then_inc(S["c_rms"], 1)

            def step(m, r, valid):
                k = STEPS * m + r
                c3, q3 = spot(r, 3)
                c4, q4 = spot(r, 4)
                if valid(5) and c4 == 1:
                    rms_pool(k - 5)
                if valid(3):
                    mask_pool(k - 3, q3, c3)
                if c4 == 0 and valid(4):
                    tail_pool(k - 4, c4)
                if valid(5) and c4 == 0:
                    rms_pool(k - 5)
                if r % 2 == 1 and valid(1):
                    tap_products(4 * m + r // 2, 0)
                if r % 2 == 0 and valid(2):
                    tap_products(4 * m + r // 2 - 1, 1)
                if valid(3):
                    inputs_pool(k - 3, q3, c3)

            pool.wait_ge(S["taps0"], 2)
            g.tensor_copy(later_r[:, :], later[:, :])
            g.tensor_copy(hot_r[:, :, :].rearrange("v q t -> v (q t)"), ones[0:V + 1, :].to_broadcast([V + 1, 4 * (PAD + T)]))
            pool.wait_ge(S["s_dt"], 1)
            g.memset(xtab[:, :], 1.0).then_inc(S["c_ones"], 1)
            pool.wait_ge(S["c_ones"], 1)
            pipeline(pool, step)

            pool.wait_ge(S["c_h3"], NCH)
            pool.wait_ge(S["ld_mlp"], 16 * N_MLP)
            def mlp_pool(m, r, valid):
                k = 4 * m + r
                if valid(0):
                    now = k - 3 if isinstance(k, int) else pool.snap(k - 3)
                    pool.wait_ge(S["c_h3"], NCH)
                    wait_past(pool, "m_fin", now)
                    g.tensor_tensor(res[:, r], h3[:, bass.ds(k * TD * P, TD * P)].rearrange("p (c d) -> p c d", d=D),
                                    trib2_bc[:, :].unsqueeze(1).to_broadcast([P, TD, D]), ALU.add).then_inc(S["m_res"], 1)

            rolling(pool, mlp_pool, NT, 4, 3)

        @block.tensor
        def _(pe):
            t = nc.tensor
            mm = t.matmul

            pe.wait_ge(S["const_ok"], 10)
            pe.wait_ge(S["e_ln"], 1)
            t.transpose(bank[3][:, 0:V], lne[:, :], ident[0:V, 0:V]).then_inc(S["e_lnT"], 1)
            pe.wait_ge(S["e_lnT_c"], 1)
            pe.wait_ge(S["ld_att"], 16 * N_ATT)
            mm(bank[3][:, 128:128 + V], attn_sb[:, :], lneT[:, :], start=True, stop=True).then_inc(S["e_pT"], 1)
            pe.wait_ge(S["e_pT_c"], 1)
            mm(bank[3][0:V, 256:256 + V], lneT[:, :], projT[:, :], start=True, stop=True).then_inc(S["e_sc"], 1)

            pe.wait_ge(S["ld_rout"], 16 * N_ROUT)
            for c in range(4):
                last = t.transpose(bank[0][:, c * P:(c + 1) * P], win_rows[:, c, :], ident[:, :])
            last.then_inc(S["w_tr"], 1)
            t.transpose(bank[1][:, 0:P], win_rows[:, 4, :], ident[:, :])
            t.transpose(bank[1][:, P:P + H], windt_rows[:, :], ident[0:H, 0:H])
            t.transpose(bank[1][:, P + H:P + H + DI // P], normw_rows, ident[0:DI // P, 0:DI // P])
            for c in range(DI // P):
                last = t.transpose(bank[1][:, (2 + c) * P - 64:(3 + c) * P - 64], wout_rows[:, c * P:(c + 1) * P], ident[:, :])
            last.then_inc(S["w_tr"], 1)
            t.transpose(bank[2][:, 0:P], tri1_rows[:, :], ident[:, :])
            t.transpose(bank[2][:, P:2 * P], tri2_rows[:, :], ident[:, :])
            t.transpose(bank[2][:, 2 * P:2 * P + E * FT], b1_rows[:, :], ident[0:E * FT, 0:E * FT]).then_inc(S["w_tr"], 1)

            pe.wait_ge(S["e_exp"], 1)
            pe.wait_ge(S["e_cnt"], 1)
            mm(bank[4][0:V, 0:B], expT[:, :], counts[:, :], start=True, stop=True).then_inc(S["e_den"], 1)
            pe.wait_ge(S["w_trc"], 3)
            def attention_pe(m, r, valid):
                k = 2 * m + r
                if valid(0):
                    pe.wait_ge(S["at_w"], k + 1)
                    wait_past(pe, "at_h", k - 1)
                    mm(bank[r][0:V, :], expT[:, :], weighted[:, r].rearrange("p j d -> p (j d)"),
                       start=True, stop=True).then_inc(S["at_num"], 1)
                if valid(1):
                    pe.wait_ge(S["at_h"], k)
                    wait_past(pe, "at_s", k - 2)
                    for j in range(GA):
                        last = t.transpose(bank[3 - r][:, j * V:(j + 1) * V], h1rows[:, 1 - r, j, :], ident[0:V, 0:V])
                    last.then_inc(S["at_t"], 1)

            rolling(pe, attention_pe, B // GA, 2, 1)

            pe.wait_ge(S["at_s"], B // GA)
            def routing_pe(m, r, valid):
                k = 2 * m + r
                if valid(0):
                    wait_past(pe, "r_c", k)
                    mm(bank[0][:, 0:N2], mean_w[:, :], hT[:, bass.ds(k * N2, N2)], start=True, stop=True).then_inc(S["r_mean"], 1)
                if valid(1):
                    pe.wait_ge(S["r_sq"], k)
                    wait_past(pe, "r_sd", k - 1)
                    mm(bank[1][:, 0:N2], mean_w[:, :], sqr2[:, 1 - r], start=True, stop=True).then_inc(S["r_var"], 1)
                if valid(2):
                    pe.wait_ge(S["r_x"], k - 1)
                    wait_past(pe, "r_lg", k - 2)
                    for j in range(2):
                        last = mm(bank[3][:, j * E:(j + 1) * E], xT_now[:, r, j * P:(j + 1) * P], router_sb[:, :], start=True, stop=True)
                    last.then_inc(S["r_rt"], 1)
                    wait_past(pe, "r_xf", k - 2)
                    for j in range(2):
                        last = t.transpose(bank[2][:, j * P:(j + 1) * P], xT_now[:, r, j * P:(j + 1) * P], ident[:, :])
                    last.then_inc(S["r_tr"], 1)

            rolling(pe, routing_pe, NI, 2, 2)

            def up(i, e, first):
                if e == 0:
                    pe.wait_ge(S["b_xlo"], i)
                for hb in range(FT // 2):
                    k = 16 * (i - 1) + 2 * e + hb
                    if not (first and e < 1):
                        pe.wait_ge(S["b_relu"], k - 1)
                    u = bank[hb]
                    for f in range(2):
                        ft = 2 * hb + f
                        for k, (w, rows) in enumerate(((w1_hi, x_hi), (w1_hi, x_lo), (w1_lo, x_hi))):
                            last = mm(u[:, f * N2:(f + 1) * N2], w[:, e, ft * P:(ft + 1) * P], rows[:, :], start=(k == 0), stop=(k == 2))
                    last.then_inc(S["b_up"], 1)

            def down(i, e, first):
                pe.wait_ge(S["b_relu"], 16 * (i - 1) + 2 * e + 2)
                gg, k4 = divmod(e, 4)
                for j in range(2):
                    if k4 == 0 and not first:
                        pe.wait_ge(S[f"b_pre{gg}{j}"], i - 1)
                    for ft in range(FT):
                        last = mm(bank[2 + 2 * gg + j][:, k4 * P:(k4 + 1) * P], hid[:, e % 2, ft, j * P:(j + 1) * P],
                                  w2_sb[:, e, ft, :], start=(ft == 0), stop=(ft == FT - 1))
                    if k4 == 3 and j == 0:
                        last.then_inc(S["b_y"], 1)
                last.then_inc(S["b_dn"], 1)

            def sum_rows(i):
                pe.wait_ge(S["b_wtc"], i)
                pe.wait_ge(S["b_o"], i)
                mm(bank[6][:, 0:N2], beta_sb[:, :], wT_now[:, :], start=True, stop=False, skip_group_check=True)
                for j in range(2):
                    last = mm(bank[6][:, j * P:(j + 1) * P], summed[:, j, :], ident[:, :], start=False, stop=True, skip_group_check=True)
                last.then_inc(S["b_z"], 1)

            def stream_mean(i):
                pe.wait_ge(S["b_h2"], i)
                mm(bank[6][:, N2:2 * N2], mean_w[:, :], hT[:, bass.ds((i - 1) * N2, N2)], start=True, stop=True).then_inc(S["b_mean"], 1)

            def stream_variance(i):
                pe.wait_ge(S["b_sq"], i)
                mm(bank[7][:, 0:N2], mean_w[:, :], sqr, start=True, stop=True).then_inc(S["b_v2"], 1)

            def expert_pe(i, first, back):
                for e in range(E):
                    up(i, e, first)
                    if back and e == 7:
                        stream_variance(i - 1)
                    if e > 0:
                        down(i, e - 1, first)
                    elif back:
                        down(i - 1, E - 1, False)
                    if back and e == 5:
                        sum_rows(i - 1)
                    if back and e == 6:
                        stream_mean(i - 1)
                pe.wait_ge(S["b_wn"], i)
                if back:
                    pe.wait_ge(S["b_sd2"], i - 1)
                for j in range(2):
                    last = t.transpose(bank[7][0:E, N2 + j * P:N2 + (j + 1) * P], w_now[:, j, :], ident[:, :])
                last.then_inc(S["b_wt"], 1)

            pe.wait_ge(S["r_xf"], NI)
            pe.wait_ge(S["r_lg"], NI)
            pe.wait_ge(S["ld_ffn"], 16 * N_FFN)
            expert_pe(1, True, False)
            with pe.Fori(2, NI + 1) as i:
                expert_pe(i, False, True)
            down(NI, E - 1, False)

            def step_products(groups):
                for q in range(2):
                    pe.wait_ge(S["s_in"], groups + q + 1)
                    for j in range(GD):
                        last = mm(bank[0][0:V, bass.ds((groups + q) * GD * H + j * H, H)], dt_in[:, q, j * V:(j + 1) * V], windt_T[:, :],
                                  start=True, stop=True)
                    last.then_inc(S["s_raw"], 1)

            with pe.Fori(1, EARLY // 2 + 1) as m:
                step_products(2 * m - 2)
            sum_rows(NI)
            stream_mean(NI)
            stream_variance(NI)
            step_products(EARLY)

            def tables(b, q):
                pe.wait_ge(S["c_seq"], b + 1)
                wait_past(pe, "c_zt", b)
                wait_past(pe, "c_ht", b)
                wait_past(pe, "c_dts", b)
                mm(bank[0][0:V, 0:BANK], xT_seq[:, q % 2], win_T[:, 0:BANK], start=True, stop=True)
                mm(bank[1][0:V, 0:P], xT_seq[:, q % 2], win_T[:, BANK:NZX], start=True, stop=True)
                t.transpose(bank[1][0:V, P:2 * P], hT_seq[:, q % 2], ident[:, :])
                for c in range(2):
                    last = mm(bank[1][:, 2 * P + 2 * H * c:2 * P + 2 * H * (c + 1)], hot[0:V, q, PAD + c * P:PAD + (c + 1) * P],
                              dt_tab[:, bass.ds(b, 1), :, :].rearrange("v a k h -> v (a k h)"), start=True, stop=True)
                last.then_inc(S["c_tab"], 1)

            def convolve(n, q, c, pair):
                pe.wait_ge(S["c_taps"], 2 * half(n, c) + pair + 1)
                if pair == 0:
                    wait_past(pe, "c_x", n)
                for k in (2 * pair, 2 * pair + 1):
                    for part in (taps_hi, taps_lo):
                        last = mm(bank[2][:, 0:CONV], hot_r[:, q, c * P + k:c * P + k + P], part[:, q % 2, k, :],
                                  start=(k == 0 and part is taps_hi), stop=(k == TAPS - 1 and part is taps_lo), skip_group_check=True)
                if pair == 1:
                    last.then_inc(S["c_cv"], 1)

            def decay_sums(n, c):
                pe.wait_ge(S["c_mask"], n + 1)
                pe.wait_ge(S["c_masklo"], n + 1)
                wait_past(pe, "c_dec", n)
                mm(bank[3][:, :], later_r[:, :], amask_hi[:, :, :].rearrange("p h l -> p (h l)"), start=True, stop=False)
                mm(bank[3][:, :], later_r[:, :], amask_lo[:, :, :].rearrange("p h l -> p (h l)"), start=False, stop=True).then_inc(S["c_seg"], 1)

            def turn_bc(n, q, c):
                pe.wait_ge(S["c_x"], n + 1)
                pe.wait_ge(S["c_cbm"], n)
                mm(bank[4][:, 2 * P:2 * P + H], (upper if c else later)[:, :], dts[:, q, c, H:2 * H], start=True, stop=True)
                t.transpose(bank[4][0:NS, 0:P], xbc[:, c, DI:DI + NS], ident[:, :])
                t.transpose(bank[4][0:NS, P:2 * P], xbc[:, c, DI + NS:CONV], ident[:, :]).then_inc(S["c_bc"], 1)

            def scores(n, c):
                pe.wait_ge(S["c_edc"], n + 1)
                mm(bank[4][:, 3 * P:4 * P], bcT[:, c, 0:P], bcT[:, c, P:2 * P], start=True, stop=True).then_inc(S["c_cb"], 1)

            def mixed(n, c):
                pe.wait_ge(S["c_mix"], n + 1)
                pe.wait_ge(S["c_xsk"], n + 1)
                wait_past(pe, "c_y", n)
                if c == 1:
                    pe.wait_ge(S["c_stc"], half(n, 1) + 1)
                    mm(bank[5][:, DI:2 * DI], bcT[:, c, P:2 * P], state[:, :], start=True, stop=True)
                for h in range(H):
                    last = mm(bank[5][:, h * HD:(h + 1) * HD], decay[:, c, h, :], xdt[:, c, h * HD:(h + 1) * HD], start=True, stop=True)
                last.then_inc(S["c_yd"], 1)

            def chunk_state(n, c):
                pe.wait_ge(S["c_xtl"], half(n, 0) + 1)
                wait_past(pe, "c_g", n)
                mm(bank[6][0:NS, DI:2 * DI], xbc[:, c, DI:DI + NS], xtail[:, :], start=True, stop=True).then_inc(S["c_st"], 1)

            def gate_rows(n, q, c):
                wait_past(pe, "c_g", n)
                wait_past(pe, "c_stc", half(n, c) + 1)
                pe.wait_ge(S["c_zlo"], half(n, c) + 1)
                rows = hot_r[0:V, q, PAD + c * P:PAD + (c + 1) * P]
                mm(bank[6][:, 0:DI], rows, z_hi[:, q, :], start=True, stop=False)
                mm(bank[6][:, 0:DI], rows, z_lo[:, q, :], start=False, stop=True).then_inc(S["c_zg"], 1)

            def turn_gated(n):
                pe.wait_ge(S["c_h3"], n)
                pe.wait_ge(S["c_g"], n + 1)
                for c in range(DI // P):
                    last = t.transpose(bank[7][:, c * P:(c + 1) * P], gated[:, c * P:(c + 1) * P], ident[:, :])
                last.then_inc(S["c_gt"], 1)

            def project(n, q, c):
                pe.wait_ge(S["c_gtc"], n + 1)
                o = bank[7][:, DI:DI + P]
                mm(o, hot[0:V, q, PAD + c * P:PAD + (c + 1) * P], htab[:, q, :], start=True, stop=False)
                mm(o, gT[:, 0:P], wout_T[:, 0, :], start=False, stop=False)
                mm(o, gT[:, P:2 * P], wout_T[:, 1, :], start=False, stop=True).then_inc(S["c_out"], 1)

            def step(m, r, valid):
                k = STEPS * m + r
                c3, q3 = spot(r, 3)
                c4, q4 = spot(r, 4)
                c5, q5 = spot(r, 5)
                c6, q6 = spot(r, 6)
                if valid(6):
                    turn_gated(k - 6)
                if valid(4):
                    decay_sums(k - 4, c4)
                    turn_bc(k - 4, q4, c4)
                if valid(3):
                    convolve(k - 3, q3, c3, 0)
                if valid(5):
                    gate_rows(k - 5, q5, c5)
                if valid(4):
                    scores(k - 4, c4)
                if valid(3):
                    convolve(k - 3, q3, c3, 1)
                if valid(6):
                    project(k - 6, q6, c6)
                if valid(4):
                    mixed(k - 4, c4)
                if r % 2 == 0 and valid(0):
                    tables(4 * m + r // 2, r // 2)
                if valid(4) and c4 == 0:
                    chunk_state(k - 4, c4)

            pe.wait_ge(S["s_dt"], 1)
            pipeline(pe, step)

            pe.wait_ge(S["c_h3"], NCH)
            def mlp_pe(m, r, valid):
                k = 4 * m + r
                if valid(1):
                    q = (r - 1) % 2
                    pe.wait_ge(S["m_xn"], k)
                    wait_past(pe, "m_xtc", k - 2)
                    for c in range(TD):
                        last = t.transpose(bank[q][:, c * P:(c + 1) * P], xn[:, q, c, :], ident[:, :])
                    last.then_inc(S["m_xt"], 1)
                if valid(2):
                    q = r % 2
                    pe.wait_ge(S["m_xtc"], k - 1)
                    wait_past(pe, "m_gel", k - 3)
                    mm(bank[2 + q][:, :], tri1_T[:, :], xnT[:, q, :], start=True, stop=True).then_inc(S["m_1"], 1)
                if valid(3):
                    q = (r - 1) % 2
                    pe.wait_ge(S["m_gel"], k - 2)
                    wait_past(pe, "m_fin", k - 4)
                    for c in range(TD):
                        last = mm(bank[4 + q][:, c * P:(c + 1) * P], gel[:, q, c * P:(c + 1) * P], tri2_T[:, :], start=True, stop=True)
                    last.then_inc(S["m_2"], 1)

            rolling(pe, mlp_pe, NT, 4, 3)

        @block.scalar
        def _(act):
            a = nc.scalar
            act.wait_ge(S["e_var"], 1)
            a.activation(stat[0:V, 9:10], stat[0:V, 8:9], ACT.Sqrt).then_inc(S["e_sd"], 1)
            act.wait_ge(S["e_sc"], 1)
            a.activation(tanh_s[:, :], bank[3][0:V, 256:256 + V], ACT.Tanh).then_inc(S["e_tanh"], 1)
            act.wait_ge(S["e_tanh"], 1)
            a.activation(expT[:, :], tanh_s[:, :], ACT.Exp).then_inc(S["e_exp"], 1)

            act.wait_ge(S["e_cnt"], 1)
            act.wait_ge(S["e_rden"], 1)
            def attention_act(m, r, valid):
                k = 2 * m + r
                if valid(0):
                    wait_past(act, "at_num", k - 1)
                    for j in range(GA):
                        last = a.activation(weighted[:, r, j, :], lne[:, :], ACT.Copy, scale=counts[:, bass.ds(k * GA + j, 1)])
                    last.then_inc(S["at_w"], 1)
                if valid(2):
                    act.wait_ge(S["at_t"], k - 1)
                    a.copy(hT[:, bass.ds((k - 2) * GA * V, GA * V)], bank[2 + r][:, 0:GA * V]).then_inc(S["at_s"], 1)

            rolling(act, attention_act, B // GA, 2, 2)

            def routing_act(m, r, valid):
                k = 2 * m + r
                if valid(1):
                    act.wait_ge(S["r_var"], k)
                    wait_past(act, "r_x", k - 1)
                    a.activation(dev[:, :], bank[1][:, 0:N2], ACT.Sqrt, bias=eps_ln[:, :]).then_inc(S["r_sd"], 1)
                if valid(2):
                    act.wait_ge(S["r_tr"], k - 1)
                    a.copy(xrows[:, bass.ds((k - 2) * N2, N2)], bank[2][:, 0:N2]).then_inc(S["r_xf"], 1)

            rolling(act, routing_act, NI, 2, 2)

            def relu(i, e, first):
                for hb in range(FT // 2):
                    k = 16 * (i - 1) + 2 * e + hb
                    act.wait_ge(S["b_up"], k + 1)
                    if hb == 0 and not (first and e < 2):
                        act.wait_ge(S["b_dn"], 8 * (i - 1) + e - 1)
                    for f in range(2):
                        ft = 2 * hb + f
                        last = a.activation(hid[:, e % 2, ft, :], bank[hb][:, f * N2:(f + 1) * N2], ACT.Relu,
                                            bias=b1_col[:, e * FT + ft:e * FT + ft + 1])
                    last.then_inc(S["b_relu"], 1)

            def turned_gates(i):
                act.wait_ge(S["b_wt"], i)
                wait_past(act, "b_z", i - 1)
                a.copy(wT_now[:, :], bank[7][0:E, N2:2 * N2]).then_inc(S["b_wtc"], 1)

            def expert_act(i, first, back):
                act.wait_ge(S["b_up"], 16 * (i - 1))
                a.copy(x_hi[:, :], xT[:, bass.ds((i - 1) * N2, N2)]).then_inc(S["b_xhi"], 1)
                if back:
                    turned_gates(i - 1)
                for e in range(E):
                    relu(i, e, first)
                    if first and e == 2:
                        act.wait_ge(S["r_gd"], 1)
                        a.activation(gexp[:, :], gdiff[:, :], ACT.Exp).then_inc(S["r_ge"], 1)
                    if back and e == 2:
                        act.wait_ge(S["b_var"], i - 1)
                        a.activation(sm[:, 5, :], sm[:, 4, :], ACT.Sqrt, bias=eps_ffn[:, :], scale=1.0 / D).then_inc(S["b_sd"], 1)
                    if back and e == 7:
                        act.wait_ge(S["b_v2"], i - 1)
                        a.activation(dev[:, :], bank[7][:, 0:N2], ACT.Sqrt, bias=eps_ln[:, :]).then_inc(S["b_sd2"], 1)

            act.wait_ge(S["w_trc"], 3)
            act.wait_ge(S["r_cp"], NI)
            expert_act(1, True, False)
            a.activation(stat[:, 12:13], eps_ln[:, :], ACT.Sqrt)
            with act.Fori(2, NI + 1) as i:
                expert_act(i, False, True)
            turned_gates(NI)

            def step_inputs(groups):
                act.wait_ge(S["s_raw"], groups)
                for q in range(2):
                    a.copy(dt_in[:, q], xT[:, bass.ds((groups + q) * GD * V, GD * V)]).then_inc(S["s_in"], 1)

            act.wait_ge(S["b_var"], NI)
            a.activation(sm[:, 5, :], sm[:, 4, :], ACT.Sqrt, bias=eps_ffn[:, :], scale=1.0 / D).then_inc(S["b_sd"], 1)
            act.wait_ge(S["b_dn"], E * NI)
            act.wait_ge(S["b_x"], NI - 1)
            with act.Fori(1, EARLY // 2 + 1) as m:
                step_inputs(2 * m - 2)
            act.wait_ge(S["b_v2"], NI)
            a.activation(dev[:, :], bank[7][:, 0:N2], ACT.Sqrt, bias=eps_ln[:, :]).then_inc(S["b_sd2"], 1)
            act.wait_ge(S["b_x"], NI)
            step_inputs(EARLY)

            act.wait_ge(S["ld_ssm"], 16 * N_SSM)
            a.activation(a_neg[:, :], alog_bc[:, :], ACT.Exp).then_inc(S["s_l"], 1)

            act.wait_ge(S["s_v"], 1)
            a.activation(dt_t[:, 1, :], dt_t[:, 1, :], ACT.Exp, scale=-1.0).then_inc(S["s_e"], 1)
            act.wait_ge(S["s_v"], 2)
            a.activation(dt_t[:, 4, :], dt_t[:, 2, :], ACT.Ln).then_inc(S["s_l"], 1)

            def tables(b, q):
                act.wait_ge(S["c_tab"], b + 1)
                wait_past(act, "c_prod", 2 * b)
                a.copy(xtab[0:V, 0:DI], bank[0][0:V, DI:2 * DI])
                a.copy(xtab[0:V, DI:CONV], bank[1][0:V, 0:P]).then_inc(S["c_tx"], 1)
                a.copy(dts_hi[:, q].rearrange("p c h -> p (c h)").bitcast(F32R), bank[1][:, 2 * P:2 * P + 4 * H])
                a.copy(dts[:, q].rearrange("p c h -> p (c h)"), bank[1][:, 2 * P:2 * P + 4 * H]).then_inc(S["c_dts"], 1)

            def more_tables(b, q):
                act.wait_ge(S["c_tab"], b + 1)
                wait_past(act, "c_out", 2 * b - 6)
                a.copy(htab[:, q, :], bank[1][0:V, P:2 * P]).then_inc(S["c_ht"], 1)
                wait_past(act, "c_zlo", b)
                a.activation(ztab[:, :], bank[0][0:V, 0:DI], ACT.Tanh).then_inc(S["c_tz"], 1)

            def round_z(b, q):
                act.wait_ge(S["c_zt"], b + 1)
                wait_past(act, "c_zg", 2 * b - 6)
                a.copy(z_hi[:, q, :], ztab[:, :]).then_inc(S["c_zhi"], 1)

            def round_taps(b, q, pair):
                act.wait_ge(S["c_prod"], 2 * b + pair + 1)
                wait_past(act, "c_cv", 2 * b - 2)
                a.copy(taps_hi[:, q, 2 * pair:2 * pair + 2, :], products[:, :, :]).then_inc(S["c_hi"], 1)

            def conv_tanh(n):
                act.wait_ge(S["c_cv"], n + 1)
                a.activation(tanh_x[:, :], bank[2][:, 0:CONV], ACT.Tanh).then_inc(S["c_tanh"], 1)

            def decays(n, r):
                wait_past(act, "c_y", n - 1)
                act.wait_ge(S["c_seg"], n + 1)
                a.activation(decay[:, r].rearrange("p h l -> p (h l)"), bank[3][:, :], ACT.Exp).then_inc(S["c_dec"], 1)

            def edges(n, r):
                wait_past(act, "c_y", n - 1)
                act.wait_ge(S["c_bc"], n + 1)
                a.copy(bcT[:, r, :], bank[4][0:NS, 0:2 * P])
                a.activation(edge[:, r, :], bank[4][:, 2 * P:2 * P + H], ACT.Exp).then_inc(S["c_edc"], 1)

            def square_sum(n, r):
                act.wait_ge(S["c_y"], n + 1)
                wait_past(act, "c_gt", n)
                a.activation(gated[:, :], y[:, r, :], ACT.Square, accum_out=ssum[:, :]).then_inc(S["c_bn"], 1)
                act.wait_ge(S["c_bn"], n + 1)
                act.wait_ge(S["c_rms"], n)
                a.mul(ms[:, :], ssum[:, :], 1.0 / DI).then_inc(S["c_sq"], 1)

            def step(m, r, valid):
                k = STEPS * m + r
                c4, c5 = (spot(r, lag)[0] for lag in (4, 5))
                if valid(6):
                    act.wait_ge(S["c_gt"], k - 5)
                    a.copy(gT[:, :], bank[7][:, 0:DI]).then_inc(S["c_gtc"], 1)
                if valid(5) and c5 == 0:
                    square_sum(k - 5, c5)
                if valid(4):
                    edges(k - 4, c4)
                    decays(k - 4, c4)
                if valid(5) and c5 == 1:
                    square_sum(k - 5, c5)
                if r % 2 == 1 and valid(1):
                    more_tables(4 * m + r // 2, r // 2)
                if valid(3):
                    conv_tanh(k - 3)
                if valid(6):
                    act.wait_ge(S["c_out"], k - 5)
                    a.copy(h3[:, bass.ds((k - 6) * P, P)], bank[7][:, DI:DI + P]).then_inc(S["c_h3"], 1)
                if r % 2 == 1 and valid(1):
                    round_z(4 * m + r // 2, r // 2)
                    round_taps(4 * m + r // 2, r // 2 % 2, 0)
                if r % 2 == 0 and valid(2):
                    round_taps(4 * m + r // 2 - 1, (r // 2 - 1) % 2, 1)
                if r % 2 == 0 and valid(0):
                    tables(4 * m + r // 2, r // 2)

            act.wait_ge(S["c_ones"], 1)
            pipeline(act, step)

            act.wait_ge(S["f_st"], 1)
            a.activation(h3_s[:, 3, :], h3_s[:, 2, :], ACT.Sqrt, bias=eps_ln[:, :], scale=1.0 / D).then_inc(S["f_sd"], 1)
            act.wait_ge(S["ld_mlp"], 16 * N_MLP)
            def mlp_act(m, r, valid):
                k = 4 * m + r
                if valid(1):
                    q = (r - 1) % 2
                    act.wait_ge(S["m_xt"], k)
                    wait_past(act, "m_1", k - 2)
                    a.copy(xnT[:, q, :], bank[q][:, :]).then_inc(S["m_xtc"], 1)
                if valid(2):
                    act.wait_ge(S["m_1"], k - 1)
                    wait_past(act, "m_2", k - 3)
                    a.activation(gel[:, r % 2, :], bank[2 + r % 2][:, :], ACT.Gelu, bias=trib1_col[:, :]).then_inc(S["m_gel"], 1)

            rolling(act, mlp_act, NT, 4, 3)

        @block.vector
        def _(dve):
            v = nc.vector
            chain = Chain(dve, "dchain")
            link = chain.link

            dve.wait_ge(S["ld_att"], 16 * N_ATT)
            link(v.bn_stats(stat[0:V, 0:6], emb_sb[:, :]))
            link(v.bn_aggr(stat[0:V, 6:8], stat[0:V, 0:6]))
            v.tensor_scalar(stat[0:V, 8:9], stat[0:V, 7:8], EPS_LN, None, ALU.add).then_inc(S["e_var"], 1)
            dve.wait_ge(S["e_sd"], 1)
            link(v.reciprocal(stat[0:V, 10:11], stat[0:V, 9:10]))
            v.tensor_scalar(lne[:, :], emb_sb[:, :], stat[0:V, 6:7], stat[0:V, 10:11], ALU.subtract, ALU.mult).then_inc(S["e_ln"], 1)
            dve.wait_ge(S["e_lnT"], 1)
            v.tensor_copy(lneT[:, :], bank[3][:, 0:V]).then_inc(S["e_lnT_c"], 1)
            dve.wait_ge(S["e_pT"], 1)
            v.tensor_copy(projT[:, :], bank[3][:, 128:128 + V]).then_inc(S["e_pT_c"], 1)

            dve.wait_ge(S["const_ok"], 10)
            for n in range(B // TOKB):
                dve.wait_ge(S[f"tok_ld{n % TOKN}"], 16 * (n // TOKN + 1))
                hots = onehot[:, n * TOKB:(n + 1) * TOKB, PAD:PAD + T]
                ins = v.tensor_scalar(hots, tok[:, n % TOKN], vocab[:, :], None, ALU.is_equal)
                ins.then_inc(S["tok_used"], 1)
                dve.wait_ge(S["tok_used"], n + 1)
                last = v.tensor_reduce(counts[:, n * TOKB:(n + 1) * TOKB], hots, AX.X, ALU.add)
            last.then_inc(S["e_cnt"], 1)

            dve.wait_ge(S["w_tr"], 1)
            v.tensor_scalar(win_T[:, 0:DI], bank[0][:, 0:DI], 0.5, None, ALU.mult)
            v.tensor_copy(win_T[:, DI:BANK], bank[0][:, DI:BANK]).then_inc(S["w_trc"], 1)
            dve.wait_ge(S["w_tr"], 2)
            v.tensor_copy(win_T[:, BANK:NZX], bank[1][:, 0:P])
            v.tensor_copy(windt_T[:, :], bank[1][:, P:P + H])
            v.tensor_copy(normw_col[:, :], bank[1][:, P + H:P + H + DI // P]).then_inc(S["w_nw"], 1)
            dve.wait_ge(S["w_nw"], 1)
            for c in range(DI // P):
                last = v.tensor_scalar(wout_T[:, c, :], bank[1][:, (2 + c) * P - 64:(3 + c) * P - 64], normw_col[:, c:c + 1], None, ALU.mult)
            last.then_inc(S["w_trc"], 1)
            dve.wait_ge(S["w_tr"], 3)
            v.tensor_tensor(tri1_T[:, :], bank[2][:, 0:P], upper[:, :], ALU.mult)
            v.tensor_tensor(tri2_T[:, :], bank[2][:, P:2 * P], upper[:, :], ALU.mult)
            v.tensor_copy(b1_col[:, :], bank[2][:, 2 * P:2 * P + E * FT]).then_inc(S["w_trc"], 1)

            dve.wait_ge(S["e_den"], 1)
            v.reciprocal(rden[:, :], bank[4][0:V, 0:B]).then_inc(S["e_rden"], 1)
            dve.wait_ge(S["e_rden"], 1)
            def attention_dve(m, r, valid):
                k = 2 * m + r
                if valid(0):
                    dve.wait_ge(S["at_num"], k + 1)
                    wait_past(dve, "at_t", k - 1)
                    for j in range(GA):
                        last = v.scalar_tensor_tensor(out=h1rows[:, r, j, :], in0=bank[r][0:V, j * D:(j + 1) * D],
                                                      scalar=rden[:, bass.ds(k * GA + j, 1)],
                                                      in1=emb_sb[:, :], op0=ALU.mult, op1=ALU.add)
                    last.then_inc(S["at_h"], 1)

            rolling(dve, attention_dve, B // GA, 2, 1)

            dve.wait_ge(S["at_s"], B // GA)

            def routing_dve(m, r, valid):
                k = 2 * m + r
                if valid(0):
                    wait_past(dve, "r_x", k - 1)
                    dve.wait_ge(S["r_mean"], k + 1)
                    v.tensor_tensor(cen2[:, r], hT[:, bass.ds(k * N2, N2)], bank[0][:, 0:N2], ALU.subtract).then_inc(S["r_c"], 1)
                if valid(1):
                    dve.wait_ge(S["r_sd"], k)
                    v.reciprocal(rstd[:, :], dev[:, :]).then_inc(S["rchain"], 1)
                    wait_past(dve, "r_cp", k - 2)
                    wait_past(dve, "r_tr", k - 2)
                    dve.wait_ge(S["rchain"], k)
                    v.tensor_tensor(xT_now[:, 1 - r], cen2[:, 1 - r], rstd[:, :], ALU.mult).then_inc(S["r_x"], 1)
                if valid(2):
                    dve.wait_ge(S["r_rt"], k - 1)
                    v.tensor_copy(logits[:, bass.ds(2 * (k - 2), 2), :].rearrange("p j e -> p (j e)"), bank[3][:, 0:2 * E]).then_inc(S["r_lg"], 1)

            rolling(dve, routing_dve, NI, 2, 2)

            dve.wait_ge(S["r_lg"], NI)
            for n in range(NTILE):
                last = v.max(top_v[:, n, :], logits[:, n, :])
            last.then_inc(S["r_top"], 1)
            dve.wait_ge(S["r_top"], 1)
            for n in range(NTILE):
                last = v.max_index(top_i[:, n, :], top_v[:, n, :], logits[:, n, :])
            last.then_inc(S["r_ti"], 1)
            dve.wait_ge(S["r_ti"], 1)
            link(v.tensor_copy(idxs[:, :, :], top_i[:, :, 0:2]))

            v.tensor_tensor(gdiff[:, :], top_v[:, :, 1], top_v[:, :, 0], ALU.subtract).then_inc(S["r_gd"], 1)
            dve.wait_ge(S["r_ge"], 1)
            link(v.tensor_scalar(gates[:, :, 1], gexp[:, :], 1.0, None, ALU.add))
            link(v.reciprocal(gates[:, :, 0], gates[:, :, 1]))
            link(v.tensor_tensor(gates[:, :, 1], gexp[:, :], gates[:, :, 0], ALU.mult))
            every = experts8[:, :].unsqueeze(1).to_broadcast([P, NTILE, E])
            for s in range(2):
                link(v.tensor_tensor(pick[:, :, :], every, idxs[:, :, s].unsqueeze(2).to_broadcast([P, NTILE, E]), ALU.is_equal))
                dst = pick if s else wgate
                link(v.tensor_tensor(dst[:, :, :], pick[:, :, :], gates[:, :, s].unsqueeze(2).to_broadcast([P, NTILE, E]), ALU.mult))
            v.tensor_tensor(wgate[:, :, :], wgate[:, :, :], pick[:, :, :], ALU.add).then_inc(S["r_gates"], 1)
            dve.wait_ge(S["r_gates"], 1)

            bch = Chain(dve, "bchain")

            def expert_sums(i, gg):
                for j in range(2):
                    k = 4 * (i - 1) + 2 * gg + j
                    if gg == 0:
                        wait_past(dve, "b_o", i - 1)
                    if j == 0:
                        dve.wait_ge(S["b_y"], 2 * (i - 1) + gg + 1)
                    else:
                        dve.wait_ge(S["b_dn"], 8 * (i - 1) + 4 * gg + 4)
                    dve.wait_ge(S["b_xb2"], k + 1)
                    v.tensor_tensor(pre[:, j, gg * BANK:(gg + 1) * BANK], bank[2 + 2 * gg + j][:, :], xb2[:, j, gg * BANK:(gg + 1) * BANK],
                                    ALU.add).then_inc(S[f"b_pre{gg}{j}"], 1)
                    dve.wait_ge(S[f"b_pre{gg}{j}"], i)
                    for e in range(4 * gg, 4 * gg + 4):
                        last = v.bn_stats(bns[:, j * E + e, :], pre[:, j, e * D:(e + 1) * D])
                if gg == 1:
                    last.then_inc(S["b_bn"], 1)

            def expert_norms(i, sums):
                bch.start((i - 1) * B_LINKS)
                col = [bns[:, :, c] for c in range(6)]
                dve.wait_ge(S["b_bn"], i)
                v.tensor_tensor(sm[:, 0, :], col[1], col[4], ALU.add)
                v.tensor_tensor(sm[:, 1, :], col[1], col[4], ALU.subtract)
                bch.link(v.tensor_tensor(sm[:, 2, :], col[2], col[5], ALU.add))
                v.tensor_scalar(sm[:, 0, :], sm[:, 0, :], 0.5, None, ALU.mult)
                bch.link(v.tensor_tensor(sm[:, 3, :], sm[:, 1, :], sm[:, 1, :], ALU.mult))
                v.scalar_tensor_tensor(out=sm[:, 4, :], in0=sm[:, 3, :], scalar=D / 4.0, in1=sm[:, 2, :],
                                       op0=ALU.mult, op1=ALU.add).then_inc(S["b_var"], 1)
                dve.wait_ge(S["b_sd"], i)
                bch.link(v.reciprocal(sm[:, 6, :], sm[:, 5, :]))
                bch.link(v.tensor_tensor(sm[:, 7, :].rearrange("p (j e) -> p j e", e=E), sm[:, 6, :].rearrange("p (j e) -> p j e", e=E),
                                         wgate[:, bass.ds(2 * (i - 1), 2), :], ALU.mult))
                for j in range(2):
                    for k in range(j * E, (j + 1) * E):
                        part = pre[:, k // E, (k % E) * D:(k % E + 1) * D]
                        last = v.tensor_scalar(part, part, sm[:, 0, k:k + 1], sm[:, 7, k:k + 1], ALU.subtract, ALU.mult)
                    last.then_inc(S["b_u"], 1)
                for j in range(2):
                    dve.wait_ge(S["b_ug"], 2 * i - 1 + j)
                    last = v.tensor_reduce(summed[:, j, :], pre[:, j, :].rearrange("p (e d) -> p d e", d=D), AX.X, ALU.add)
                last.then_inc(S["b_o"], 1)
                if sums:
                    expert_sums(i + 1, 0)
                now = bass.ds((i - 1) * N2, N2)
                dve.wait_ge(S["b_z"], i)
                v.tensor_tensor(hT[:, now], bank[6][:, 0:N2], hT[:, now], ALU.add).then_inc(S["b_h2"], 1)
                dve.wait_ge(S["b_mean"], i)
                v.tensor_tensor(cen, hT[:, now], bank[6][:, N2:2 * N2], ALU.subtract).then_inc(S["b_c"], 1)
                dve.wait_ge(S["b_sd2"], i)
                bch.link(v.reciprocal(rstd[:, :], dev[:, :]))
                v.tensor_tensor(xT[:, now], cen, rstd[:, :], ALU.mult).then_inc(S["b_x"], 1)

            expert_sums(1, 0)
            expert_sums(1, 1)
            with dve.Fori(2, NI + 1) as i:
                expert_norms(i - 1, True)
                assert bch.n == B_LINKS
                expert_sums(i, 1)
            expert_norms(NI, False)

            dve.wait_ge(S["ld_ssm"], 16 * N_SSM)
            dve.wait_ge(S["taps0"], 2)
            v.tensor_scalar(convb_half[:, :], convb_row[:, :], 0.5, None, ALU.mult)
            v.tensor_scalar(tapw[0:V, :, :], convw_raw.rearrange("p (c k) -> p k c", k=TAPS), 0.5, None, ALU.mult).then_inc(S["s_aneg"], 1)
            dve.wait_ge(S["s_l"], 1)
            link(v.tensor_scalar(a_neg[:, :], a_neg[:, :], -1.0, None, ALU.mult))

            dve.wait_ge(S["s_raw"], B // GD)
            link(v.tensor_tensor(dt_t[:, 0, :].rearrange("p (b h) -> p b h", h=H), bank[0][0:V, 0:B * H].rearrange("p (b h) -> p b h", h=H),
                                 dtb_bc[:, :].unsqueeze(1).to_broadcast([V, B, H]), ALU.add))
            link(v.tensor_scalar(dt_t[:, 2, :], dt_t[:, 0, :], -1.0, None, ALU.mult))
            v.tensor_tensor(dt_t[:, 1, :], dt_t[:, 0, :], dt_t[:, 2, :], ALU.max).then_inc(S["s_v"], 1)
            dve.wait_ge(S["s_e"], 1)
            v.tensor_scalar(dt_t[:, 2, :], dt_t[:, 1, :], 1.0, None, ALU.add).then_inc(S["s_v"], 1)
            dve.wait_ge(S["s_v"], 2)
            link(v.tensor_scalar(dt_t[:, 3, :], dt_t[:, 2, :], 1.0, None, ALU.subtract))
            dve.wait_ge(S["s_l"], 2)
            link(v.tensor_scalar(dt_t[:, 2, :], dt_t[:, 3, :], 0.0, None, ALU.is_equal))
            v.tensor_tensor(dt_t[:, 3, :], dt_t[:, 3, :], dt_t[:, 2, :], ALU.add)
            link(v.tensor_tensor(dt_t[:, 4, :], dt_t[:, 4, :], dt_t[:, 2, :], ALU.add))
            link(v.reciprocal(dt_t[:, 2, :], dt_t[:, 3, :]))
            link(v.tensor_tensor(dt_t[:, 4, :], dt_t[:, 4, :], dt_t[:, 2, :], ALU.mult))
            link(v.tensor_tensor(dt_t[:, 4, :], dt_t[:, 4, :], dt_t[:, 1, :], ALU.mult))
            by_seq = dt_t[:, :, :].rearrange("v k (b h) -> v k b h", h=H)
            link(v.scalar_tensor_tensor(out=dt_tab[:, :, 0, :], in0=by_seq[:, 0], scalar=0.0, in1=by_seq[:, 4], op0=ALU.max, op1=ALU.add))
            link(v.tensor_tensor(dt_tab[:, :, 1, :], dt_tab[:, :, 0, :], a_neg[0:V, :].unsqueeze(1).to_broadcast([V, B, H]), ALU.mult))
            dve.wait_ge(S["zpad"], 16)
            v.memset(stat[:, 14:15], 0.0).then_inc(S["s_dt"], 1)

            def by_head(ap):
                return ap.rearrange("p (h d) -> p h d", h=H)

            def sequence(b, q):
                wait_past(dve, "c_tab", b - 1)
                wait_past(dve, "c_out", 2 * b - 6)
                v.tensor_copy(xT_seq[:, q % 2], xT[:, bass.ds(b * V, V)])
                v.tensor_copy(hT_seq[:, q % 2], hT[:, bass.ds(b * V, V)])
                v.tensor_copy(hot_r[0:V, q, :], onehot[:, bass.ds(b, 1), :].rearrange("p a t -> p (a t)")).then_inc(S["c_seq"], 1)

            def z_rest(b, q):
                dve.wait_ge(S["c_zhi"], b + 1)
                wait_past(dve, "c_zg", 2 * b - 6)
                v.tensor_tensor(z_lo[:, q, :], ztab[:, :], z_hi[:, q, :].bitcast(F32), ALU.subtract).then_inc(S["c_zlo"], 1)

            def rest_mask(n, q, c):
                if c == 0:
                    dve.wait_ge(S["c_dts"], half(n, 0) + 1)
                    v.tensor_tensor(dts_lo[:, q], dts[:, q], dts_hi[:, q], ALU.subtract).then_inc(S["c_dtlo"], 1)
                    dve.wait_ge(S["c_dtlo"], half(n, 0) + 1)
                wait_past(dve, "c_seg", n)
                v.tensor_tensor(amask_lo[:, :, :], upper[:, :].unsqueeze(1).to_broadcast([P, H, P]),
                                dts_lo[:, q, c, H:2 * H].unsqueeze(2).to_broadcast([P, H, P]), ALU.mult).then_inc(S["c_masklo"], 1)

            def tap_rests(b, q, pair):
                dve.wait_ge(S["c_hi"], 2 * b + pair + 1)
                taps = slice(2 * pair, 2 * pair + 2)
                v.tensor_tensor(taps_lo[:, q, taps, :], products[:, :, :], taps_hi[:, q, taps, :].bitcast(F32), ALU.subtract).then_inc(
                    S["c_taps"], 1)

            def z_table(b, q):
                dve.wait_ge(S["c_tz"], b + 1)
                dve.wait_ge(S["c_ht"], b + 1)
                v.scalar_tensor_tensor(out=ztab[:, :], in0=ztab[:, :], scalar=1.0, in1=bank[0][0:V, 0:DI],
                                       op0=ALU.add, op1=ALU.mult).then_inc(S["c_zt"], 1)

            def silu(n, r, c):
                if c == 0:
                    dve.wait_ge(S["c_st"], half(n, 0))
                dve.wait_ge(S["c_tanh"], n + 1)
                v.scalar_tensor_tensor(out=xbc[:, r, :], in0=tanh_x[:, :], scalar=1.0, in1=bank[2][:, 0:CONV],
                                       op0=ALU.add, op1=ALU.mult).then_inc(S["c_x"], 1)

            def causal_scores(n, r):
                dve.wait_ge(S["c_cb"], n + 1)
                v.tensor_tensor(cbm[:, r, :], bank[4][:, 3 * P:4 * P], upper[:, :], ALU.mult).then_inc(S["c_cbm"], 1)
                dve.wait_ge(S["c_cbm"], n + 1)
                dve.wait_ge(S["c_dec"], n + 1)
                v.tensor_tensor(decay[:, r], decay[:, r], cbm[:, r].unsqueeze(1).to_broadcast([P, H, P]), ALU.mult).then_inc(S["c_mix"], 1)

            def combine(n, r, c):
                dve.wait_ge(S["c_yd"], n + 1)
                dve.wait_ge(S["c_xsk"], n + 1)
                if c == 0:
                    v.tensor_tensor(y[:, r, :], bank[5][:, 0:DI], xskip[:, r, :], ALU.add).then_inc(S["c_y"], 1)
                else:
                    v.tensor_tensor(by_head(yoff[:, :]), by_head(bank[5][:, DI:2 * DI]),
                                    edge[:, r, :].unsqueeze(2).to_broadcast([P, H, HD]), ALU.mult)
                    v.tensor_tensor(y[:, r, :], bank[5][:, 0:DI], xskip[:, r, :], ALU.add).then_inc(S["c_yin"], 1)
                    dve.wait_ge(S["c_yin"], half(n, 1) + 1)
                    v.tensor_tensor(y[:, r, :], y[:, r, :], yoff[:, :], ALU.add).then_inc(S["c_y"], 1)

            def gate(n, r):
                dve.wait_ge(S["c_rms"], n + 1)
                v.tensor_scalar(rms[:, 1:2], rms[:, 0:1], EPS_RMS, None, ALU.add).then_inc(S["c_yo"], 1)
                dve.wait_ge(S["c_yo"], 2 * n + 1)
                v.reciprocal(rms[:, 2:3], rms[:, 1:2]).then_inc(S["c_yo"], 1)
                dve.wait_ge(S["c_yo"], 2 * n + 2)
                dve.wait_ge(S["c_zg"], n + 1)
                v.scalar_tensor_tensor(out=gated[:, :], in0=y[:, r, :], scalar=rms[:, 2:3], in1=bank[6][:, 0:DI],
                                       op0=ALU.mult, op1=ALU.mult).then_inc(S["c_g"], 1)

            def step(m, r, valid):
                k = STEPS * m + r
                (c3, q3), (c4, _), (c5, _) = (spot(r, lag) for lag in (3, 4, 5))
                if r % 2 == 0 and valid(2):
                    tap_rests(4 * m + r // 2 - 1, (r // 2 - 1) % 2, 0)
                if r % 2 == 1 and valid(3):
                    tap_rests(4 * m + r // 2 - 1, (r // 2 - 1) % 2, 1)
                if valid(5) and c5 == 0:
                    dve.wait_ge(S["c_st"], half(k - 5, 0) + 1)
                    v.tensor_copy(state[:, :], bank[6][0:NS, DI:2 * DI]).then_inc(S["c_stc"], 1)
                if r % 2 == 1 and valid(3):
                    rest_mask(k - 3, q3, c3)
                if valid(4):
                    causal_scores(k - 4, c4)
                if r % 2 == 0 and valid(0):
                    sequence(4 * m + r // 2, r // 2)
                if r % 2 == 1 and valid(1):
                    z_table(4 * m + r // 2, r // 2)
                if r % 2 == 0 and valid(3):
                    rest_mask(k - 3, q3, c3)
                if r % 2 == 0 and valid(2):
                    z_rest(4 * m + r // 2 - 1, (r // 2 - 1) % 4)
                if valid(5):
                    gate(k - 5, c5)
                if valid(3):
                    silu(k - 3, c3, c3)
                if valid(6):
                    n = k - 6
                    dve.wait_ge(S["c_h3"], n + 1)
                    v.bn_stats(h3_bns[:, bass.ds(n, 1), :].rearrange("p a s -> p (a s)"), h3[:, bass.ds(n * P, P)]).then_inc(S["c_dt"], 1)
                if valid(4):
                    combine(k - 4, c4, c4)
            dve.wait_ge(S["c_ones"], 1)
            pipeline(dve, step)

            dve.wait_ge(S["c_dt"], NCH)
            col = [h3_bns[:, :, c] for c in range(6)]
            v.tensor_tensor(h3_s[:, 0, :], col[1], col[4], ALU.add)
            v.tensor_tensor(h3_s[:, 1, :], col[1], col[4], ALU.subtract)
            link(v.tensor_tensor(h3_s[:, 2, :], col[2], col[5], ALU.add))
            v.tensor_scalar(h3_s[:, 0, :], h3_s[:, 0, :], 0.5, None, ALU.mult)
            link(v.tensor_tensor(h3_s[:, 3, :], h3_s[:, 1, :], h3_s[:, 1, :], ALU.mult))
            v.scalar_tensor_tensor(out=h3_s[:, 2, :], in0=h3_s[:, 3, :], scalar=D / 4.0, in1=h3_s[:, 2, :],
                                   op0=ALU.mult, op1=ALU.add).then_inc(S["f_st"], 1)
            dve.wait_ge(S["f_sd"], 1)
            link(v.reciprocal(h3_s[:, 4, :], h3_s[:, 3, :]))

            def mlp_dve(m, r, valid):
                k = 4 * m + r
                if valid(0):
                    wait_past(dve, "m_xt", k - 1)
                    for c in range(TD):
                        n = TD * k + c
                        last = v.tensor_scalar(xn[:, r % 2, c, :], h3[:, bass.ds(n * P, P)], h3_s[:, 0, bass.ds(n, 1)], h3_s[:, 4, bass.ds(n, 1)],
                                               ALU.subtract, ALU.mult)
                    last.then_inc(S["m_xn"], 1)
                if valid(3):
                    q = (r - 3) % 4
                    dve.wait_ge(S["m_2"], k - 2)
                    dve.wait_ge(S["m_res"], k - 2)
                    wait_past(dve, f"m_st{q}", 16 * (m + (r - 3 - q) // 4))
                    v.tensor_tensor(fin[:, q], bank[4 + q % 2][:, :].rearrange("p (c d) -> p c d", d=D), res[:, q], ALU.add).then_inc(S["m_fin"], 1)

            rolling(dve, mlp_dve, NT, 4, 3)


_INS = ['x', 'L0_tok_embed_weight', 'L0_attn_attention_weights', 'L0_ffn_router_w', 'L0_ffn_w1', 'L0_ffn_b1',
        'L0_ffn_w2', 'L0_ffn_b2', 'L0_ffn_gamma', 'L0_ffn_beta', 'L1_attn_W_in', 'L1_attn_conv_w',
        'L1_attn_conv_b', 'L1_attn_A_log', 'L1_attn_dt_bias', 'L1_attn_D', 'L1_attn_norm_w', 'L1_attn_W_out',
        'L1_ffn_W1', 'L1_ffn_b1', 'L1_ffn_W2', 'L1_ffn_b2']


def kernel(**inputs):
    import numpy as _np
    import concourse.bacc as _bacc
    from concourse import mybir as _mybir
    from concourse.bass_utils import run_bass_kernel_spmd as _run

    nc = _bacc.Bacc("TRN2", target_bir_lowering=False, num_devices=1)
    arrays, args = {}, []
    for name in _INS:
        a = _np.ascontiguousarray(inputs[name])
        arrays[f"in_{name}"] = a
        args.append(nc.dram_tensor(f"in_{name}", a.shape, _mybir.dt.from_np(a.dtype), kind="ExternalInput").ap())
    b, t = inputs['x'].shape
    d = inputs['L0_tok_embed_weight'].shape[1]
    out = nc.dram_tensor("out", (b, t, d), _mybir.dt.float32, kind="ExternalOutput").ap()
    lm_tower(nc, *args, out)
    r = _run(nc, [arrays], core_ids=[0])
    return r.results[0]["out"]
```
